# Optimizing a Trainium2 kernel written in Bass

```python
import numpy as np
import jax
import jax.numpy as jnp

def _softmax(x, axis=-1):
    return jax.nn.softmax(x, axis=axis)

def _gelu(x):
    return jax.nn.gelu(x, approximate=True)

def _silu(x):
    return jax.nn.silu(x)

def _sigmoid(x):
    return jax.nn.sigmoid(x)

def _layernorm(x, axis=-1, eps=1e-05):
    m = jnp.mean(x, axis=axis, keepdims=True)
    v = jnp.var(x, axis=axis, keepdims=True)
    return (x - m) / jnp.sqrt(v + eps)

def _scatter_add(tgt, idx, src, axis=0):
    return tgt.at[idx].add(src)

def _segment_sum(src, seg, n):
    return jax.ops.segment_sum(src, seg, n)
kernel_name = 'mk_sandwich_d1_jaxref_r4_f5bb2b'

def setup_inputs(seed: int=0):
    np.random.seed(seed)
    _w = jnp.asarray

    def _L0_attn_setup():
        import math
        import jax, jax.numpy as jnp
        import numpy as np
        D = 256
        H = 16
        CH = 8
        EPS = 1e-05

        def _layernorm(x, w, b):
            mu = jnp.mean(x, axis=-1, keepdims=True)
            var = jnp.mean((x - mu) ** 2, axis=-1, keepdims=True)
            return (x - mu) * jax.lax.rsqrt(var + EPS) * w + b

        def _token_diffusion(x, Wqk, Wv, Wo, tau):
            b, n, d = x.shape
            dh = d // H
            qk = (x @ Wqk).reshape(b, n, H, dh).transpose(0, 2, 1, 3)
            v = (x @ Wv).reshape(b, n, H, dh).transpose(0, 2, 1, 3)
            dot = jnp.einsum('bhnd,bhmd->bhnm', qk, qk)
            q2 = jnp.sum(qk * qk, axis=-1)
            logits = (2.0 * dot - q2[..., :, None] - q2[..., None, :]) / math.sqrt(dh)
            logits = logits * tau
            attn = jax.nn.softmax(logits, axis=-1)
            out = jnp.einsum('bhnm,bhmd->bhnd', attn, v)
            out = out.transpose(0, 2, 1, 3).reshape(b, n, d)
            return out @ Wo

        def _channel_diffusion(x, Wqk, Wv, Wo, tau):
            b, n, d = x.shape
            dh = d // CH
            qk = (x @ Wqk).transpose(0, 2, 1).reshape(b, CH, dh, n)
            v = (x @ Wv).transpose(0, 2, 1).reshape(b, CH, dh, n)
            dot = jnp.einsum('bhcn,bhdn->bhcd', qk, qk)
            q2 = jnp.sum(qk * qk, axis=-1)
            logits = (2.0 * dot - q2[..., :, None] - q2[..., None, :]) / math.sqrt(n)
            logits = logits * tau
            attn = jax.nn.softmax(logits, axis=-1)
            out = jnp.einsum('bhcd,bhdn->bhcn', attn, v)
            out = out.reshape(b, d, n).transpose(0, 2, 1)
            return out @ Wo
        key = jax.random.key(seed)
        ks = jax.random.split(key, 8)
        s = 1.0 / math.sqrt(D)
        inp = {'x': jax.random.normal(ks[0], (8, 256, D), dtype=jnp.float32), 'Wqk_t': jax.random.normal(ks[1], (D, D), dtype=jnp.float32) * s, 'Wv_t': jax.random.normal(ks[2], (D, D), dtype=jnp.float32) * s, 'Wo_t': jax.random.normal(ks[3], (D, D), dtype=jnp.float32) * s, 'tau_t': jnp.ones((H, 1, 1), dtype=jnp.float32), 'Wqk_c': jax.random.normal(ks[4], (D, D), dtype=jnp.float32) * s, 'Wv_c': jax.random.normal(ks[5], (D, D), dtype=jnp.float32) * s, 'Wo_c': jax.random.normal(ks[6], (D, D), dtype=jnp.float32) * s, 'tau_c': jnp.ones((CH, 1, 1), dtype=jnp.float32), 'ln1_w': jnp.ones((D,), dtype=jnp.float32), 'ln1_b': jnp.zeros((D,), dtype=jnp.float32), 'ln2_w': jnp.ones((D,), dtype=jnp.float32), 'ln2_b': jnp.zeros((D,), dtype=jnp.float32), 'gamma1': 0.0001 * jnp.ones((D,), dtype=jnp.float32), 'gamma2': 0.0001 * jnp.ones((D,), dtype=jnp.float32)}
        return inp
    _L0_attn_in = _L0_attn_setup()

    def _L0_ffn_setup():
        import jax, jax.numpy as jnp
        import numpy as np
        EMBED_DIM = 256
        HIDDEN_DIM = 1024
        NUM_EXPERTS = 8
        TOP_K = 2
        key = jax.random.key(seed)
        ks = jax.random.split(key, 4)
        std1 = float(np.sqrt(2.0 / EMBED_DIM))
        std2 = float(np.sqrt(2.0 / HIDDEN_DIM))
        x = jax.random.normal(ks[0], (1, 512, EMBED_DIM), dtype=jnp.float32)
        w_router = jax.random.normal(ks[1], (EMBED_DIM, NUM_EXPERTS), dtype=jnp.float32) * 0.02
        w1 = jax.random.normal(ks[2], (NUM_EXPERTS, EMBED_DIM, HIDDEN_DIM), dtype=jnp.float32) * std1
        b1 = jnp.zeros((NUM_EXPERTS, HIDDEN_DIM), dtype=jnp.float32)
        w2 = jax.random.normal(ks[3], (NUM_EXPERTS, HIDDEN_DIM, EMBED_DIM), dtype=jnp.float32) * std2
        b2 = jnp.zeros((NUM_EXPERTS, EMBED_DIM), dtype=jnp.float32)
        return {'x': x, 'w_router': w_router, 'w1': w1, 'b1': b1, 'w2': w2, 'b2': b2}
    _L0_ffn_in = _L0_ffn_setup()
    _d = {'L0_attn_x': _L0_attn_in['x'], 'L0_attn_Wqk_t': _L0_attn_in['Wqk_t'], 'L0_attn_Wv_t': _L0_attn_in['Wv_t'], 'L0_attn_Wo_t': _L0_attn_in['Wo_t'], 'L0_attn_tau_t': _L0_attn_in['tau_t'], 'L0_attn_Wqk_c': _L0_attn_in['Wqk_c'], 'L0_attn_Wv_c': _L0_attn_in['Wv_c'], 'L0_attn_Wo_c': _L0_attn_in['Wo_c'], 'L0_attn_tau_c': _L0_attn_in['tau_c'], 'L0_attn_ln1_w': _L0_attn_in['ln1_w'], 'L0_attn_ln1_b': _L0_attn_in['ln1_b'], 'L0_attn_ln2_w': _L0_attn_in['ln2_w'], 'L0_attn_ln2_b': _L0_attn_in['ln2_b'], 'L0_attn_gamma1': _L0_attn_in['gamma1'], 'L0_attn_gamma2': _L0_attn_in['gamma2'], 'L0_ffn_w_router': _L0_ffn_in['w_router'], 'L0_ffn_w1': _L0_ffn_in['w1'], 'L0_ffn_b1': _L0_ffn_in['b1'], 'L0_ffn_w2': _L0_ffn_in['w2'], 'L0_ffn_b2': _L0_ffn_in['b2']}
    _x0 = _d['L0_attn_x']
    _d['L0_attn_x'] = jax.random.normal(jax.random.fold_in(jax.random.key(seed), 1), (8, 512, 256), dtype=_x0.dtype)
    del _x0
    return _d

def reference(L0_attn_x, L0_attn_Wqk_t, L0_attn_Wv_t, L0_attn_Wo_t, L0_attn_tau_t, L0_attn_Wqk_c, L0_attn_Wv_c, L0_attn_Wo_c, L0_attn_tau_c, L0_attn_ln1_w, L0_attn_ln1_b, L0_attn_ln2_w, L0_attn_ln2_b, L0_attn_gamma1, L0_attn_gamma2, L0_ffn_w_router, L0_ffn_w1, L0_ffn_b1, L0_ffn_w2, L0_ffn_b2):

    def _L0_attn_ref(x, Wqk_t, Wv_t, Wo_t, tau_t, Wqk_c, Wv_c, Wo_c, tau_c, ln1_w, ln1_b, ln2_w, ln2_b, gamma1, gamma2):
        import math
        import jax, jax.numpy as jnp
        import numpy as np
        D = 256
        H = 16
        CH = 8
        EPS = 1e-05

        def _layernorm(x, w, b):
            mu = jnp.mean(x, axis=-1, keepdims=True)
            var = jnp.mean((x - mu) ** 2, axis=-1, keepdims=True)
            return (x - mu) * jax.lax.rsqrt(var + EPS) * w + b

        def _token_diffusion(x, Wqk, Wv, Wo, tau):
            b, n, d = x.shape
            dh = d // H
            qk = (x @ Wqk).reshape(b, n, H, dh).transpose(0, 2, 1, 3)
            v = (x @ Wv).reshape(b, n, H, dh).transpose(0, 2, 1, 3)
            dot = jnp.einsum('bhnd,bhmd->bhnm', qk, qk)
            q2 = jnp.sum(qk * qk, axis=-1)
            logits = (2.0 * dot - q2[..., :, None] - q2[..., None, :]) / math.sqrt(dh)
            logits = logits * tau
            attn = jax.nn.softmax(logits, axis=-1)
            out = jnp.einsum('bhnm,bhmd->bhnd', attn, v)
            out = out.transpose(0, 2, 1, 3).reshape(b, n, d)
            return out @ Wo

        def _channel_diffusion(x, Wqk, Wv, Wo, tau):
            b, n, d = x.shape
            dh = d // CH
            qk = (x @ Wqk).transpose(0, 2, 1).reshape(b, CH, dh, n)
            v = (x @ Wv).transpose(0, 2, 1).reshape(b, CH, dh, n)
            dot = jnp.einsum('bhcn,bhdn->bhcd', qk, qk)
            q2 = jnp.sum(qk * qk, axis=-1)
            logits = (2.0 * dot - q2[..., :, None] - q2[..., None, :]) / math.sqrt(n)
            logits = logits * tau
            attn = jax.nn.softmax(logits, axis=-1)
            out = jnp.einsum('bhcd,bhdn->bhcn', attn, v)
            out = out.reshape(b, d, n).transpose(0, 2, 1)
            return out @ Wo
        x = x + _token_diffusion(_layernorm(x, ln1_w, ln1_b), Wqk_t, Wv_t, Wo_t, tau_t) * gamma1
        x = x + _channel_diffusion(_layernorm(x, ln2_w, ln2_b), Wqk_c, Wv_c, Wo_c, tau_c) * gamma2
        return x

    def _L0_ffn_ref(x, w_router, w1, b1, w2, b2):
        import jax, jax.numpy as jnp
        import numpy as np
        EMBED_DIM = 256
        HIDDEN_DIM = 1024
        NUM_EXPERTS = 8
        TOP_K = 2
        orig_shape = x.shape
        xf = x.reshape(-1, EMBED_DIM)
        logits = xf @ w_router
        probs = jax.nn.softmax(logits, axis=-1)
        topk_w, topk_idx = jax.lax.top_k(probs, TOP_K)
        mask = jax.nn.one_hot(topk_idx, NUM_EXPERTS, dtype=xf.dtype)
        weights = jnp.sum(topk_w[..., None] * mask, axis=1)
        h = jnp.einsum('te,ieh->tih', xf, w1) + b1
        h = jax.nn.gelu(h)
        out = jnp.einsum('tih,ihe->tie', h, w2) + b2
        out = jnp.sum(out * weights[..., None], axis=1)
        return out.reshape(orig_shape)
    x = L0_attn_x
    x = x + _layernorm(_L0_attn_ref(_layernorm(x, axis=-1), L0_attn_Wqk_t, L0_attn_Wv_t, L0_attn_Wo_t, L0_attn_tau_t, L0_attn_Wqk_c, L0_attn_Wv_c, L0_attn_Wo_c, L0_attn_tau_c, L0_attn_ln1_w, L0_attn_ln1_b, L0_attn_ln2_w, L0_attn_ln2_b, L0_attn_gamma1, L0_attn_gamma2), axis=-1)
    x = x + _layernorm(_L0_ffn_ref(_layernorm(x, axis=-1), L0_ffn_w_router, L0_ffn_w1, L0_ffn_b1, L0_ffn_w2, L0_ffn_b2), axis=-1)
    return x

_drawn_inputs = setup_inputs


def setup_inputs(seed=0):
    import zlib

    import numpy as np

    out = dict(_drawn_inputs(seed))
    spreads = {'L0_attn_tau_t': (1.0, 0.6),
     'L0_attn_tau_c': (1.0, 0.2),
     'L0_attn_ln1_w': (1.0, 0.6),
     'L0_attn_ln1_b': (0.0, 2.0),
     'L0_attn_ln2_w': (1.0, 0.6),
     'L0_attn_ln2_b': (0.0, 0.8),
     'L0_attn_gamma1': (9.999999747378752e-05, 0.6),
     'L0_attn_gamma2': (9.999999747378752e-05, 0.6),
     'L0_ffn_b1': (0.0, 0.1),
     'L0_ffn_b2': (0.0, 0.1)}
    factors = {'L0_attn_Wqk_t': 8.0,
     'L0_attn_Wv_t': 8.0,
     'L0_attn_Wo_t': 8.0,
     'L0_attn_Wv_c': 8.0,
     'L0_attn_Wo_c': 8.0}
    for name, (base, spread) in spreads.items():
        noise = np.random.default_rng([zlib.crc32(name.encode()), seed]).standard_normal(out[name].shape)
        drawn = base * np.exp(spread * noise) if base else spread * noise
        out[name] = jnp.asarray(drawn.astype(out[name].dtype))
    for name, factor in factors.items():
        out[name] = (out[name] * factor).astype(out[name].dtype)
    return out
```

```python
import math
from contextlib import ExitStack

import numpy as np

import concourse.bass as bass
from concourse import mybir

B, N, D = 8, 512, 256
H, DH = 16, 16
CH, CDH = 8, 32
NE, HID = 8, 1024
EPS = 1e-5
P = 128
C = N // P
KC = D // P
TOK = B * N
TROWS = 256
TH = TROWS // P
TILES = (2 * TOK + NE * (TROWS - 1)) // TROWS
THR = TOK // TROWS
ROW = D + 4
WROW = 2 * HID * D // P + HID // P
GROUPS = H // 4
SETS = 2 * GROUPS
UNITS = 4 * SETS
KA = 102
PRE_USES, POST_USES = 7, 22
FREE = 2
LOADS = 16 * 14

CONST = {}
_at = 0
for _name, _width in [("ident", P), ("lower", P), ("ones", P), ("neg_half", P), ("indicator", 2 * H),
                      ("iota8", 4 * NE), ("region", 4 * NE), ("token", B * C), ("steps", NE * THR),
                      ("tiles", TILES), ("iota_t", TILES * NE), ("lane", 1), ("dump", TH)]:
    CONST[_name] = (_at, _width)
    _at += _width
NCONST = _at
VEC = {}
_at = 0
for _name, _width in [("gamma1", D), ("gamma2", D), ("tau_t", H), ("tau_c", 2), ("ln1_w", KC), ("ln1_b", KC),
                      ("ln2_w", KC), ("ln2_b", KC), ("router", KC * NE)]:
    VEC[_name] = (_at, _width)
    _at += _width
NVEC = _at

PRE_AT = {0: ["norm1"], 1: ["xt"], 5: ["qk"], 8: ["sq"], 12: ["v"]}
POST_AT = {2: ["untok"], 3: ["ontok"], 4: ["proj"], 6: ["x2t"], 7: ["qkc"], 8: ["gram"], 9: ["dist"],
           10: ["mix"], 11: ["weff", "chan"], 13: ["z3t"], 14: ["logits"], 15: ["prefix"]}


def schedule(eng, do):
    def body(b, par, pre, post, first):
        for pos in range(2 * SETS):
            do["att"](b, par, pos, first)
            for name in PRE_AT.get(pos, []):
                if pre:
                    do[name](b + 1, 1 - par)
            for name in POST_AT.get(pos, []):
                if post:
                    do[name](b - 1, 1 - par)
            do["att_end"](b, par, pos, first)

    for pos in range(2 * SETS):
        for name in PRE_AT.get(pos, []):
            do[name](0, 0)
    body(0, 0, True, False, True)
    with eng.Fori(0, B // 2 - 1) as lap:
        b = 2 * lap + 1
        body(b, 1, True, True, False)
        body(b + 1, 0, True, True, False)
    body(B - 1, 1, False, True, False)
    do["drain"](B - 1, 1)
    for pos in range(2 * SETS):
        for name in POST_AT.get(pos, []):
            do[name](B - 1, 1)


def at_least(eng, sem, value):
    if not isinstance(value, int) or value > 0:
        eng.wait_ge(sem, value)


def wait_alone(eng, sem, value, spare):
    eng.wait_ge(sem, value)
    eng.sem_inc(spare, 1)


class Chain:
    def __init__(self, eng, sem, per):
        self.eng, self.sem, self.per, self.n, self.b = eng, sem, per, 0, 0

    def did(self, ins):
        ins.then_inc(self.sem, 1)
        self.n += 1

    def at(self, b):
        assert self.n in (0, self.per), (self.n, self.per)
        self.b, self.n = b, 0

    def wait(self, spare=None):
        self.eng.wait_ge(self.sem, self.b * self.per + self.n)
        if spare is not None:
            self.eng.sem_inc(spare, 1)


def program(nc, x, weights, vecs, consts, experts, b2, out):
    f32, bf16, i32, u32 = mybir.dt.float32, mybir.dt.bfloat16, mybir.dt.int32, mybir.dt.uint32
    ACT, ALU, AX = mybir.ActivationFunctionType, mybir.AluOpType, mybir.AxisListType
    ds = bass.ds
    IND = bass.IndirectOffsetOnAxis

    qs = nc.dram_tensor("q_parts", (KC, 3, P, N), bf16, kind="Internal").ap()
    ns = nc.dram_tensor("norm_parts", (H, 3, N), bf16, kind="Internal").ap()
    rows = nc.dram_tensor("expert_rows", (NE * TOK, ROW), f32, kind="Internal").ap()
    ys = nc.dram_tensor("choice_rows", (2 * TOK + TILES * TROWS, D), f32, kind="Internal").ap()

    outer = ExitStack()
    with outer:
        def make(ctx):
            return (lambda n, s, d: ctx.enter_context(nc.sbuf_tensor(n, s, d)),
                    lambda n, s, d: ctx.enter_context(nc.psum_tensor(n, s, d)),
                    lambda n: ctx.enter_context(nc.semaphore(n)))

        sb, _, sem = make(outer)
        alone = sem("alone")
        X = sb("X", [P, B * C, D], f32)
        KT = sb("KT", [P, NCONST], f32)
        COUNT = sb("COUNT", [P, C + 1, NE], f32)

        def const(name):
            a, w = CONST[name]
            return KT[:, a:a + w]

        def rsqrt(v, chain, out_ap, var, y, t):
            chain.did(v.tensor_scalar(y.bitcast(i32), var.bitcast(i32), -0.5, 1597463007.0, ALU.mult, ALU.add))
            chain.wait()
            for n in range(3):
                chain.did(v.tensor_tensor(t, y, y, ALU.mult))
                chain.wait()
                chain.did(v.scalar_tensor_tensor(t, t, -0.5, var, ALU.mult, ALU.mult))
                chain.wait()
                chain.did(v.scalar_tensor_tensor(out_ap if n == 2 else y, t, 1.5, y, ALU.add, ALU.mult))
                chain.wait()

        def stats(v, chain, src, st, mv, var, y, t, r):
            v.sem_inc(alone, 1)
            for c in range(C):
                chain.did(v.bn_stats(st[:, c, :], src(c)))
            chain.wait(alone)
            for c in range(C):
                chain.did(v.bn_aggr(mv[:, c, :], st[:, c, :]))
            chain.wait()
            chain.did(v.tensor_scalar_add(var, mv[:, :, 1], EPS))
            chain.wait()
            rsqrt(v, chain, r, var, y, t)
        STATS = 19

        mix = ExitStack()
        with mix:
            sb, pb, sem = make(mix)
            W = sb("W", [P, 6, KC, D], f32)
            wqk, wv, wo, wqkc, wvt, woc = range(6)
            VV = sb("VV", [P, NVEC], f32)
            MU = sb("MU", [P, B * C], f32)
            RS = sb("RS", [P, B * C], f32)
            ST = sb("ST", [P, C, 6], f32)
            MV = sb("MV", [P, C, 2], f32)
            SM = sb("SM", [P, 6, C], f32)
            Z1 = sb("Z1", [P, C, D], f32)
            XT = sb("XT", [P, KC, N], f32)
            QF = sb("QF", [P, KC, N], f32)
            QR = sb("QR", [P, KC, N], f32)
            QP = sb("QP", [P, KC, 3, N], bf16)
            SQ = sb("SQ", [P, KC, N], f32)
            NF = sb("NF", [H, 2, N], f32)
            NP = sb("NP", [H, 3, N], bf16)
            OPA = sb("OPA", [KA, 2, 8 * N], bf16)
            OPB = sb("OPB", [KA, 2, 8 * N], bf16)
            VA = sb("VA", [P, 2, C, H, 32], f32)
            E = sb("E", [P, 2, 4, 2, N], f32)
            OT = sb("OT", [P, GROUPS, N], f32)
            ON = sb("ON", [P, C, D], f32)
            REC = sb("REC", [P, C, H], f32)
            OTN = sb("OTN", [P, KC, N], f32)
            ST2 = sb("ST2", [P, C, 6], f32)
            MV2 = sb("MV2", [P, C, 2], f32)
            SM2 = sb("SM2", [P, 6, C], f32)
            X1 = sb("X1", [P, C, D], f32)
            Z2, X2T, QC, Z3T = ON, OTN, ON, OTN
            GS = sb("GS", [P, 2, P], f32)
            DG = sb("DG", [P, 2, P], f32)
            L = sb("L", [P, 2, CDH], f32)
            LX = sb("LX", [P, 2, CDH], f32)
            LS = sb("LS", [P, 4, 2], f32)
            AT = sb("AT", [P, 2, P], f32)
            MB = sb("MB", [P, KC, D], f32)
            WE = sb("WE", [P, KC, D], f32)
            PAY = sb("PAY", [P, C, ROW], f32)
            ZERO = sb("ZERO", [P, 8 * ROW], f32)
            LG = sb("LG", [P, C, NE], f32)
            PR = sb("PR", [P, C, NE], f32)
            R4 = sb("R4", [P, 3, C], f32)
            TOP = sb("TOP", [P, C, NE], f32)
            TI = sb("TI", [P, C, NE], u32)
            TF = sb("TF", [P, C, NE], f32)
            OH = sb("OH", [P, 3, C, NE], f32)
            PX = sb("PX", [P, 2, C, NE], f32)
            RK = sb("RK", [P, 3, C, NE], f32)
            SF = sb("SF", [P, 2, C], f32)
            SLOT = sb("SLOT", [P, 2, C], i32)

            PS = pb("PS", [P, 2, 2, N], f32)
            PO = pb("PO", [P, N], f32)
            PA = pb("PA", [P, N], f32)
            PB = pb("PB", [P, 2, N], f32)

            def vec(name):
                a, w = VEC[name]
                return VV[:, a:a + w]

            x_loaded, w_loaded, x_rest = sem("x_loaded"), sem("w_loaded"), sem("x_rest")
            setup_done, setup_pool = sem("setup_done"), sem("setup_pool")
            pre_links, post_links = sem("pre_links"), sem("post_links")
            z1_ready, xt_ready = sem("z1_ready"), sem("xt_ready")
            qf_ready, sq_ready, qp_ready, np_ready = sem("qf_ready"), sem("sq_ready"), sem("qp_ready"), sem("np_ready")
            pre_full, pre_free = sem("pre_full"), sem("pre_free")
            post_full, post_free = sem("post_full"), sem("post_free")
            q_written = sem("q_written")
            op_loaded = [sem("op_loaded0"), sem("op_loaded1")]
            s_full, e_ready, pv_done, po_read = sem("s_full"), sem("e_ready"), sem("pv_done"), sem("po_read")
            on_ready, otn_ready, z2_ready, x2t_ready = sem("on_ready"), sem("otn_ready"), sem("z2_ready"), sem("x2t_ready")
            qc_ready, dg_ready, l_ready, lx_ready, at_ready = (sem("qc_ready"), sem("dg_ready"), sem("l_ready"),
                                                              sem("lx_ready"), sem("at_ready"))
            mb_ready, we_ready, z3_ready, z3t_ready = sem("mb_ready"), sem("we_ready"), sem("z3_ready"), sem("z3t_ready")
            lg_ready, pr_ready, oh_ready, slot_ready = sem("lg_ready"), sem("pr_ready"), sem("oh_ready"), sem("slot_ready")
            rows_clear = sem("rows_clear")
            sent, rows_free = sem("sent"), sem("rows_free")

            block = mix.enter_context(nc.Block())

            @block.sync
            def _(sp):
                xv = x.rearrange("(b p c) e -> b p c e", p=P, c=C)
                sp.dma_start(X[:, 0:C, :], xv[0]).then_inc(x_loaded, 16)
                sp.dma_start(VV[:, :], vecs).then_inc(w_loaded, 16)
                sp.dma_start(KT[:, :], consts).then_inc(w_loaded, 16)
                sp.dma_start(W[:, :, :, :], weights.rearrange("p (w k n) -> p w k n", w=6, k=KC)).then_inc(w_loaded, 16)
                for b in range(1, B):
                    sp.dma_start(X[:, C * b:C * b + C, :], xv[b]).then_inc(x_rest, 16)
                sp.wait_ge(setup_pool, 4)
                for i in range(NE * TOK // (8 * P)):
                    sp.dma_start(rows[8 * P * i:8 * P * (i + 1)].rearrange("(p r) e -> p (r e)", p=P), ZERO[:, :]
                                 ).then_inc(rows_clear, 16)
                sp.wait_ge(setup_done, 1)

                def store(b, m):
                    wait_alone(sp, qp_ready, KC * b + m + 1, alone)
                    at_least(sp, op_loaded[m], LOADS * b)
                    sp.dma_start(qs[m].rearrange("x p n -> p x n"), QP[:, m, :, :]).then_inc(q_written, 16)

                def store_norms(b):
                    at_least(sp, np_ready, b + 1)
                    sp.dma_start(ns, NP[:, :, :]).then_inc(q_written, 16)

                def load(b, m):
                    wait_alone(sp, q_written, 48 * (b + 1), alone)
                    at_least(sp, s_full, UNITS * b - UNITS // 2 * (1 - m))
                    v = qs[m]
                    src = [v[k].rearrange("(h d) n -> d h n", d=DH) for k in range(3)]
                    a, o = OPA[:, m, :].rearrange("p (h n) -> p h n", h=8), OPB[:, m, :].rearrange("p (h n) -> p h n", h=8)
                    order_a, order_b = (0, 1, 2, 0, 1, 0), (0, 0, 0, 1, 1, 2)
                    for k in range(6):
                        sp.dma_start(a[DH * k:DH * k + DH], src[order_a[k]]).then_inc(op_loaded[m], 16)
                        sp.dma_start(o[DH * k:DH * k + DH], src[order_b[k]]).then_inc(op_loaded[m], 16)
                    nv = ns[8 * m:8 * m + 8].rearrange("h x n -> x h n")
                    sp.dma_start(a[6 * DH:6 * DH + 3], nv).then_inc(op_loaded[m], 16)
                    sp.dma_start(o[6 * DH + 3:6 * DH + 6], nv).then_inc(op_loaded[m], 16)

                def nothing(*_):
                    pass

                def att(b, par, pos, first):
                    if pos == 2:
                        load(b, 1)

                do = dict.fromkeys(["norm1", "xt", "qk", "v", "untok", "ontok", "proj", "x2t", "qkc", "gram",
                                    "dist", "mix", "weff", "chan", "z3t", "logits", "prefix", "drain", "att_end"], nothing)
                do["att"] = att

                def sq(b, par):
                    store(b, 0)
                    store(b, 1)
                    store_norms(b)
                    load(b, 0)
                do["sq"] = sq
                schedule(sp, do)

            @block.gpsimd
            def _(pool):
                g = nc.gpsimd
                pool.sem_inc(rows_free, 1)
                g.memset(VA[:, :, :, :, :], 1.0).then_inc(setup_pool, 1)
                g.memset(AT[:, :, :], 0.0).then_inc(setup_pool, 1)
                g.memset(ZERO[:, :], 0.0).then_inc(setup_pool, 1)
                g.memset(COUNT[:, :, :], 0.0).then_inc(setup_pool, 1)

                def nothing(*_):
                    pass
                do = dict.fromkeys(["att", "att_end", "drain", "norm1", "xt", "qk", "v", "untok", "ontok", "proj", "x2t",
                                    "qkc", "gram", "dist", "mix", "weff", "chan", "z3t", "logits", "prefix", "sq"], nothing)

                def qk(b, par):
                    for m in range(KC):
                        pool.wait_ge(qf_ready, KC * b + m + 1)
                        g.tensor_tensor(SQ[:, m, :], QF[:, m, :], QF[:, m, :], ALU.mult).then_inc(sq_ready, 1)
                do["qk"] = qk

                def prefix(b, par):
                    if isinstance(b, int) and b == 0 or not isinstance(b, int):
                        pool.wait_ge(rows_clear, 16 * NE * TOK // (8 * P))
                    wait_alone(pool, slot_ready, b + 1, alone)
                    for c in range(C):
                        for k in range(2):
                            g.indirect_dma_start(out=rows, out_offset=IND(ap=SLOT[:, k, c:c + 1], axis=0),
                                                 in_=PAY[:, c, :], in_offset=None).then_inc(sent, 16)
                    pool.wait_ge(sent, 16 * 2 * C * (b + 1))
                    pool.sem_inc(rows_free, 1)
                do["prefix"] = prefix
                schedule(pool, do)

            @block.scalar
            def _(act):
                a = nc.scalar
                act.wait_ge(setup_done, 1)

                def nothing(*_):
                    pass
                do = dict.fromkeys(["norm1", "xt", "qk", "sq", "v", "untok", "ontok", "proj", "x2t",
                                    "qkc", "gram", "mix", "weff", "chan", "z3t", "prefix"], nothing)

                def att(b, par, pos, first):
                    s = pos // 2
                    if pos % 2 == 0:
                        at_least(act, pv_done, SETS * b + s - 1)
                    for i in range(2):
                        h = 2 * (pos % 2) + i
                        u = 4 * s + h
                        act.wait_ge(s_full, UNITS * b + u + 1)
                        a.activation(E[:, s % 2, h, :, :], PS[:, u % 2, :, :], ACT.Exp,
                                     scale=vec("tau_t")[:, 4 * (s // 2) + h:4 * (s // 2) + h + 1]).then_inc(e_ready, 1)
                do["att"] = att

                def evacuate(b, g):
                    act.wait_ge(pv_done, SETS * b + 2 * g + 2)
                    if g == 0:
                        at_least(act, post_full, POST_USES * (b - 1) + C)
                    a.copy(OT[:, g, :], PO[:, :]).then_inc(po_read, 1)

                def att_end(b, par, pos, first):
                    if pos % 4 == 1:
                        if pos > 1:
                            evacuate(b, pos // 4 - 1)
                        elif not first:
                            evacuate(b - 1, GROUPS - 1)
                do["att_end"] = att_end
                do["drain"] = lambda b, par: evacuate(b, GROUPS - 1)

                def dist(b, par):
                    act.wait_ge(l_ready, b + 1)
                    for k in range(2):
                        a.activation(LX[:, k, :], L[:, k, :], ACT.Exp, bias=LS[:, 1, k:k + 1],
                                     accum_out=LS[:, 2, k:k + 1]).then_inc(lx_ready, 1)
                do["dist"] = dist

                def logits(b, par):
                    act.wait_ge(lg_ready, b + 1)
                    a.activation(PR[:, :, :], LG[:, :, :], ACT.Exp).then_inc(pr_ready, 1)
                do["logits"] = logits
                schedule(act, do)

            @block.vector
            def _(dve):
                v = nc.vector
                v.memset(OPA[6 * DH:KA, :, :], 1.0)
                v.memset(OPB[6 * DH:KA, :, :], 1.0)
                dve.sem_inc(post_free, FREE)
                dve.wait_ge(w_loaded, 48)
                dve.wait_ge(setup_pool, 4)
                v.tensor_scalar_mul(vec("tau_t"), vec("tau_t"), 2.0 / math.sqrt(DH))
                v.tensor_scalar_mul(vec("tau_c"), vec("tau_c"), 2.0 / math.sqrt(N))
                for k in range(KC):
                    v.tensor_tensor(W[:, wo, k, :], W[:, wo, k, :], vec("gamma1"), ALU.mult)
                    last = v.tensor_tensor(W[:, woc, k, :], W[:, woc, k, :], vec("gamma2"), ALU.mult)
                last.then_inc(setup_done, 1)
                dve.wait_ge(setup_done, 1)

                pre = Chain(dve, pre_links, STATS + 16 + 2 * KC + 3)
                post = Chain(dve, post_links, 3 * STATS + 6 * C + 27)

                def take(b, j):
                    dve.wait_ge(pre_full, PRE_USES * b + j + 1)

                def takep(b, j):
                    dve.wait_ge(post_full, POST_USES * b + j + 1)
                    return PB[:, j % 2, :]

                def xs(b, c, n=1):
                    return X[:, ds(C * b + c, n), :]

                def nothing(*_):
                    pass
                do = dict.fromkeys(["att", "att_end", "drain"], nothing)

                def norm1(b, par):
                    pre.at(b)
                    if isinstance(b, int) and b == 0:
                        dve.wait_ge(x_loaded, 16)
                    if isinstance(b, int) and b == 1:
                        dve.wait_ge(x_rest, 16 * (B - 1))
                    var, y, t, r, var2, s1 = (SM[:, i, :] for i in range(6))
                    stats(v, pre, lambda c: X[:, ds(C * b + c, 1), :].rearrange("p a e -> p (a e)"), ST, MV, var, y, t, r)
                    pre.did(v.tensor_copy(MU[:, ds(C * b, C)], MV[:, :, 0]))
                    pre.did(v.tensor_copy(RS[:, ds(C * b, C)], r))
                    pre.did(v.tensor_tensor(t, r, r, ALU.mult))
                    pre.wait()
                    pre.did(v.tensor_tensor(t, t, MV[:, :, 1], ALU.mult))
                    pre.wait()
                    pre.did(v.tensor_scalar_add(var2, t, EPS))
                    pre.wait()
                    rsqrt(v, pre, s1, var2, y, t)
                    pre.did(v.tensor_tensor(s1, s1, r, ALU.mult))
                    pre.wait()
                    for c in range(C):
                        i = v.tensor_scalar(Z1[:, c:c + 1, :], xs(b, c), MV[:, c, 0:1], s1[:, c:c + 1],
                                            ALU.subtract, ALU.mult)
                    i.then_inc(z1_ready, 1)
                do["norm1"] = norm1

                def xt(b, par):
                    for k in range(KC):
                        take(b, k)
                        i = v.tensor_scalar(XT[:, k, :], PA[:, :], vec("ln1_w")[:, k:k + 1], vec("ln1_b")[:, k:k + 1],
                                            ALU.mult, ALU.add)
                        i.then_inc(pre_free, 1)
                do["xt"] = xt

                def qk(b, par):
                    at_least(dve, q_written, 48 * b)
                    at_least(dve, sq_ready, KC * b)
                    for m in range(KC):
                        take(b, 2 + m)
                        v.tensor_copy(QF[:, m, :], PA[:, :]).then_inc(pre_free, 1)
                        dve.wait_ge(pre_free, PRE_USES * b + 3 + m)
                        v.tensor_copy(QP[:, m, 0, :], QF[:, m, :]).then_inc(qf_ready, 1)
                        dve.wait_ge(qf_ready, KC * b + m + 1)
                        pre.did(v.tensor_tensor(QR[:, m, :], QF[:, m, :], QP[:, m, 0, :], ALU.subtract))
                        pre.wait()
                        pre.did(v.tensor_copy(QP[:, m, 1, :], QR[:, m, :]))
                        pre.wait()
                        v.tensor_tensor(QP[:, m, 2, :], QR[:, m, :], QP[:, m, 1, :], ALU.subtract).then_inc(qp_ready, 1)
                do["qk"] = qk

                def sq(b, par):
                    take(b, 4)
                    v.tensor_copy(NF[:, 0, :], PA[0:H, :]).then_inc(pre_free, 1)
                    dve.wait_ge(pre_free, PRE_USES * b + 5)
                    pre.did(v.tensor_copy(NP[:, 0, :], NF[:, 0, :]))
                    pre.wait()
                    pre.did(v.tensor_tensor(NF[:, 1, :], NF[:, 0, :], NP[:, 0, :], ALU.subtract))
                    pre.wait()
                    pre.did(v.tensor_copy(NP[:, 1, :], NF[:, 1, :]))
                    pre.wait()
                    v.tensor_tensor(NP[:, 2, :], NF[:, 1, :], NP[:, 1, :], ALU.subtract).then_inc(np_ready, 1)
                do["sq"] = sq

                def vv(b, par):
                    at_least(dve, pv_done, SETS * (b - 1))
                    for i in range(2):
                        take(b, 5 + i)
                        v.tensor_copy(VA[:, par, 2 * i:2 * i + 2, :, 0:DH],
                                      PA[:, :].rearrange("p (c h d) -> p c h d", c=2, h=H)).then_inc(pre_free, 1)
                do["v"] = vv

                def untok(b, par):
                    post.at(b)
                    for c in range(C):
                        ps = takep(b, c).rearrange("p (h e) -> p h e", e=32)
                        post.did(v.reciprocal(REC[:, c, :], ps[:, :, DH]))
                        post.wait()
                        v.tensor_tensor(ON[:, c, :].rearrange("p (h e) -> p h e", e=DH), ps[:, :, 0:DH],
                                        REC[:, c, :].unsqueeze(2).to_broadcast([P, H, DH]), ALU.mult).then_inc(post_free, 1)
                do["untok"] = untok

                def ontok(b, par):
                    for m in range(KC):
                        v.tensor_copy(OTN[:, m, :], takep(b, 4 + m)).then_inc(post_free, 1)
                    mus, rss = SM2[:, 4, :], SM2[:, 5, :]
                    post.did(v.tensor_copy(mus, MU[:, ds(C * b, C)]))
                    post.did(v.tensor_copy(rss, RS[:, ds(C * b, C)]))
                    post.wait()
                    for c in range(C):
                        post.did(v.tensor_scalar(X1[:, c:c + 1, :], xs(b, c), mus[:, c:c + 1], rss[:, c:c + 1],
                                                 ALU.subtract, ALU.mult))
                    post.wait()
                do["ontok"] = ontok

                def stats2(b, src):
                    var, y, t, r = (SM2[:, i, :] for i in range(4))
                    stats(v, post, src, ST2, MV2, var, y, t, r)
                    return MV2, r

                def proj(b, par):
                    for i in range(2):
                        v.tensor_tensor(X1[:, 2 * i:2 * i + 2, :], takep(b, 6 + i).rearrange("p (c e) -> p c e", c=2),
                                        X1[:, 2 * i:2 * i + 2, :], ALU.add).then_inc(post_free, 1)
                    dve.wait_ge(post_free, FREE + POST_USES * b + 8)
                    mv, r = stats2(b, lambda c: X1[:, c, :])
                    for c in range(C):
                        i = v.tensor_scalar(Z2[:, c, :], X1[:, c, :], mv[:, c, 0:1], r[:, c:c + 1], ALU.subtract, ALU.mult)
                    i.then_inc(z2_ready, 1)
                do["proj"] = proj

                def x2t(b, par):
                    for k in range(KC):
                        v.tensor_scalar(X2T[:, k, :], takep(b, 8 + k), vec("ln2_w")[:, k:k + 1], vec("ln2_b")[:, k:k + 1],
                                        ALU.mult, ALU.add).then_inc(post_free, 1)
                do["x2t"] = x2t

                def qkc(b, par):
                    for i in range(2):
                        v.tensor_copy(QC[:, 2 * i:2 * i + 2, :],
                                      takep(b, 10 + i).rearrange("p (c e) -> p c e", c=2)).then_inc(post_free, 1)
                do["qkc"] = qkc

                def gram(b, par):
                    v.tensor_copy(GS[:, :, :], takep(b, 12)[:, 0:2 * P].rearrange("p (k e) -> p k e", k=2)).then_inc(post_free, 1)
                    dve.wait_ge(post_free, FREE + POST_USES * b + 13)
                    v.tensor_tensor(DG[:, :, :], GS[:, :, :], const("ident").unsqueeze(1).to_broadcast([P, 2, P]),
                                    ALU.mult).then_inc(dg_ready, 1)
                do["gram"] = gram

                def dist(b, par):
                    ps = takep(b, 13)[:, 0:2 * P].rearrange("p (k e) -> p k e", k=2)
                    for q in range(4):
                        r = slice(CDH * q, CDH * q + CDH)
                        i = v.tensor_tensor(L[r, :, :], ps[r, :, r], GS[r, :, r], ALU.add)
                        if q < 3:
                            post.did(i)
                    i.then_inc(post_free, 1)
                    dve.wait_ge(post_free, FREE + POST_USES * b + 14)
                    post.wait()
                    for k in range(2):
                        post.did(v.tensor_scalar_mul(L[:, k, :], L[:, k, :], vec("tau_c")[:, k:k + 1]))
                    post.wait()
                    post.did(v.reduce_max(LS[:, 0, :], L[:, :, :], AX.X))
                    post.wait()
                    v.tensor_scalar_mul(LS[:, 1, :], LS[:, 0, :], -1.0).then_inc(l_ready, 1)
                do["dist"] = dist

                def mixc(b, par):
                    dve.wait_ge(lx_ready, 2 * b + 2)
                    post.did(v.reciprocal(LS[:, 3, :], LS[:, 2, :]))
                    post.wait()
                    for k in range(2):
                        post.did(v.tensor_scalar_mul(LX[:, k, :], LX[:, k, :], LS[:, 3, k:k + 1]))
                    post.wait()
                    for q in range(4):
                        r = slice(CDH * q, CDH * q + CDH)
                        i = v.tensor_copy(AT[r, :, r], LX[r, :, :])
                    i.then_inc(at_ready, 1)
                    v.tensor_copy(MB[:, :, :], takep(b, 14).rearrange("p (k e) -> p k e", k=2)).then_inc(post_free, 1)
                do["mix"] = mixc

                def weff(b, par):
                    v.tensor_copy(WE[:, :, :], takep(b, 15).rearrange("p (k e) -> p k e", k=2)).then_inc(post_free, 1)
                do["weff"] = weff

                def chan(b, par):
                    for i in range(2):
                        v.tensor_tensor(X1[:, 2 * i:2 * i + 2, :], takep(b, 16 + i).rearrange("p (c e) -> p c e", c=2),
                                        X1[:, 2 * i:2 * i + 2, :], ALU.add).then_inc(post_free, 1)
                    dve.wait_ge(post_free, FREE + POST_USES * b + 18)
                    mv, r = stats2(b, lambda c: X1[:, c, :])
                    for c in range(C):
                        post.did(v.tensor_scalar(X1[:, c, :], X1[:, c, :], mv[:, c, 0:1], r[:, c:c + 1], ALU.subtract, ALU.mult))
                    post.wait()
                    post.did(v.tensor_tensor(xs(b, 0, C), xs(b, 0, C), X1[:, :, :], ALU.add))
                    post.wait()
                    mv, r = stats2(b, lambda c: X[:, ds(C * b + c, 1), :].rearrange("p a e -> p (a e)"))
                    dve.wait_ge(rows_free, b + 1)
                    for c in range(C):
                        i = v.tensor_scalar(PAY[:, c:c + 1, 0:D], xs(b, c), mv[:, c, 0:1], r[:, c:c + 1], ALU.subtract, ALU.mult)
                    i.then_inc(z3_ready, 1)
                do["chan"] = chan

                def z3t(b, par):
                    for k in range(KC):
                        v.tensor_copy(Z3T[:, k, :], takep(b, 18 + k)).then_inc(post_free, 1)
                do["z3t"] = z3t

                def bc(ap):
                    return ap.unsqueeze(2).to_broadcast([P, C, NE])

                def logits(b, par):
                    ps = takep(b, 20)[:, 0:C * NE].rearrange("p (c e) -> p c e", e=NE)
                    post.did(v.reduce_max(R4[:, 0, :], ps, AX.X))
                    post.wait()
                    v.tensor_tensor(LG[:, :, :], ps, bc(R4[:, 0, :]), ALU.subtract).then_inc(post_free, 1)
                    dve.wait_ge(post_free, FREE + POST_USES * b + 21)
                    v.tensor_copy(PAY[:, :, D + 3], const("token").rearrange("p (b c) -> p b c", c=C)[:, ds(b, 1), :]
                                  .rearrange("p a c -> p (a c)")).then_inc(lg_ready, 1)
                    dve.wait_ge(pr_ready, b + 1)
                    post.did(v.reduce_sum(R4[:, 1, :], PR[:, :, :], AX.X))
                    post.wait()
                    post.did(v.reciprocal(R4[:, 2, :], R4[:, 1, :]))
                    post.wait()
                    post.did(v.tensor_tensor(PR[:, :, :], PR[:, :, :], bc(R4[:, 2, :]), ALU.mult))
                    post.wait(alone)
                    for c in range(C):
                        post.did(v.max(TOP[:, c, :], PR[:, c, :]))
                    post.wait(alone)
                    for c in range(C):
                        post.did(v.max_index(TI[:, c, :], TOP[:, c, :], PR[:, c, :]))
                    post.wait()
                    post.did(v.tensor_copy(TF[:, :, 0:2], TI[:, :, 0:2]))
                    post.wait()
                    iota = const("iota8").rearrange("p (c e) -> p c e", e=NE)
                    for k in range(2):
                        post.did(v.tensor_tensor(OH[:, k, :, :], iota, bc(TF[:, :, k]), ALU.is_equal))
                    post.did(v.tensor_copy(PAY[:, :, D:D + 2], TOP[:, :, 0:2]))
                    post.did(v.tensor_copy(PAY[:, :, D + 2], TF[:, :, 0]))
                    post.wait()
                    v.tensor_tensor(OH[:, 2, :, :], OH[:, 0, :, :], OH[:, 1, :, :], ALU.add).then_inc(oh_ready, 1)
                do["logits"] = logits

                def prefix(b, par):
                    v.tensor_copy(PX[:, :, :, :], takep(b, 21)[:, 0:2 * C * NE].rearrange("p (k c e) -> p k c e", k=2, c=C)
                                  ).then_inc(post_free, 1)
                    dve.wait_ge(post_free, FREE + POST_USES * b + 22)
                    for c in range(C):
                        post.did(v.tensor_tensor(COUNT[:, c + 1, :], COUNT[:, c, :], PX[:, 1, c, :], ALU.add))
                        post.wait()
                    post.did(v.tensor_tensor(RK[:, 0, :, :], COUNT[:, 0:C, :], PX[:, 0, :, :], ALU.add))
                    post.wait()
                    post.did(v.tensor_copy(COUNT[:, 0, :], COUNT[:, C, :]))
                    post.did(v.tensor_tensor(RK[:, 0, :, :], RK[:, 0, :, :],
                                             const("region").rearrange("p (c e) -> p c e", e=NE), ALU.add))
                    post.wait()
                    for k in range(2):
                        post.did(v.tensor_tensor(RK[:, 1 + k, :, :], RK[:, 0, :, :], OH[:, k, :, :], ALU.mult))
                    post.wait()
                    post.did(v.reduce_sum(SF[:, :, :], RK[:, 1:3, :, :], AX.X))
                    post.wait()
                    v.tensor_copy(SLOT[:, :, :], SF[:, :, :]).then_inc(slot_ready, 1)
                do["prefix"] = prefix
                schedule(dve, do)

            @block.tensor
            def _(pe):
                t = nc.tensor
                ident = const("ident")
                pe.wait_ge(w_loaded, 48)
                pe.wait_ge(setup_done, 1)

                def give(b, j):
                    at_least(pe, pre_free, PRE_USES * b + j)
                    return PA

                def givep(b, j):
                    pe.wait_ge(post_free, FREE + POST_USES * b + j - 1)
                    return PB[:, j % 2, :]

                do = {}

                def pv(b, par, s, jc):
                    g, jp = s // 2, s % 2
                    if jc == 0:
                        pe.wait_ge(e_ready, UNITS * b + 4 * s + 4)
                        if jp == 0:
                            at_least(pe, po_read, GROUPS * b + g)
                    for h in range(4):
                        i = t.matmul(PO[32 * h:32 * h + 32, :], VA[:, par, 2 * jp + jc, 4 * g + h, :],
                                     E[:, s % 2, h, jc, :], start=(jp == 0 and jc == 0), stop=(jp == 1 and jc == 1))
                    if jc == 1:
                        i.then_inc(pv_done, 1)

                def att(b, par, pos, first):
                    s = pos // 2
                    m = s // (SETS // 2)
                    if pos == 0:
                        pe.wait_ge(pre_free, PRE_USES * (b + 1))
                    if pos % SETS == 0:
                        pe.wait_ge(op_loaded[m], LOADS * (b + 1))
                    for i in range(2):
                        h = 2 * (pos % 2) + i
                        u = 4 * s + h
                        at_least(pe, e_ready, UNITS * b + u - 1)
                        hh = (4 * (s // 2) + h) % 8
                        for jc in range(2):
                            key = hh * N + (2 * (s % 2) + jc) * P
                            ins = t.matmul(PS[:, u % 2, jc, :], OPA[0:KA, m, key:key + P], OPB[0:KA, m, hh * N:hh * N + N],
                                           start=True, stop=True)
                        ins.then_inc(s_full, 1)
                do["att"] = att

                def att_end(b, par, pos, first):
                    if pos > 1:
                        pv(b, par, pos // 2 - 1, pos % 2)
                    elif not first:
                        pv(b - 1, 1 - par, SETS - 1, pos % 2)
                do["att_end"] = att_end

                def drain(b, par):
                    pv(b, par, SETS - 1, 0)
                    pv(b, par, SETS - 1, 1)
                do["drain"] = drain

                def norm1(b, par):
                    pass
                do["norm1"] = norm1

                def xt(b, par):
                    pe.wait_ge(z1_ready, b + 1)
                    for k in range(KC):
                        ps = give(b, k)
                        for c in range(C):
                            i = t.transpose(ps[:, c * P:c * P + P], Z1[:, c, k * P:k * P + P], ident)
                        i.then_inc(pre_full, 1)
                do["xt"] = xt

                def qk(b, par):
                    for m in range(KC):
                        ps = give(b, 2 + m)
                        for k in range(KC):
                            i = t.matmul(ps[:, :], W[:, wqk, k, m * P:m * P + P], XT[:, k, :], start=(k == 0), stop=(k == KC - 1))
                        i.then_inc(pre_full, 1)
                do["qk"] = qk

                def sq(b, par):
                    ps = give(b, 4)
                    for m in range(KC):
                        pe.wait_ge(sq_ready, KC * b + m + 1)
                        i = t.matmul(ps[0:H, :], const("indicator")[:, H * m:H * m + H], SQ[:, m, :], start=(m == 0), stop=(m == KC - 1))
                    i.then_inc(pre_full, 1)
                do["sq"] = sq

                def vv(b, par):
                    for i in range(2):
                        ps = give(b, 5 + i)
                        for c in range(2):
                            for k in range(KC):
                                cc = 2 * i + c
                                ins = t.matmul(ps[:, c * D:c * D + D], XT[:, k, cc * P:cc * P + P], W[:, wv, k, :],
                                               start=(k == 0), stop=(k == KC - 1))
                        ins.then_inc(pre_full, 1)
                do["v"] = vv

                def untok(b, par):
                    pe.wait_ge(po_read, GROUPS * (b + 1))
                    for c in range(C):
                        ps = givep(b, c)
                        for g in range(GROUPS):
                            i = t.transpose(ps[:, g * P:g * P + P], OT[:, g, c * P:c * P + P], ident)
                        i.then_inc(post_full, 1)
                do["untok"] = untok

                def ontok(b, par):
                    pe.wait_ge(post_free, FREE + POST_USES * b + C)
                    for m in range(KC):
                        ps = givep(b, 4 + m)
                        for c in range(C):
                            i = t.transpose(ps[:, c * P:c * P + P], ON[:, c, m * P:m * P + P], ident)
                        i.then_inc(post_full, 1)
                do["ontok"] = ontok

                def rows_times(b, j, lhs, rhs):
                    for i in range(2):
                        ps = givep(b, j + i)
                        for c in range(2):
                            for k in range(KC):
                                cc = 2 * i + c
                                ins = t.matmul(ps[:, c * D:c * D + D], lhs[:, k, cc * P:cc * P + P], rhs(k),
                                               start=(k == 0), stop=(k == KC - 1))
                        ins.then_inc(post_full, 1)

                def proj(b, par):
                    pe.wait_ge(post_free, FREE + POST_USES * b + 6)
                    rows_times(b, 6, OTN, lambda k: W[:, wo, k, :])
                do["proj"] = proj

                def x2t(b, par):
                    pe.wait_ge(z2_ready, b + 1)
                    for k in range(KC):
                        ps = givep(b, 8 + k)
                        for c in range(C):
                            i = t.transpose(ps[:, c * P:c * P + P], Z2[:, c, k * P:k * P + P], ident)
                        i.then_inc(post_full, 1)
                do["x2t"] = x2t

                def qkc(b, par):
                    pe.wait_ge(post_free, FREE + POST_USES * b + 10)
                    rows_times(b, 10, X2T, lambda k: W[:, wqkc, k, :])
                do["qkc"] = qkc

                def gram(b, par):
                    pe.wait_ge(post_free, FREE + POST_USES * b + 12)
                    ps = givep(b, 12)
                    for k in range(2):
                        for c in range(C):
                            i = t.matmul(ps[:, k * P:k * P + P], QC[:, c, k * P:k * P + P], QC[:, c, k * P:k * P + P],
                                         start=(c == 0), stop=(c == C - 1))
                    i.then_inc(post_full, 1)
                do["gram"] = gram

                def dist(b, par):
                    pe.wait_ge(dg_ready, b + 1)
                    ps = givep(b, 13)
                    for k in range(2):
                        t.matmul(ps[:, k * P:k * P + P], DG[:, k, :], const("neg_half"), start=True, stop=False)
                        i = t.matmul(ps[:, k * P:k * P + P], const("neg_half"), DG[:, k, :], start=False, stop=True)
                    i.then_inc(post_full, 1)
                do["dist"] = dist

                def mixc(b, par):
                    pe.wait_ge(at_ready, b + 1)
                    ps = givep(b, 14)
                    for k in range(2):
                        i = t.matmul(ps[:, k * D:k * D + D], AT[:, k, :], W[:, woc, k, :], start=True, stop=True)
                    i.then_inc(post_full, 1)
                do["mix"] = mixc

                def weff(b, par):
                    pe.wait_ge(post_free, FREE + POST_USES * b + 15)
                    ps = givep(b, 15)
                    for m in range(KC):
                        for k in range(KC):
                            i = t.matmul(ps[:, m * D:m * D + D], W[:, wvt, k, m * P:m * P + P], MB[:, k, :],
                                         start=(k == 0), stop=(k == KC - 1))
                    i.then_inc(post_full, 1)
                do["weff"] = weff

                def chan(b, par):
                    pe.wait_ge(post_free, FREE + POST_USES * b + 16)
                    rows_times(b, 16, X2T, lambda k: WE[:, k, :])
                do["chan"] = chan

                def z3t(b, par):
                    pe.wait_ge(z3_ready, b + 1)
                    for k in range(KC):
                        ps = givep(b, 18 + k)
                        for c in range(C):
                            i = t.transpose(ps[:, c * P:c * P + P], PAY[:, c, k * P:k * P + P], ident)
                        i.then_inc(post_full, 1)
                do["z3t"] = z3t

                def logits(b, par):
                    pe.wait_ge(post_free, FREE + POST_USES * b + 20)
                    ps = givep(b, 20)
                    for c in range(C):
                        for k in range(KC):
                            i = t.matmul(ps[:, c * NE:c * NE + NE], Z3T[:, k, c * P:c * P + P], vec("router")[:, k * NE:k * NE + NE],
                                         start=(k == 0), stop=(k == KC - 1))
                    i.then_inc(post_full, 1)
                do["logits"] = logits

                def prefix(b, par):
                    pe.wait_ge(oh_ready, b + 1)
                    ps = givep(b, 21)
                    sel = OH[:, 2, :, :].rearrange("p c e -> p (c e)")
                    t.matmul(ps[:, 0:C * NE], const("lower"), sel, start=True, stop=True)
                    t.matmul(ps[:, C * NE:2 * C * NE], const("ones"), sel, start=True, stop=True).then_inc(post_full, 1)
                do["prefix"] = prefix
                schedule(pe, do)

        stage2(nc, make, X, COUNT, const, alone, rows, ys, experts, b2)
        stage3(nc, make, X, stats, STATS, ys, out)


def stage2(nc, make, X, COUNT, const, alone, rows, ys, experts, b2):
    f32, i32 = mybir.dt.float32, mybir.dt.int32
    ACT, ALU, AX = mybir.ActivationFunctionType, mybir.AluOpType, mybir.AxisListType
    ds = bass.ds
    IND = bass.IndirectOffsetOnAxis
    RING = 3
    W1, W2 = KC * HID, HID // P * D
    HC = HID // P
    assert TILES % RING == 0
    ctx = ExitStack()
    with ctx:
        sb, pb, sem = make(ctx)
        TB = sb("TB", [P, TILES, NE], f32)
        OE = sb("OE", [P, TILES, NE], f32)
        T1 = sb("T1", [P, NE], f32)
        CS = sb("CS", [P, 2, 2 * NE], f32)
        TS = sb("TS", [P, NE, THR], f32)
        TF = sb("TFE", [P, 6, TILES], f32)
        RF = sb("RF", [P, TILES, 8], f32)
        RI = sb("RI", [P, TILES, 4], i32)
        IX = sb("IX", [P, RING, 4], i32)
        FX = sb("FX", [P, RING, 8], f32)
        XG = sb("XG", [P, RING, TH, ROW], f32)
        WG = sb("WG", [P, RING, WROW], f32)
        BG = sb("BG", [P, RING, D], f32)
        XT = sb("XTE", [P, KC, TROWS], f32)
        HT = sb("HT", [P, RING, HC, TROWS], f32)
        Y = sb("Y", [P, RING, TH, D], f32)
        G = sb("G", [P, RING, 4, TH], f32)
        DI = sb("DI", [P, RING, TH], i32)
        PT = pb("PT", [P, KC, TROWS], f32)
        PH = pb("PH", [P, HC // 2, 2, TROWS], f32)
        PY = pb("PY", [P, RING, TH, D], f32)

        table_links, tile_links = sem("table_links"), sem("tile_links")
        ix_ready = [sem(f"ix_ready{r}") for r in range(RING)]
        gathered = [sem(f"gathered{r}") for r in range(RING)]
        xt_full, xt_copied = sem("xt_full"), sem("xt_copied")
        h_full, h_ready = sem("h_full"), sem("h_ready")
        y_full, y_read, y_ready = sem("y_full"), sem("y_read"), sem("y_ready")
        y_sent = [sem(f"y_sent{r}") for r in range(RING)]
        block = ctx.enter_context(nc.Block())
        LAPS = TILES // RING

        def over_tiles(eng, do):
            for r in range(RING):
                do(0, r, r)
            with eng.Fori(1, LAPS - 1) as lap:
                for r in range(RING):
                    do(lap, r, lap * RING + r)
            for r in range(RING):
                do(LAPS - 1, r, TILES - RING + r)

        def follows(tile, n):
            return not isinstance(tile, int) or tile + n < TILES

        @block.vector
        def _(dve):
            v = nc.vector
            linked = [0]

            def link(i):
                linked[0] += 1
                i.then_inc(table_links, 1)
                dve.wait_ge(table_links, linked[0])

            rows_of = COUNT[:, 0, :]
            link(v.memset(CS[:, :, :], 0.0))
            link(v.tensor_tensor(TS[:, :, :], rows_of.unsqueeze(2).to_broadcast([P, NE, THR]),
                                 const("steps").rearrange("p (e k) -> p e k", e=NE), ALU.is_gt))
            link(v.reduce_sum(T1[:, :], TS[:, :, :], AX.X))
            link(v.tensor_copy(CS[:, 0, NE:2 * NE], T1[:, :]))
            for n, s in enumerate((1, 2, 4)):
                a, o = CS[:, n % 2, :], CS[:, (n + 1) % 2, :]
                link(v.tensor_tensor(o[:, NE:2 * NE], a[:, NE:2 * NE], a[:, NE - s:2 * NE - s], ALU.add))
            ends = CS[:, 1, NE:2 * NE]
            tile, expert, first, n_rows, rank, t = (TF[:, i, :] for i in range(6))
            link(v.tensor_scalar(t, const("tiles"), 1.0, None, ALU.add))
            link(v.tensor_scalar(tile, t, ends[:, NE - 1:NE], -1.0, ALU.min, ALU.add))
            link(v.tensor_tensor(TB[:, :, :], tile.unsqueeze(2).to_broadcast([P, TILES, NE]),
                                 ends.unsqueeze(1).to_broadcast([P, TILES, NE]), ALU.is_ge))
            link(v.reduce_sum(expert, TB[:, :, :], AX.X))
            link(v.tensor_tensor(TB[:, :, :], TB[:, :, :], T1[:, :].unsqueeze(1).to_broadcast([P, TILES, NE]), ALU.mult))
            link(v.reduce_sum(first, TB[:, :, :], AX.X))
            link(v.tensor_tensor(OE[:, :, :], const("iota_t").rearrange("p (t e) -> p t e", e=NE),
                                 expert.unsqueeze(2).to_broadcast([P, TILES, NE]), ALU.is_equal))
            link(v.tensor_tensor(OE[:, :, :], OE[:, :, :], rows_of.unsqueeze(1).to_broadcast([P, TILES, NE]), ALU.mult))
            link(v.reduce_sum(n_rows, OE[:, :, :], AX.X))
            link(v.tensor_tensor(rank, const("tiles"), first, ALU.subtract))
            link(v.tensor_scalar(rank, rank, float(TROWS), const("lane"), ALU.mult, ALU.add))
            for i in range(TH):
                link(v.tensor_scalar(t, rank, float(i * P), None, ALU.add))
                link(v.tensor_tensor(RF[:, :, 4 + i], t, n_rows, ALU.is_lt))
                link(v.tensor_scalar(tile, n_rows, 1.0, None, ALU.subtract))
                link(v.tensor_tensor(t, t, tile, ALU.min))
                link(v.scalar_tensor_tensor(RF[:, :, i], expert, float(TOK), t, ALU.mult, ALU.add))
                link(v.tensor_scalar(RF[:, :, 6 + i], const("tiles"), float(TROWS), const("dump")[:, i:i + 1], ALU.mult, ALU.add))
            link(v.tensor_scalar(RF[:, :, 2], expert, float(P), const("lane"), ALU.mult, ALU.add))
            link(v.tensor_copy(RF[:, :, 3], expert))
            link(v.tensor_copy(RI[:, :, :], RF[:, :, 0:4]))

            def prepare(tile, r):
                v.tensor_copy(IX[:, r:r + 1, :], RI[:, ds(tile, 1), :]).then_inc(ix_ready[r], 1)
                v.tensor_copy(FX[:, r:r + 1, :], RF[:, ds(tile, 1), :]).then_inc(ix_ready[r], 1)

            for r in range(RING - 1):
                prepare(r, r)
            links = Chain(dve, tile_links, 7)

            def do(lap, r, tile):
                links.n = links.per
                links.at(tile)
                if follows(tile, RING - 1):
                    prepare(tile + RING - 1, (r + RING - 1) % RING)
                dve.wait_ge(gathered[r], 64 * (lap + 1))
                if not isinstance(tile, int) or tile > 0:
                    dve.wait_ge(h_full, HC // 2 * tile)
                dve.wait_ge(xt_full, tile + 1)
                v.tensor_copy(XT[:, :, :], PT[:, :, :]).then_inc(xt_copied, 1)
                g = [G[:, r, i, :] for i in range(4)]
                w0, w1, e0, token = (XG[:, r, :, D + i] for i in range(4))
                dve.wait_ge(ix_ready[r], 2 * (lap + 1))
                links.did(v.tensor_scalar(g[0], e0, FX[:, r, 3:4], None, ALU.is_equal))
                links.did(v.tensor_tensor(g[1], w0, w1, ALU.subtract))
                links.wait()
                links.did(v.tensor_tensor(g[1], g[1], g[0], ALU.mult))
                links.did(v.tensor_scalar(g[2], g[0], -float(TOK), float(TOK), ALU.mult, ALU.add))
                links.wait()
                links.did(v.tensor_tensor(g[3], g[1], w1, ALU.add))
                links.did(v.tensor_tensor(g[2], g[2], token, ALU.add))
                links.wait()
                links.did(v.tensor_tensor(g[2], g[2], FX[:, r, 6:8], ALU.subtract))
                links.wait()
                v.tensor_tensor(g[2], g[2], FX[:, r, 4:6], ALU.mult).then_inc(y_read, 1)
                dve.wait_ge(y_read, 2 * tile + 1)
                at_least(dve, y_sent[r], 16 * TH * lap)
                v.tensor_tensor(DI[:, r, :], g[2], FX[:, r, 6:8], ALU.add).then_inc(y_ready, 1)
                dve.wait_ge(y_full, tile + 1)
                v.tensor_tensor(Y[:, r, :, :], PY[:, r, :, :], BG[:, r:r + 1, :].to_broadcast([P, TH, D]), ALU.add
                                ).then_inc(y_read, 1)
                dve.wait_ge(y_read, 2 * tile + 2)
                for i in range(TH):
                    v.tensor_scalar_mul(Y[:, r, i, :], Y[:, r, i, :], g[3][:, i:i + 1]).then_inc(y_ready, 1)
            over_tiles(dve, do)

        @block.gpsimd
        def _(pool):
            g = nc.gpsimd

            def gather(lap, r, tile):
                pool.wait_ge(ix_ready[r], 2 * (lap + 1))
                if not isinstance(tile, int) or tile >= RING:
                    pool.wait_ge(y_full, tile - RING + 1)
                    pool.wait_ge(y_ready, 3 * (tile - RING + 1))
                pool.sem_inc(alone, 1)
                for i in range(TH):
                    g.indirect_dma_start(out=XG[:, r, i, :], out_offset=None, in_=rows,
                                         in_offset=IND(ap=IX[:, r, i:i + 1], axis=0)).then_inc(gathered[r], 16)
                g.indirect_dma_start(out=WG[:, r, :], out_offset=None, in_=experts,
                                     in_offset=IND(ap=IX[:, r, 2:3], axis=0)).then_inc(gathered[r], 16)
                g.indirect_dma_start(out=BG[:, r, :], out_offset=None, in_=b2,
                                     in_offset=IND(ap=IX[:, r, 3:4], axis=0)).then_inc(gathered[r], 16)

            for r in range(RING - 1):
                gather(0, r, r)

            def do(lap, r, tile):
                if follows(tile, RING - 1):
                    gather(lap + (1 if r > 0 else 0), (r + RING - 1) % RING, tile + RING - 1)
                wait_alone(pool, y_ready, 3 * tile + 3, alone)
                for i in range(TH):
                    g.indirect_dma_start(out=ys, out_offset=IND(ap=DI[:, r, i:i + 1], axis=0),
                                         in_=Y[:, r, i, :], in_offset=None).then_inc(y_sent[r], 16)
            over_tiles(pool, do)
            for r in range(RING):
                pool.wait_ge(y_sent[r], 16 * TH * LAPS)

        @block.scalar
        def _(act):
            def do(lap, r, tile):
                if not isinstance(tile, int) or tile >= RING:
                    act.wait_ge(y_full, tile - RING + 1)
                act.wait_ge(gathered[r], 64 * (lap + 1))
                for c in range(HC):
                    if c % 2 == 0:
                        act.wait_ge(h_full, HC // 2 * tile + c // 2 + 1)
                    nc.scalar.activation(HT[:, r, c, :], PH[:, c // 2, c % 2, :], ACT.Gelu_apprx_tanh,
                                         bias=WG[:, r, W1 + W2 + c:W1 + W2 + c + 1]).then_inc(h_ready, 1)
            over_tiles(act, do)

        @block.tensor
        def _(pe):
            t = nc.tensor

            def turn(lap, r, tile):
                pe.wait_ge(gathered[r], 64 * (lap + 1))
                at_least(pe, xt_copied, tile)
                for k in range(KC):
                    for i in range(TH):
                        last = t.transpose(PT[:, k, i * P:i * P + P], XG[:, r, i, k:D:KC], const("ident"))
                last.then_inc(xt_full, 1)

            turn(0, 0, 0)

            def do(lap, r, tile):
                pe.wait_ge(xt_copied, tile + 1)
                for c in range(HC):
                    if not isinstance(tile, int) or tile > 0:
                        if c % 2 == 0:
                            pe.wait_ge(h_ready, HC * tile - HC + c + 2)
                    for k in range(KC):
                        i = t.matmul(PH[:, c // 2, c % 2, :], WG[:, r, k * HID + c:(k + 1) * HID:HC], XT[:, k, :],
                                     start=(k == 0), stop=(k == KC - 1))
                    if c % 2 == 1:
                        i.then_inc(h_full, 1)
                if follows(tile, 1):
                    turn(lap + (1 if r == RING - 1 else 0), (r + 1) % RING, tile + 1)
                if not isinstance(tile, int) or tile >= RING:
                    pe.wait_ge(y_read, 2 * (tile - RING + 1))
                for i in range(TH):
                    for c in range(HC):
                        if i == 0:
                            pe.wait_ge(h_ready, HC * tile + c + 1)
                        last = t.matmul(PY[:, r, i, :], HT[:, r, c, i * P:i * P + P], WG[:, r, W1 + c * D:W1 + (c + 1) * D],
                                        start=(c == 0), stop=(c == HC - 1))
                last.then_inc(y_full, 1)
            over_tiles(pe, do)


def stage3(nc, make, X, stats, stats_links, ys, out):
    f32 = mybir.dt.float32
    ALU = mybir.AluOpType
    ds = bass.ds
    ctx = ExitStack()
    with ctx:
        sb, pb, sem = make(ctx)
        YC = sb("YC", [P, 2, 2, C, D], f32)
        S = sb("S", [P, 2, C, D], f32)
        T = sb("T", [P, 2, C, D], f32)
        O = sb("O", [P, 2, C, D], f32)
        ST = sb("STF", [P, C, 6], f32)
        MV = sb("MVF", [P, C, 2], f32)
        SM = sb("SMF", [P, 4, C], f32)
        loaded = [sem("y_loaded0"), sem("y_loaded1")]
        summed, normed, added = sem("summed"), sem("normed"), sem("added")
        stored = [sem("stored0"), sem("stored1")]
        links = sem("finish_links")
        block = ctx.enter_context(nc.Block())
        yv = ys[0:2 * TOK].rearrange("(k b p c) e -> b p k (c e)", k=2, p=P, c=C)
        ov = out.rearrange("(b p c) e -> b p (c e)", p=P, c=C)

        def over_batches(eng, do):
            for r in range(2):
                do(0, r, r)
            with eng.Fori(1, B // 2) as lap:
                for r in range(2):
                    do(lap, r, 2 * lap + r)

        @block.sync
        def _(sp):
            def do(lap, r, b):
                at_least(sp, summed, b - 1) if isinstance(b, int) else sp.wait_ge(summed, b - 1)
                sp.dma_start(YC[:, r, :, :, :].rearrange("p k c e -> p k (c e)"), yv[ds(b, 1)].rearrange("a p k f -> (a p) k f")
                             ).then_inc(loaded[r], 16)
            over_batches(sp, do)

        @block.gpsimd
        def _(pool):
            def do(lap, r, b):
                pool.wait_ge(loaded[r], 16 * (lap + 1))
                at_least(pool, normed, b - 1)
                nc.gpsimd.tensor_tensor(S[:, r, :, :], YC[:, r, 0, :, :], YC[:, r, 1, :, :], ALU.add).then_inc(summed, 1)
            over_batches(pool, do)

        @block.vector
        def _(dve):
            v = nc.vector
            chain = Chain(dve, links, stats_links)

            def do(lap, r, b):
                chain.n = 0
                chain.at(b)
                dve.wait_ge(summed, b + 1)
                var, y, t, rs = (SM[:, i, :] for i in range(4))
                stats(v, chain, lambda c: S[:, r, c, :], ST, MV, var, y, t, rs)
                at_least(dve, added, b - 1)
                for c in range(C):
                    i = v.tensor_scalar(T[:, r, c, :], S[:, r, c, :], MV[:, c, 0:1], rs[:, c:c + 1], ALU.subtract, ALU.mult)
                i.then_inc(normed, 1)
                dve.wait_ge(normed, b + 1)
                at_least(dve, stored[r], 16 * lap)
                v.tensor_tensor(O[:, r, :, :], T[:, r, :, :], X[:, ds(C * b, C), :], ALU.add).then_inc(added, 1)
            over_batches(dve, do)

        @block.scalar
        def _(act):
            def do(lap, r, b):
                act.wait_ge(added, b + 1)
                act.dma_start(ov[ds(b, 1)].rearrange("a p f -> (a p) f"), O[:, r, :, :].rearrange("p c e -> p (c e)")
                              ).then_inc(stored[r], 16)
            over_batches(act, do)
            for r in range(2):
                act.wait_ge(stored[r], 16 * B // 2)


def constants():
    a = np.zeros((P, NCONST), np.float32)

    def put(name, value):
        at, w = CONST[name]
        a[:, at:at + w] = np.broadcast_to(value, (P, w))

    p, q = np.arange(P)[:, None], np.arange(P)[None, :]
    put("ident", p == q)
    put("lower", p < q)
    put("ones", 1)
    put("neg_half", np.where(p // CDH == q // CDH, -0.5, 0))
    put("indicator", np.concatenate([np.where(8 * m + p // DH == np.arange(H), -0.5, 0) for m in range(KC)], 1))
    put("iota8", np.tile(np.arange(NE), C))
    put("region", np.tile(np.arange(NE) * TOK, C))
    put("token", (np.arange(B)[None, :, None] * N + p[:, :, None] * C + np.arange(C)).reshape(P, -1))
    put("steps", np.tile(np.arange(THR) * TROWS, NE))
    put("tiles", np.arange(TILES))
    put("iota_t", np.tile(np.arange(NE), TILES))
    put("lane", p)
    put("dump", 2 * TOK + np.arange(TH) * P + p)
    return a


def kernel(**inputs):
    import concourse.bacc as bacc
    from concourse.bass_utils import run_bass_kernel_spmd
    g = {k.split("_", 2)[2]: np.asarray(v) for k, v in inputs.items()}

    def cols(v, n):
        return v.reshape(n, P).T

    def square(w):
        return w.reshape(KC, P, D).transpose(1, 0, 2).reshape(P, KC * D)

    vecs = np.zeros((P, NVEC), np.float32)
    for name, value in [("gamma1", g["gamma1"]), ("gamma2", g["gamma2"]), ("tau_t", g["tau_t"].reshape(-1)),
                        ("tau_c", cols(np.repeat(g["tau_c"].reshape(-1), CDH), 2)),
                        ("ln1_w", cols(g["ln1_w"], KC)), ("ln1_b", cols(g["ln1_b"], KC)),
                        ("ln2_w", cols(g["ln2_w"], KC)), ("ln2_b", cols(g["ln2_b"], KC)),
                        ("router", g["w_router"].reshape(KC, P, NE).transpose(1, 0, 2).reshape(P, -1))]:
        at, w = VEC[name]
        vecs[:, at:at + w] = np.broadcast_to(value, (P, w))
    arrays = {
        "x": g["x"].reshape(TOK, D),
        "weights": np.concatenate([square(g[n]) for n in ("Wqk_t", "Wv_t", "Wo_t", "Wqk_c")]
                                  + [square(np.ascontiguousarray(g["Wv_c"].T)), square(g["Wo_c"])], 1),
        "vecs": vecs,
        "consts": constants(),
        "experts": np.concatenate([g["w1"].reshape(NE * P, -1), g["w2"].reshape(NE * P, -1),
                                   g["b1"].reshape(NE * P, -1)], 1),
        "b2": g["b2"],
    }
    arrays = {k: np.ascontiguousarray(v) for k, v in arrays.items()}
    nc = bacc.Bacc("TRN2", target_bir_lowering=False, num_devices=1)
    aps = [nc.dram_tensor(k, v.shape, mybir.dt.from_np(v.dtype), kind="ExternalInput").ap() for k, v in arrays.items()]
    out = nc.dram_tensor("out", (TOK, D), mybir.dt.float32, kind="ExternalOutput").ap()
    program(nc, *aps, out)
    result = run_bass_kernel_spmd(nc, [arrays], core_ids=[0])
    return result.results[0]["out"].reshape(B, N, D)
```

```python
import math
from contextlib import ExitStack

import numpy as np

import concourse.bass as bass
from concourse import mybir

B, N, D = 8, 512, 256
H, DH = 16, 16
CH, CDH = 8, 32
NE, HID = 8, 1024
EPS = 1e-5
P = 128
C = N // P
KC = D // P
TOK = B * N
TROWS = 256
TH = TROWS // P
TILES = (2 * TOK + NE * (TROWS - 1)) // TROWS
THR = TOK // TROWS
ROW = D + 4
W1ROW = (D + 1) * HID // P
W2ROW = HID * D // P + D
DVE2 = 3
GROUPS = H // 4
SETS = 2 * GROUPS
UNITS = 4 * SETS
KA = 102
PRE_USES, POST_USES = 7, 22
BANK = POST_USES // 2
LOADS = 16 * 14

CONST = {}
_at = 0
for _name, _width in [("ident", P), ("lower", P), ("ones", P), ("neg_half", P), ("indicator", 2 * H),
                      ("iota8", 4 * NE), ("region", 4 * NE), ("token", B * C), ("steps", NE * THR),
                      ("tiles", TILES), ("iota_t", TILES * NE), ("lane", 1), ("dump", TH)]:
    CONST[_name] = (_at, _width)
    _at += _width
NCONST = _at
VEC = {}
_at = 0
for _name, _width in [("gamma1", D), ("gamma2", D), ("tau_t", H), ("tau_c", 2), ("ln1_w", KC), ("ln1_b", KC),
                      ("ln2_w", KC), ("ln2_b", KC), ("router", KC * NE)]:
    VEC[_name] = (_at, _width)
    _at += _width
NVEC = _at

PRE_AT = {0: ["norm1"], 3: ["xt"], 4: ["qk0"], 5: ["qk1"], 7: ["sq"], 14: ["v0"], 15: ["v1"]}
POST_AT = {3: ["residual"], 4: ["untok"], 5: ["ontok"], 6: ["proj"], 8: ["x2t"], 9: ["qkc", "clear"], 10: ["gram"],
           11: ["dist"], 12: ["mix"], 13: ["weff", "chan"]}
LATE_AT = {1: ["z3t"], 2: ["logits"], 3: ["prefix"]}
STEPS = [name for at in (PRE_AT, POST_AT, LATE_AT) for names in at.values() for name in names]


def schedule(eng, own):
    do = dict.fromkeys(STEPS + ["att", "att_end", "drain"], lambda *_: None)
    do.update(own)

    def body(b, par, att=True, pre=False, post=False, late=False, first=False):
        for pos in range(2 * SETS):
            if att:
                do["att"](b, par, pos, first)
            for flag, at, of, of_par in ((pre, PRE_AT, b + 1, 1 - par), (late, LATE_AT, b - 2, par),
                                         (post, POST_AT, b - 1, 1 - par)):
                for name in at.get(pos, []):
                    if flag:
                        do[name](of, of_par)
            if att:
                do["att_end"](b, par, pos, first)

    body(-1, 1, att=False, pre=True)
    body(0, 0, pre=True, first=True)
    body(1, 1, pre=True, post=True)
    body(2, 0, pre=True, post=True, late=True)
    with eng.Fori(0, B // 2 - 2) as lap:
        b = 2 * lap + 3
        body(b, 1, pre=True, post=True, late=True)
        body(b + 1, 0, pre=True, post=True, late=True)
    body(B - 1, 1, post=True, late=True)
    do["drain"](B - 1, 1)
    body(B, 0, att=False, post=True, late=True)
    body(B + 1, 1, att=False, late=True)


def at_least(eng, sem, value):
    if not isinstance(value, int) or value > 0:
        eng.wait_ge(sem, value)


def wait_alone(eng, sem, value, spare):
    eng.wait_ge(sem, value)
    eng.sem_inc(spare, 1)


class Chain:
    def __init__(self, eng, sem, per):
        self.eng, self.sem, self.per, self.n, self.b = eng, sem, per, 0, 0

    def did(self, ins):
        ins.then_inc(self.sem, 1)
        self.n += 1

    def at(self, b):
        assert self.n in (0, self.per), (self.n, self.per)
        self.b, self.n = b, 0

    def wait(self, spare=None):
        self.eng.wait_ge(self.sem, self.b * self.per + self.n)
        if spare is not None:
            self.eng.sem_inc(spare, 1)


def program(nc, x, weights, vecs, consts, experts1, experts2, out):
    f32, bf16, i32, u32 = mybir.dt.float32, mybir.dt.bfloat16, mybir.dt.int32, mybir.dt.uint32
    ACT, ALU, AX = mybir.ActivationFunctionType, mybir.AluOpType, mybir.AxisListType
    ds = bass.ds
    IND = bass.IndirectOffsetOnAxis

    qs = nc.dram_tensor("q_parts", (KC, 3, P, N), bf16, kind="Internal").ap()
    ns = nc.dram_tensor("norm_parts", (H, 3, N), bf16, kind="Internal").ap()
    rows = nc.dram_tensor("expert_rows", (NE * TOK, ROW), f32, kind="Internal").ap()
    ys = nc.dram_tensor("choice_rows", (2 * TOK + TILES * TROWS, D), f32, kind="Internal").ap()

    outer = ExitStack()
    with outer:
        def make(ctx):
            return (lambda n, s, d: ctx.enter_context(nc.sbuf_tensor(n, s, d)),
                    lambda n, s, d: ctx.enter_context(nc.psum_tensor(n, s, d)),
                    lambda n: ctx.enter_context(nc.semaphore(n)))

        sb, _, sem = make(outer)
        alone = sem("alone")
        X = sb("X", [P, B * C, D], f32)
        KT = sb("KT", [P, NCONST], f32)
        COUNT = sb("COUNT", [P, C + 1, NE], f32)

        def const(name):
            a, w = CONST[name]
            return KT[:, a:a + w]

        def rsqrt(v, chain, out_ap, var, y, t):
            chain.did(v.tensor_scalar(y.bitcast(i32), var.bitcast(i32), -0.5, 1597463007.0, ALU.mult, ALU.add))
            chain.wait()
            for n in range(3):
                chain.did(v.tensor_tensor(t, y, y, ALU.mult))
                chain.wait()
                chain.did(v.scalar_tensor_tensor(t, t, -0.5, var, ALU.mult, ALU.mult))
                chain.wait()
                chain.did(v.scalar_tensor_tensor(out_ap if n == 2 else y, t, 1.5, y, ALU.add, ALU.mult))
                chain.wait()

        def stats(v, chain, src, st, mv, var, y, t, r):
            v.sem_inc(alone, 1)
            for c in range(C):
                chain.did(v.bn_stats(st[:, c, :], src(c)))
            chain.wait(alone)
            for c in range(C):
                chain.did(v.bn_aggr(mv[:, c, :], st[:, c, :]))
            chain.wait()
            chain.did(v.tensor_scalar_add(var, mv[:, :, 1], EPS))
            chain.wait()
            rsqrt(v, chain, r, var, y, t)
        STATS = 19

        mix = ExitStack()
        with mix:
            sb, pb, sem = make(mix)
            W = sb("W", [P, 6, KC, D], f32)
            wqk, wv, wo, wqkc, wvt, woc = range(6)
            VV = sb("VV", [P, NVEC], f32)
            MU = sb("MU", [P, B * C], f32)
            RS = sb("RS", [P, B * C], f32)
            ST = sb("ST", [P, C, 6], f32)
            MV = sb("MV", [P, C, 2], f32)
            SM = sb("SM", [P, 4, 2, C], f32)
            Z1 = sb("Z1", [P, C, D], f32)
            XT = sb("XT", [P, KC, N], f32)
            QF = sb("QF", [P, KC, N], f32)
            QR = sb("QR", [P, KC, N], f32)
            QP = sb("QP", [P, KC, 3, N], bf16)
            SQ = sb("SQ", [P, KC, N], f32)
            NF = sb("NF", [H, 2, N], f32)
            NP = sb("NP", [H, 3, N], bf16)
            OPA = sb("OPA", [KA, 2, 8 * N], bf16)
            OPB = sb("OPB", [KA, 2, 8 * N], bf16)
            VA = sb("VA", [P, 2, C, H, 32], f32)
            E = sb("E", [P, 2, 4, 2, N], f32)
            OT = sb("OT", [P, GROUPS, N], f32)
            ON = sb("ON", [P, C, D], f32)
            REC = sb("REC", [P, C, H], f32)
            OTN = sb("OTN", [P, KC, N], f32)
            ST2 = sb("ST2", [P, C, 6], f32)
            MV2 = sb("MV2", [P, C, 2], f32)
            SM2 = sb("SM2", [P, 6, C], f32)
            X1 = sb("X1", [P, C, D], f32)
            Z2, X2T, QC, Z3T = ON, OTN, ON, OTN
            GS = sb("GS", [P, 2, P], f32)
            DG = sb("DG", [P, 2, P], f32)
            L = sb("L", [P, 2, CDH], f32)
            LX = sb("LX", [P, 2, CDH], f32)
            LS = sb("LS", [P, 4, 2], f32)
            AT = sb("AT", [P, 2, P], f32)
            MB = sb("MB", [P, KC, D], f32)
            WE = sb("WE", [P, KC, D], f32)
            PAY = sb("PAY", [P, C, ROW], f32)
            ZERO = sb("ZERO", [P, C * ROW], f32)
            LG = sb("LG", [P, C, NE], f32)
            PR = sb("PR", [P, C, NE], f32)
            R4 = sb("R4", [P, 3, C], f32)
            TOP = sb("TOP", [P, C, NE], f32)
            TI = sb("TI", [P, C, NE], u32)
            TF = sb("TF", [P, C, NE], f32)
            OH = sb("OH", [P, 3, C, NE], f32)
            PX = sb("PX", [P, 2, C, NE], f32)
            RK = sb("RK", [P, 3, C, NE], f32)
            SF = sb("SF", [P, 2, C], f32)
            SLOT = sb("SLOT", [P, 2, C], i32)

            PS = pb("PS", [P, 2, 2, N], f32)
            PO = pb("PO", [P, N], f32)
            PA = pb("PA", [P, N], f32)
            PB = pb("PB", [P, 2, N], f32)

            def vec(name):
                a, w = VEC[name]
                return VV[:, a:a + w]

            x_loaded, w_loaded, x_rest = sem("x_loaded"), sem("w_loaded"), sem("x_rest")
            setup_done, setup_pool = sem("setup_done"), sem("setup_pool")
            pre_links, post_links = sem("pre_links"), sem("post_links")
            z1_ready, rs_ready = sem("z1_ready"), sem("rs_ready")
            qf_ready, sq_ready, qp_ready, np_ready = sem("qf_ready"), sem("sq_ready"), sem("qp_ready"), sem("np_ready")
            pre_full, pre_free = sem("pre_full"), sem("pre_free")
            post_full = sem("post_full")
            post_free = [sem("post_free0"), sem("post_free1")]
            q_written = sem("q_written")
            op_loaded = [sem("op_loaded0"), sem("op_loaded1")]
            s_full, e_ready, pv_done, po_read = sem("s_full"), sem("e_ready"), sem("pv_done"), sem("po_read")
            on_ready, otn_ready, z2_ready, x2t_ready = sem("on_ready"), sem("otn_ready"), sem("z2_ready"), sem("x2t_ready")
            qc_ready, dg_ready, l_ready, lx_ready, at_ready = (sem("qc_ready"), sem("dg_ready"), sem("l_ready"),
                                                              sem("lx_ready"), sem("at_ready"))
            mb_ready, we_ready, z3_ready, z3t_ready = sem("mb_ready"), sem("we_ready"), sem("z3_ready"), sem("z3t_ready")
            lg_ready, pr_ready, oh_ready, slot_ready = sem("lg_ready"), sem("pr_ready"), sem("oh_ready"), sem("slot_ready")
            rows_clear, x1_ready, x1_links = sem("rows_clear"), sem("x1_ready"), sem("x1_links")
            sent, rows_free = sem("sent"), sem("rows_free")

            def emptied(eng, b, j):
                eng.wait_ge(post_free[j % 2], BANK * b + j // 2 + 2)

            block = mix.enter_context(nc.Block())

            @block.sync
            def _(sp):
                xv = x.rearrange("(b p c) e -> b p c e", p=P, c=C)
                sp.dma_start(X[:, 0:C, :], xv[0]).then_inc(x_loaded, 16)
                sp.dma_start(VV[:, :], vecs).then_inc(w_loaded, 16)
                sp.dma_start(KT[:, :], consts).then_inc(w_loaded, 16)
                sp.dma_start(W[:, :, :, :], weights.rearrange("p (w k n) -> p w k n", w=6, k=KC)).then_inc(w_loaded, 16)
                for b in range(1, B):
                    sp.dma_start(X[:, C * b:C * b + C, :], xv[b]).then_inc(x_rest, 16)
                sp.wait_ge(setup_pool, 4)
                sp.wait_ge(setup_done, 1)

                def store(b, m):
                    wait_alone(sp, qp_ready, KC * b + m + 1, alone)
                    at_least(sp, op_loaded[m], LOADS * b)
                    sp.dma_start(qs[m].rearrange("x p n -> p x n"), QP[:, m, :, :]).then_inc(q_written, 16)

                def store_norms(b):
                    at_least(sp, np_ready, b + 1)
                    sp.dma_start(ns, NP[:, :, :]).then_inc(q_written, 16)

                def load(b, m):
                    wait_alone(sp, q_written, 48 * (b + 1), alone)
                    at_least(sp, s_full, UNITS * b - UNITS // 2 * (1 - m))
                    v = qs[m]
                    src = [v[k].rearrange("(h d) n -> d h n", d=DH) for k in range(3)]
                    a, o = OPA[:, m, :].rearrange("p (h n) -> p h n", h=8), OPB[:, m, :].rearrange("p (h n) -> p h n", h=8)
                    order_a, order_b = (0, 1, 2, 0, 1, 0), (0, 0, 0, 1, 1, 2)
                    for k in range(6):
                        sp.dma_start(a[DH * k:DH * k + DH], src[order_a[k]]).then_inc(op_loaded[m], 16)
                        sp.dma_start(o[DH * k:DH * k + DH], src[order_b[k]]).then_inc(op_loaded[m], 16)
                    nv = ns[8 * m:8 * m + 8].rearrange("h x n -> x h n")
                    sp.dma_start(a[6 * DH:6 * DH + 3], nv).then_inc(op_loaded[m], 16)
                    sp.dma_start(o[6 * DH + 3:6 * DH + 6], nv).then_inc(op_loaded[m], 16)

                def att(b, par, pos, first):
                    if pos == 0:
                        load(b, 1)

                do = {"att": att}

                def clear(b, par):
                    at_least(sp, rows_free, b + 1)
                    sp.dma_start(rows.rearrange("(e b p r) f -> b p e (r f)", e=NE, b=B, p=P)[ds(b, 1)]
                                 .rearrange("a p e f -> (a p) e f"),
                                 ZERO[:, :].unsqueeze(1).to_broadcast([P, NE, C * ROW])).then_inc(rows_clear, 16)
                do["clear"] = clear

                def sq(b, par):
                    store(b, 0)
                    store(b, 1)
                    store_norms(b)
                    load(b, 0)
                do["sq"] = sq
                schedule(sp, do)

            @block.gpsimd
            def _(pool):
                g = nc.gpsimd
                pool.sem_inc(rows_free, 1)
                g.memset(VA[:, :, :, :, :], 1.0).then_inc(setup_pool, 1)
                g.memset(AT[:, :, :], 0.0).then_inc(setup_pool, 1)
                g.memset(ZERO[:, :], 0.0).then_inc(setup_pool, 1)
                g.memset(COUNT[:, :, :], 0.0).then_inc(setup_pool, 1)

                do = {}

                def qk(m):
                    def step(b, par):
                        pool.wait_ge(qf_ready, KC * b + m + 1)
                        g.tensor_tensor(SQ[:, m, :], QF[:, m, :], QF[:, m, :], ALU.mult).then_inc(sq_ready, 1)
                    return step
                do["qk0"], do["qk1"] = qk(0), qk(1)

                def residual(b, par):
                    at_least(pool, z3_ready, b)
                    mus, rss = SM2[:, 4, :], SM2[:, 5, :]
                    pool.wait_ge(rs_ready, b + 1)
                    g.tensor_copy(mus, MU[:, ds(C * b, C)]).then_inc(x1_links, 1)
                    g.tensor_copy(rss, RS[:, ds(C * b, C)]).then_inc(x1_links, 1)
                    pool.wait_ge(x1_links, 2 * b + 2)
                    g.tensor_tensor(X1[:, :, :], X[:, ds(C * b, C), :], mus.unsqueeze(2).to_broadcast([P, C, D]), ALU.subtract
                                    ).then_inc(x1_ready, 1)
                    pool.wait_ge(x1_ready, 2 * b + 1)
                    g.tensor_tensor(X1[:, :, :], X1[:, :, :], rss.unsqueeze(2).to_broadcast([P, C, D]), ALU.mult
                                    ).then_inc(x1_ready, 1)
                do["residual"] = residual

                def prefix(b, par):
                    pool.wait_ge(rows_clear, 16 * (b + 1))
                    wait_alone(pool, slot_ready, b + 1, alone)
                    for c in range(C):
                        for k in range(2):
                            g.indirect_dma_start(out=rows, out_offset=IND(ap=SLOT[:, k, c:c + 1], axis=0),
                                                 in_=PAY[:, c, :], in_offset=None).then_inc(sent, 16)
                    pool.wait_ge(sent, 16 * 2 * C * (b + 1))
                    pool.sem_inc(rows_free, 1)
                do["prefix"] = prefix
                schedule(pool, do)

            @block.scalar
            def _(act):
                a = nc.scalar
                act.wait_ge(setup_done, 1)

                do = {}

                def take(b, j):
                    act.wait_ge(pre_full, PRE_USES * b + j + 1)

                def takep(b, j):
                    act.wait_ge(post_full, POST_USES * b + j + 1)
                    return PB[:, j % 2, :]

                def affine(dst, src, w, bias):
                    return a.activation(dst, src, ACT.Identity, scale=w, bias=bias)

                def xt(b, par):
                    for k in range(KC):
                        take(b, k)
                        affine(XT[:, k, :], PA[:, :], vec("ln1_w")[:, k:k + 1], vec("ln1_b")[:, k:k + 1]).then_inc(pre_free, 1)
                do["xt"] = xt

                def qk(m):
                    def step(b, par):
                        take(b, 2 + m)
                        at_least(act, sq_ready, KC * b)
                        at_least(act, qp_ready, KC * b)
                        at_least(act, q_written, 48 * b)
                        a.copy(QF[:, m, :], PA[:, :]).then_inc(qf_ready, 1)
                        a.copy(QP[:, m, 0, :], PA[:, :]).then_inc(pre_free, 1)
                    return step
                do["qk0"], do["qk1"] = qk(0), qk(1)

                def vv(i):
                    def step(b, par):
                        take(b, 5 + i)
                        at_least(act, pv_done, SETS * (b - 1))
                        a.copy(VA[:, par, 2 * i:2 * i + 2, :, 0:DH],
                               PA[:, :].rearrange("p (c h d) -> p c h d", c=2, h=H)).then_inc(pre_free, 1)
                    return step
                do["v0"], do["v1"] = vv(0), vv(1)

                def ontok(b, par):
                    for m in range(KC):
                        a.copy(OTN[:, m, :], takep(b, 4 + m)).then_inc(post_free[m], 1)
                do["ontok"] = ontok

                def x2t(b, par):
                    for k in range(KC):
                        affine(X2T[:, k, :], takep(b, 8 + k), vec("ln2_w")[:, k:k + 1], vec("ln2_b")[:, k:k + 1]
                               ).then_inc(post_free[k], 1)
                do["x2t"] = x2t

                def qkc(b, par):
                    for i in range(2):
                        a.copy(QC[:, 2 * i:2 * i + 2, :], takep(b, 10 + i).rearrange("p (c e) -> p c e", c=2)
                               ).then_inc(post_free[i], 1)
                do["qkc"] = qkc

                def mixc(b, par):
                    a.copy(MB[:, :, :], takep(b, 14).rearrange("p (k e) -> p k e", k=2)).then_inc(post_free[0], 1)
                do["mix"] = mixc

                def weff(b, par):
                    a.copy(WE[:, :, :], takep(b, 15).rearrange("p (k e) -> p k e", k=2)).then_inc(post_free[1], 1)
                do["weff"] = weff

                def z3t(b, par):
                    for k in range(KC):
                        a.copy(Z3T[:, k, :], takep(b, 18 + k)).then_inc(post_free[k], 1)
                do["z3t"] = z3t

                def att(b, par, pos, first):
                    s = pos // 2
                    if pos % 2 == 0:
                        at_least(act, pv_done, SETS * b + s - 1)
                    for i in range(2):
                        h = 2 * (pos % 2) + i
                        u = 4 * s + h
                        act.wait_ge(s_full, UNITS * b + u + 1)
                        a.activation(E[:, s % 2, h, :, :], PS[:, u % 2, :, :], ACT.Exp,
                                     scale=vec("tau_t")[:, 4 * (s // 2) + h:4 * (s // 2) + h + 1]).then_inc(e_ready, 1)
                do["att"] = att

                def evacuate(b, g):
                    act.wait_ge(pv_done, SETS * b + 2 * g + 2)
                    if g == 0:
                        at_least(act, post_full, POST_USES * (b - 1) + C)
                    a.copy(OT[:, g, :], PO[:, :]).then_inc(po_read, 1)

                def att_end(b, par, pos, first):
                    if pos % 4 == 1:
                        if pos > 1:
                            evacuate(b, pos // 4 - 1)
                        elif not first:
                            evacuate(b - 1, GROUPS - 1)
                do["att_end"] = att_end
                do["drain"] = lambda b, par: evacuate(b, GROUPS - 1)

                def dist(b, par):
                    act.wait_ge(l_ready, b + 1)
                    for k in range(2):
                        a.activation(LX[:, k, :], L[:, k, :], ACT.Exp, bias=LS[:, 1, k:k + 1],
                                     accum_out=LS[:, 2, k:k + 1]).then_inc(lx_ready, 1)
                do["dist"] = dist

                def logits(b, par):
                    act.wait_ge(lg_ready, b + 1)
                    a.activation(PR[:, :, :], LG[:, :, :], ACT.Exp).then_inc(pr_ready, 1)
                do["logits"] = logits
                schedule(act, do)

            @block.vector
            def _(dve):
                v = nc.vector
                v.memset(OPA[6 * DH:KA, :, :], 1.0)
                v.memset(OPB[6 * DH:KA, :, :], 1.0)
                for bank in range(2):
                    dve.sem_inc(post_free[bank], 1)
                dve.wait_ge(w_loaded, 48)
                dve.wait_ge(setup_pool, 4)
                v.tensor_scalar_mul(vec("tau_t"), vec("tau_t"), 2.0 / math.sqrt(DH))
                v.tensor_scalar_mul(vec("tau_c"), vec("tau_c"), 2.0 / math.sqrt(N))
                for k in range(KC):
                    v.tensor_tensor(W[:, wo, k, :], W[:, wo, k, :], vec("gamma1"), ALU.mult)
                    last = v.tensor_tensor(W[:, woc, k, :], W[:, woc, k, :], vec("gamma2"), ALU.mult)
                last.then_inc(setup_done, 1)
                dve.wait_ge(setup_done, 1)

                pre = Chain(dve, pre_links, 2 * C + 3 + 10 + 2 * KC + 3)
                post = Chain(dve, post_links, 3 * STATS + 5 * C + 25)

                def take(b, j):
                    dve.wait_ge(pre_full, PRE_USES * b + j + 1)

                def takep(b, j):
                    dve.wait_ge(post_full, POST_USES * b + j + 1)
                    return PB[:, j % 2, :]

                def xs(b, c, n=1):
                    return X[:, ds(C * b + c, n), :]

                do = {}

                def norm1(b, par):
                    pre.at(b)
                    if isinstance(b, int) and b == 0:
                        dve.wait_ge(x_loaded, 16)
                    if isinstance(b, int) and b == 1:
                        dve.wait_ge(x_rest, 16 * (B - 1))
                    var, y, t, r = (SM[:, i, :, :] for i in range(4))
                    dve.sem_inc(alone, 1)
                    for c in range(C):
                        pre.did(v.bn_stats(ST[:, c, :], X[:, ds(C * b + c, 1), :].rearrange("p a e -> p (a e)")))
                    pre.wait(alone)
                    for c in range(C):
                        pre.did(v.bn_aggr(MV[:, c, :], ST[:, c, :]))
                    pre.wait()
                    pre.did(v.tensor_scalar_add(var[:, 0, :], MV[:, :, 1], EPS))
                    pre.did(v.tensor_scalar(var[:, 1, :], MV[:, :, 1], 1.0 + EPS, EPS * EPS, ALU.mult, ALU.add))
                    pre.did(v.tensor_copy(MU[:, ds(C * b, C)], MV[:, :, 0]))
                    pre.wait()
                    rsqrt(v, pre, r, var, y, t)
                    for c in range(C):
                        i = v.tensor_scalar(Z1[:, c:c + 1, :], xs(b, c), MV[:, c, 0:1], r[:, 1, c:c + 1],
                                            ALU.subtract, ALU.mult)
                    i.then_inc(z1_ready, 1)
                    v.tensor_copy(RS[:, ds(C * b, C)], r[:, 0, :]).then_inc(rs_ready, 1)
                do["norm1"] = norm1

                def qk(m):
                    def step(b, par):
                        dve.wait_ge(pre_free, PRE_USES * b + 3 + m)
                        pre.did(v.tensor_tensor(QR[:, m, :], QF[:, m, :], QP[:, m, 0, :], ALU.subtract))
                        pre.wait()
                        pre.did(v.tensor_copy(QP[:, m, 1, :], QR[:, m, :]))
                        pre.wait()
                        v.tensor_tensor(QP[:, m, 2, :], QR[:, m, :], QP[:, m, 1, :], ALU.subtract).then_inc(qp_ready, 1)
                    return step
                do["qk0"], do["qk1"] = qk(0), qk(1)

                def sq(b, par):
                    take(b, 4)
                    v.tensor_copy(NF[:, 0, :], PA[0:H, :]).then_inc(pre_free, 1)
                    dve.wait_ge(pre_free, PRE_USES * b + 5)
                    pre.did(v.tensor_copy(NP[:, 0, :], NF[:, 0, :]))
                    pre.wait()
                    pre.did(v.tensor_tensor(NF[:, 1, :], NF[:, 0, :], NP[:, 0, :], ALU.subtract))
                    pre.wait()
                    pre.did(v.tensor_copy(NP[:, 1, :], NF[:, 1, :]))
                    pre.wait()
                    v.tensor_tensor(NP[:, 2, :], NF[:, 1, :], NP[:, 1, :], ALU.subtract).then_inc(np_ready, 1)
                do["sq"] = sq

                def untok(b, par):
                    post.at(b)
                    for c in range(C):
                        ps = takep(b, c).rearrange("p (h e) -> p h e", e=32)
                        post.did(v.reciprocal(REC[:, c, :], ps[:, :, DH]))
                        post.wait()
                        v.tensor_tensor(ON[:, c, :].rearrange("p (h e) -> p h e", e=DH), ps[:, :, 0:DH],
                                        REC[:, c, :].unsqueeze(2).to_broadcast([P, H, DH]), ALU.mult).then_inc(post_free[c % 2], 1)
                do["untok"] = untok

                def stats2(b, src):
                    var, y, t, r = (SM2[:, i, :] for i in range(4))
                    stats(v, post, src, ST2, MV2, var, y, t, r)
                    return MV2, r

                def proj(b, par):
                    dve.wait_ge(x1_ready, 2 * (b + 1))
                    dve.sem_inc(alone, 1)
                    for i in range(2):
                        v.tensor_tensor(X1[:, 2 * i:2 * i + 2, :], takep(b, 6 + i).rearrange("p (c e) -> p c e", c=2),
                                        X1[:, 2 * i:2 * i + 2, :], ALU.add).then_inc(post_free[i], 1)
                    emptied(dve, b, 6)
                    emptied(dve, b, 7)
                    mv, r = stats2(b, lambda c: X1[:, c, :])
                    for c in range(C):
                        i = v.tensor_scalar(Z2[:, c, :], X1[:, c, :], mv[:, c, 0:1], r[:, c:c + 1], ALU.subtract, ALU.mult)
                    i.then_inc(z2_ready, 1)
                do["proj"] = proj

                def gram(b, par):
                    v.tensor_copy(GS[:, :, :], takep(b, 12)[:, 0:2 * P].rearrange("p (k e) -> p k e", k=2)).then_inc(post_free[0], 1)
                    emptied(dve, b, 12)
                    v.tensor_tensor(DG[:, :, :], GS[:, :, :], const("ident").unsqueeze(1).to_broadcast([P, 2, P]),
                                    ALU.mult).then_inc(dg_ready, 1)
                do["gram"] = gram

                def dist(b, par):
                    ps = takep(b, 13)[:, 0:2 * P].rearrange("p (k e) -> p k e", k=2)
                    for q in range(4):
                        r = slice(CDH * q, CDH * q + CDH)
                        i = v.tensor_tensor(L[r, :, :], ps[r, :, r], GS[r, :, r], ALU.add)
                        if q < 3:
                            post.did(i)
                    i.then_inc(post_free[1], 1)
                    emptied(dve, b, 13)
                    post.wait()
                    for k in range(2):
                        post.did(v.tensor_scalar_mul(L[:, k, :], L[:, k, :], vec("tau_c")[:, k:k + 1]))
                    post.wait()
                    post.did(v.reduce_max(LS[:, 0, :], L[:, :, :], AX.X))
                    post.wait()
                    v.tensor_scalar_mul(LS[:, 1, :], LS[:, 0, :], -1.0).then_inc(l_ready, 1)
                do["dist"] = dist

                def mixc(b, par):
                    dve.wait_ge(lx_ready, 2 * b + 2)
                    post.did(v.reciprocal(LS[:, 3, :], LS[:, 2, :]))
                    post.wait()
                    for k in range(2):
                        post.did(v.tensor_scalar_mul(LX[:, k, :], LX[:, k, :], LS[:, 3, k:k + 1]))
                    post.wait()
                    for q in range(4):
                        r = slice(CDH * q, CDH * q + CDH)
                        i = v.tensor_copy(AT[r, :, r], LX[r, :, :])
                    i.then_inc(at_ready, 1)
                do["mix"] = mixc

                def chan(b, par):
                    for i in range(2):
                        v.tensor_tensor(X1[:, 2 * i:2 * i + 2, :], takep(b, 16 + i).rearrange("p (c e) -> p c e", c=2),
                                        X1[:, 2 * i:2 * i + 2, :], ALU.add).then_inc(post_free[i], 1)
                    emptied(dve, b, 16)
                    emptied(dve, b, 17)
                    mv, r = stats2(b, lambda c: X1[:, c, :])
                    for c in range(C):
                        post.did(v.tensor_scalar(X1[:, c, :], X1[:, c, :], mv[:, c, 0:1], r[:, c:c + 1], ALU.subtract, ALU.mult))
                    post.wait()
                    post.did(v.tensor_tensor(xs(b, 0, C), xs(b, 0, C), X1[:, :, :], ALU.add))
                    post.wait()
                    mv, r = stats2(b, lambda c: X[:, ds(C * b + c, 1), :].rearrange("p a e -> p (a e)"))
                    dve.wait_ge(rows_free, b + 1)
                    for c in range(C):
                        i = v.tensor_scalar(PAY[:, c:c + 1, 0:D], xs(b, c), mv[:, c, 0:1], r[:, c:c + 1], ALU.subtract, ALU.mult)
                    i.then_inc(z3_ready, 1)
                do["chan"] = chan

                def bc(ap):
                    return ap.unsqueeze(2).to_broadcast([P, C, NE])

                def logits(b, par):
                    post.b = b
                    ps = takep(b, 20)[:, 0:C * NE].rearrange("p (c e) -> p c e", e=NE)
                    post.did(v.reduce_max(R4[:, 0, :], ps, AX.X))
                    post.wait()
                    v.tensor_tensor(LG[:, :, :], ps, bc(R4[:, 0, :]), ALU.subtract).then_inc(post_free[0], 1)
                    emptied(dve, b, 20)
                    v.tensor_copy(PAY[:, :, D + 3], const("token").rearrange("p (b c) -> p b c", c=C)[:, ds(b, 1), :]
                                  .rearrange("p a c -> p (a c)")).then_inc(lg_ready, 1)
                    dve.wait_ge(pr_ready, b + 1)
                    post.did(v.reduce_sum(R4[:, 1, :], PR[:, :, :], AX.X))
                    post.wait()
                    post.did(v.reciprocal(R4[:, 2, :], R4[:, 1, :]))
                    post.wait()
                    post.did(v.tensor_tensor(PR[:, :, :], PR[:, :, :], bc(R4[:, 2, :]), ALU.mult))
                    post.wait(alone)
                    for c in range(C):
                        post.did(v.max(TOP[:, c, :], PR[:, c, :]))
                    post.wait(alone)
                    for c in range(C):
                        post.did(v.max_index(TI[:, c, :], TOP[:, c, :], PR[:, c, :]))
                    post.wait()
                    post.did(v.tensor_copy(TF[:, :, 0:2], TI[:, :, 0:2]))
                    post.wait()
                    iota = const("iota8").rearrange("p (c e) -> p c e", e=NE)
                    for k in range(2):
                        post.did(v.tensor_tensor(OH[:, k, :, :], iota, bc(TF[:, :, k]), ALU.is_equal))
                    post.did(v.tensor_copy(PAY[:, :, D:D + 2], TOP[:, :, 0:2]))
                    post.did(v.tensor_copy(PAY[:, :, D + 2], TF[:, :, 0]))
                    post.wait()
                    v.tensor_tensor(OH[:, 2, :, :], OH[:, 0, :, :], OH[:, 1, :, :], ALU.add).then_inc(oh_ready, 1)
                do["logits"] = logits

                def prefix(b, par):
                    v.tensor_copy(PX[:, :, :, :], takep(b, 21)[:, 0:2 * C * NE].rearrange("p (k c e) -> p k c e", k=2, c=C)
                                  ).then_inc(post_free[1], 1)
                    emptied(dve, b, 21)
                    for c in range(C):
                        post.did(v.tensor_tensor(COUNT[:, c + 1, :], COUNT[:, c, :], PX[:, 1, c, :], ALU.add))
                        post.wait()
                    post.did(v.tensor_tensor(RK[:, 0, :, :], COUNT[:, 0:C, :], PX[:, 0, :, :], ALU.add))
                    post.wait()
                    post.did(v.tensor_copy(COUNT[:, 0, :], COUNT[:, C, :]))
                    post.did(v.tensor_tensor(RK[:, 0, :, :], RK[:, 0, :, :],
                                             const("region").rearrange("p (c e) -> p c e", e=NE), ALU.add))
                    post.wait()
                    for k in range(2):
                        post.did(v.tensor_tensor(RK[:, 1 + k, :, :], RK[:, 0, :, :], OH[:, k, :, :], ALU.mult))
                    post.wait()
                    post.did(v.reduce_sum(SF[:, :, :], RK[:, 1:3, :, :], AX.X))
                    post.wait()
                    v.tensor_copy(SLOT[:, :, :], SF[:, :, :]).then_inc(slot_ready, 1)
                do["prefix"] = prefix
                schedule(dve, do)

            @block.tensor
            def _(pe):
                t = nc.tensor
                ident = const("ident")
                pe.wait_ge(w_loaded, 48)
                pe.wait_ge(setup_done, 1)

                def give(b, j):
                    at_least(pe, pre_free, PRE_USES * b + j)
                    return PA

                def givep(b, j):
                    pe.wait_ge(post_free[j % 2], BANK * b + j // 2 + 1)
                    return PB[:, j % 2, :]

                do = {}

                def pv(b, par, s, jc):
                    g, jp = s // 2, s % 2
                    if jc == 0:
                        pe.wait_ge(e_ready, UNITS * b + 4 * s + 4)
                        if s == 0:
                            pe.wait_ge(pre_free, PRE_USES * (b + 1))
                        if jp == 0:
                            at_least(pe, po_read, GROUPS * b + g)
                    for h in range(4):
                        i = t.matmul(PO[32 * h:32 * h + 32, :], VA[:, par, 2 * jp + jc, 4 * g + h, :],
                                     E[:, s % 2, h, jc, :], start=(jp == 0 and jc == 0), stop=(jp == 1 and jc == 1))
                    if jc == 1:
                        i.then_inc(pv_done, 1)

                def att(b, par, pos, first):
                    s = pos // 2
                    m = s // (SETS // 2)
                    if pos % SETS == 0:
                        pe.wait_ge(op_loaded[m], LOADS * (b + 1))
                    for i in range(2):
                        h = 2 * (pos % 2) + i
                        u = 4 * s + h
                        at_least(pe, e_ready, UNITS * b + u - 1)
                        hh = (4 * (s // 2) + h) % 8
                        for jc in range(2):
                            key = hh * N + (2 * (s % 2) + jc) * P
                            ins = t.matmul(PS[:, u % 2, jc, :], OPA[0:KA, m, key:key + P], OPB[0:KA, m, hh * N:hh * N + N],
                                           start=True, stop=True)
                        ins.then_inc(s_full, 1)
                do["att"] = att

                def att_end(b, par, pos, first):
                    if pos > 1:
                        pv(b, par, pos // 2 - 1, pos % 2)
                    elif not first:
                        pv(b - 1, 1 - par, SETS - 1, pos % 2)
                do["att_end"] = att_end

                def drain(b, par):
                    pv(b, par, SETS - 1, 0)
                    pv(b, par, SETS - 1, 1)
                do["drain"] = drain

                def xt(b, par):
                    pe.wait_ge(z1_ready, b + 1)
                    for k in range(KC):
                        ps = give(b, k)
                        for c in range(C):
                            i = t.transpose(ps[:, c * P:c * P + P], Z1[:, c, k * P:k * P + P], ident)
                        i.then_inc(pre_full, 1)
                do["xt"] = xt

                def qk(m):
                    def step(b, par):
                        ps = give(b, 2 + m)
                        for k in range(KC):
                            i = t.matmul(ps[:, :], W[:, wqk, k, m * P:m * P + P], XT[:, k, :], start=(k == 0), stop=(k == KC - 1))
                        i.then_inc(pre_full, 1)
                    return step
                do["qk0"], do["qk1"] = qk(0), qk(1)

                def sq(b, par):
                    ps = give(b, 4)
                    for m in range(KC):
                        pe.wait_ge(sq_ready, KC * b + m + 1)
                        i = t.matmul(ps[0:H, :], const("indicator")[:, H * m:H * m + H], SQ[:, m, :], start=(m == 0), stop=(m == KC - 1))
                    i.then_inc(pre_full, 1)
                do["sq"] = sq

                def vv(i):
                    def step(b, par):
                        ps = give(b, 5 + i)
                        for c in range(2):
                            for k in range(KC):
                                cc = 2 * i + c
                                ins = t.matmul(ps[:, c * D:c * D + D], XT[:, k, cc * P:cc * P + P], W[:, wv, k, :],
                                               start=(k == 0), stop=(k == KC - 1))
                        ins.then_inc(pre_full, 1)
                    return step
                do["v0"], do["v1"] = vv(0), vv(1)

                def untok(b, par):
                    pe.wait_ge(po_read, GROUPS * (b + 1))
                    for c in range(C):
                        ps = givep(b, c)
                        for g in range(GROUPS):
                            i = t.transpose(ps[:, g * P:g * P + P], OT[:, g, c * P:c * P + P], ident)
                        i.then_inc(post_full, 1)
                do["untok"] = untok

                def ontok(b, par):
                    emptied(pe, b, 2)
                    emptied(pe, b, 3)
                    for m in range(KC):
                        ps = givep(b, 4 + m)
                        for c in range(C):
                            i = t.transpose(ps[:, c * P:c * P + P], ON[:, c, m * P:m * P + P], ident)
                        i.then_inc(post_full, 1)
                do["ontok"] = ontok

                def rows_times(b, j, lhs, rhs):
                    for i in range(2):
                        ps = givep(b, j + i)
                        for c in range(2):
                            for k in range(KC):
                                cc = 2 * i + c
                                ins = t.matmul(ps[:, c * D:c * D + D], lhs[:, k, cc * P:cc * P + P], rhs(k),
                                               start=(k == 0), stop=(k == KC - 1))
                        ins.then_inc(post_full, 1)

                def proj(b, par):
                    emptied(pe, b, 4)
                    emptied(pe, b, 5)
                    rows_times(b, 6, OTN, lambda k: W[:, wo, k, :])
                do["proj"] = proj

                def x2t(b, par):
                    pe.wait_ge(z2_ready, b + 1)
                    for k in range(KC):
                        ps = givep(b, 8 + k)
                        for c in range(C):
                            i = t.transpose(ps[:, c * P:c * P + P], Z2[:, c, k * P:k * P + P], ident)
                        i.then_inc(post_full, 1)
                do["x2t"] = x2t

                def qkc(b, par):
                    emptied(pe, b, 8)
                    emptied(pe, b, 9)
                    rows_times(b, 10, X2T, lambda k: W[:, wqkc, k, :])
                do["qkc"] = qkc

                def gram(b, par):
                    emptied(pe, b, 10)
                    emptied(pe, b, 11)
                    ps = givep(b, 12)
                    for k in range(2):
                        for c in range(C):
                            i = t.matmul(ps[:, k * P:k * P + P], QC[:, c, k * P:k * P + P], QC[:, c, k * P:k * P + P],
                                         start=(c == 0), stop=(c == C - 1))
                    i.then_inc(post_full, 1)
                do["gram"] = gram

                def dist(b, par):
                    pe.wait_ge(dg_ready, b + 1)
                    ps = givep(b, 13)
                    for k in range(2):
                        t.matmul(ps[:, k * P:k * P + P], DG[:, k, :], const("neg_half"), start=True, stop=False)
                        i = t.matmul(ps[:, k * P:k * P + P], const("neg_half"), DG[:, k, :], start=False, stop=True)
                    i.then_inc(post_full, 1)
                do["dist"] = dist

                def mixc(b, par):
                    pe.wait_ge(at_ready, b + 1)
                    ps = givep(b, 14)
                    for k in range(2):
                        i = t.matmul(ps[:, k * D:k * D + D], AT[:, k, :], W[:, woc, k, :], start=True, stop=True)
                    i.then_inc(post_full, 1)
                do["mix"] = mixc

                def weff(b, par):
                    emptied(pe, b, 14)
                    ps = givep(b, 15)
                    for m in range(KC):
                        for k in range(KC):
                            i = t.matmul(ps[:, m * D:m * D + D], W[:, wvt, k, m * P:m * P + P], MB[:, k, :],
                                         start=(k == 0), stop=(k == KC - 1))
                    i.then_inc(post_full, 1)
                do["weff"] = weff

                def chan(b, par):
                    emptied(pe, b, 15)
                    rows_times(b, 16, X2T, lambda k: WE[:, k, :])
                do["chan"] = chan

                def z3t(b, par):
                    pe.wait_ge(z3_ready, b + 1)
                    for k in range(KC):
                        ps = givep(b, 18 + k)
                        for c in range(C):
                            i = t.transpose(ps[:, c * P:c * P + P], PAY[:, c, k * P:k * P + P], ident)
                        i.then_inc(post_full, 1)
                do["z3t"] = z3t

                def logits(b, par):
                    emptied(pe, b, 18)
                    emptied(pe, b, 19)
                    ps = givep(b, 20)
                    for c in range(C):
                        for k in range(KC):
                            i = t.matmul(ps[:, c * NE:c * NE + NE], Z3T[:, k, c * P:c * P + P], vec("router")[:, k * NE:k * NE + NE],
                                         start=(k == 0), stop=(k == KC - 1))
                    i.then_inc(post_full, 1)
                do["logits"] = logits

                def prefix(b, par):
                    pe.wait_ge(oh_ready, b + 1)
                    ps = givep(b, 21)
                    sel = OH[:, 2, :, :].rearrange("p c e -> p (c e)")
                    t.matmul(ps[:, 0:C * NE], const("lower"), sel, start=True, stop=True)
                    t.matmul(ps[:, C * NE:2 * C * NE], const("ones"), sel, start=True, stop=True).then_inc(post_full, 1)
                do["prefix"] = prefix
                schedule(pe, do)

        stage2(nc, make, X, COUNT, const, alone, rows, ys, experts1, experts2)
        stage3(nc, make, X, stats, STATS, ys, out)


def stage2(nc, make, X, COUNT, const, alone, rows, ys, experts1, experts2):
    f32, f32r, i32 = mybir.dt.float32, mybir.dt.float32r, mybir.dt.int32
    ACT, ALU, AX = mybir.ActivationFunctionType, mybir.AluOpType, mybir.AxisListType
    ds = bass.ds
    IND = bass.IndirectOffsetOnAxis
    HC = HID // P
    PAIRS = HC // 2
    PIECE = KC * HID // PAIRS
    LOOP_FROM, LOOP_TO = 3, TILES - 4
    assert (LOOP_TO - LOOP_FROM) % 2 == 0 and KC * HID == HC * D
    ctx = ExitStack()
    with ctx:
        sb, pb, sem = make(ctx)
        TB = sb("TB", [P, TILES, NE], f32)
        OE = sb("OE", [P, TILES, NE], f32)
        T1 = sb("T1", [P, NE], f32)
        CS = sb("CS", [P, 2, 2 * NE], f32)
        TS = sb("TS", [P, NE, THR], f32)
        TF = sb("TFE", [P, 6, TILES], f32)
        RF = sb("RF", [P, TILES, 8], f32)
        RI = sb("RI", [P, TILES, 4], i32)
        RC = sb("RC", [P, TILES + 2, 4], i32)
        IX = sb("IX", [P, 2, 4], i32)
        FX = sb("FX", [P, 8], f32)
        XG = sb("XG", [P, 2, TH, ROW], f32)
        WG1 = sb("WG1", [P, 2, W1ROW], f32)
        WG2 = sb("WG2", [P, 2, W2ROW], f32)
        B1 = sb("B1", [P, 2, HC], f32)
        BW = sb("BW", [P, 2, TH, D], f32)
        W1P = sb("W1P", [P, 2, 2, KC * HID], f32r)
        W2P = sb("W2P", [P, 2, HC * D], f32r)
        XP = sb("XP", [P, 2, KC, TROWS], f32r)
        HF = sb("HF", [P, HC, TROWS], f32)
        HP = sb("HP", [P, 2, 2, HC, TROWS], f32r)
        Y = sb("Y", [P, 2, TH, D], f32)
        G = sb("G", [P, 4, TH], f32)
        GT = sb("GT", [P, TILES, 2, TH], f32)
        GY = sb("GY", [P, 2, 2, TH], f32)
        DI = sb("DI", [P, 2, TH], i32)
        PT = pb("PT", [P, KC, TROWS], f32)
        PH = pb("PH", [P, PAIRS, 2, TROWS], f32)
        PY = pb("PY", [P, 2, TH, D], f32)

        table_links, table_done, tile_links = sem("table_links"), sem("table_done"), sem("tile_links")
        ix_ready = [sem("ix_ready0"), sem("ix_ready1")]
        x_gathered = [sem("x_gathered0"), sem("x_gathered1")]
        w1_gathered = [sem("w1_gathered0"), sem("w1_gathered1")]
        w2_gathered = [sem("w2_gathered0"), sem("w2_gathered1")]
        y_sent = [sem("y_sent0"), sem("y_sent1")]
        w1_hi, w1_lo, w2_hi, w2_lo, w2_lo_pool = sem("w1_hi"), sem("w1_lo"), sem("w2_hi"), sem("w2_lo"), sem("w2_lo_pool")
        b1_ready, gy_ready, b2_ready = sem("b1_ready"), sem("gy_ready"), sem("b2_ready")
        xt_full, x_hi, x_lo, x_noted = sem("xt_full"), sem("x_hi"), sem("x_lo"), sem("x_noted")
        h_full, h_raw, h_hi, h_lo = sem("h_full"), sem("h_raw"), sem("h_hi"), sem("h_lo")
        y_full, y_summed, y_ready = sem("y_full"), sem("y_summed"), sem("y_ready")
        block = ctx.enter_context(nc.Block())

        def over_turns(eng, do):
            for t in range(-2, LOOP_FROM):
                do(t, t % 2, t // 2)
            with eng.Fori(0, (LOOP_TO - LOOP_FROM) // 2) as lap:
                for i in range(2):
                    t = LOOP_FROM + i
                    do(2 * lap + t, t % 2, lap + t // 2)
            for t in range(LOOP_TO, TILES + 2):
                do(t, t % 2, t // 2)

        def is_tile(t):
            return not isinstance(t, int) or 0 <= t < TILES

        def other(r, n, k):
            return (r + k) % 2, n + (r + k) // 2

        def piece(tile, q):
            return tile[:, q * PIECE:(q + 1) * PIECE]

        @block.vector
        def _(dve):
            v = nc.vector
            linked = [0]

            def link(i):
                linked[0] += 1
                i.then_inc(table_links, 1)
                dve.wait_ge(table_links, linked[0])

            rows_of = COUNT[:, 0, :]
            link(v.memset(CS[:, :, :], 0.0))
            link(v.tensor_tensor(TS[:, :, :], rows_of.unsqueeze(2).to_broadcast([P, NE, THR]),
                                 const("steps").rearrange("p (e k) -> p e k", e=NE), ALU.is_gt))
            link(v.reduce_sum(T1[:, :], TS[:, :, :], AX.X))
            link(v.tensor_copy(CS[:, 0, NE:2 * NE], T1[:, :]))
            for n, s in enumerate((1, 2, 4)):
                a, o = CS[:, n % 2, :], CS[:, (n + 1) % 2, :]
                link(v.tensor_tensor(o[:, NE:2 * NE], a[:, NE:2 * NE], a[:, NE - s:2 * NE - s], ALU.add))
            ends = CS[:, 1, NE:2 * NE]
            tile, expert, first, n_rows, rank, t = (TF[:, i, :] for i in range(6))
            link(v.tensor_scalar(t, const("tiles"), 1.0, None, ALU.add))
            link(v.tensor_scalar(tile, t, ends[:, NE - 1:NE], -1.0, ALU.min, ALU.add))
            link(v.tensor_tensor(TB[:, :, :], tile.unsqueeze(2).to_broadcast([P, TILES, NE]),
                                 ends.unsqueeze(1).to_broadcast([P, TILES, NE]), ALU.is_ge))
            link(v.reduce_sum(expert, TB[:, :, :], AX.X))
            link(v.tensor_tensor(TB[:, :, :], TB[:, :, :], T1[:, :].unsqueeze(1).to_broadcast([P, TILES, NE]), ALU.mult))
            link(v.reduce_sum(first, TB[:, :, :], AX.X))
            link(v.tensor_tensor(OE[:, :, :], const("iota_t").rearrange("p (t e) -> p t e", e=NE),
                                 expert.unsqueeze(2).to_broadcast([P, TILES, NE]), ALU.is_equal))
            link(v.tensor_tensor(OE[:, :, :], OE[:, :, :], rows_of.unsqueeze(1).to_broadcast([P, TILES, NE]), ALU.mult))
            link(v.reduce_sum(n_rows, OE[:, :, :], AX.X))
            link(v.tensor_tensor(rank, const("tiles"), first, ALU.subtract))
            link(v.tensor_scalar(rank, rank, float(TROWS), const("lane"), ALU.mult, ALU.add))
            for i in range(TH):
                link(v.tensor_scalar(t, rank, float(i * P), None, ALU.add))
                link(v.tensor_tensor(RF[:, :, 4 + i], t, n_rows, ALU.is_lt))
                link(v.tensor_scalar(tile, n_rows, 1.0, None, ALU.subtract))
                link(v.tensor_tensor(t, t, tile, ALU.min))
                link(v.scalar_tensor_tensor(RF[:, :, i], expert, float(TOK), t, ALU.mult, ALU.add))
                link(v.tensor_scalar(RF[:, :, 6 + i], const("tiles"), float(TROWS), const("dump")[:, i:i + 1], ALU.mult, ALU.add))
            link(v.tensor_scalar(RF[:, :, 2], expert, float(P), const("lane"), ALU.mult, ALU.add))
            link(v.tensor_copy(RF[:, :, 3], expert))
            link(v.tensor_copy(RI[:, :, :], RF[:, :, 0:4]))

            link(v.memset(RC[:, :, :], 0))
            link(v.tensor_copy(RC[:, 0:TILES, 0:2], RI[:, :, 0:2]))
            link(v.tensor_copy(RC[:, 0:TILES - 1, 2], RI[:, 1:TILES, 2]))
            link(v.tensor_copy(RC[:, 2:TILES + 2, 3], RI[:, :, 2]))

            def note_indices(t, r):
                v.tensor_copy(IX[:, r:r + 1, :], RC[:, ds(t + 2, 1), :]).then_inc(ix_ready[r], 1)
            dve.sem_inc(table_done, 1)

            note_indices(-2, 0)
            note_indices(-1, 1)

            notes = Chain(dve, tile_links, 7)

            def results(t, r, n):
                dve.wait_ge(y_full, t + 1)
                dve.wait_ge(b2_ready, t + 1)
                at_least(dve, y_sent[r], 16 * TH * n)
                for i in range(TH):
                    v.scalar_tensor_tensor(Y[:, r, i, :], PY[:, r, i, :], GY[:, r, 0, i:i + 1], BW[:, r, i, :], ALU.mult, ALU.add
                                           ).then_inc(y_ready, 1)
                v.tensor_copy(DI[:, r, :], GY[:, r, 1, :]).then_inc(y_ready, 1)

            def rows_in_parts(t):
                dve.wait_ge(xt_full, t + 1)
                if is_tile(t - 1):
                    dve.wait_ge(h_full, PAIRS * t)
                v.tensor_copy(XP[:, 0, :, :], PT[:, :, :]).then_inc(x_hi, 1)
                dve.wait_ge(x_hi, t + 1)
                v.tensor_tensor(XP[:, 1, :, :], PT[:, :, :], XP[:, 0, :, :].bitcast(f32), ALU.subtract).then_inc(x_lo, 1)

            def do(t, r, n):
                s1, n1 = other(r, n, 1)
                sm, nm = other(r, n, -1)
                g = [G[:, i, :] for i in range(4)]
                w0, w1, e0, token = (XG[:, s1, :, D + i] for i in range(4))

                def note(j):
                    if j == 0:
                        notes.at(t + 1)
                        dve.wait_ge(x_gathered[s1], 16 * TH * (n1 + 1))
                        notes.did(v.tensor_copy(FX[:, :].unsqueeze(1), RF[:, ds(t + 1, 1), :]))
                        notes.did(v.tensor_tensor(g[1], w0, w1, ALU.subtract))
                        notes.wait()
                    elif j == 1:
                        notes.did(v.tensor_scalar(g[0], e0, FX[:, 3:4], None, ALU.is_equal))
                        notes.wait()
                        notes.did(v.tensor_tensor(g[1], g[1], g[0], ALU.mult))
                        notes.did(v.tensor_scalar(g[2], g[0], -float(TOK), float(TOK), ALU.mult, ALU.add))
                        notes.wait()
                    elif j == 2:
                        v.tensor_tensor(GT[:, ds(t + 1, 1), 0, :], g[1].unsqueeze(1), w1.unsqueeze(1), ALU.add
                                        ).then_inc(x_noted, 1)
                        v.tensor_tensor(g[2], g[2], token, ALU.add).then_inc(x_noted, 1)
                        dve.wait_ge(x_noted, 3 * (t + 1) + 2)
                        notes.did(v.tensor_tensor(g[2], g[2], FX[:, 6:8], ALU.subtract))
                        notes.wait()
                    else:
                        notes.did(v.tensor_tensor(g[2], g[2], FX[:, 4:6], ALU.mult))
                        notes.wait()
                        v.tensor_tensor(GT[:, ds(t + 1, 1), 1, :], g[2].unsqueeze(1), FX[:, 6:8].unsqueeze(1), ALU.add
                                        ).then_inc(x_noted, 1)

                for j in range(PAIRS):
                    if j < 2 and is_tile(t - 1):
                        for q in (2 * j, 2 * j + 1):
                            if q < DVE2:
                                dve.wait_ge(w2_hi, PAIRS * (t - 1) + q + 1)
                                v.tensor_tensor(piece(W2P[:, 1, :], q), piece(WG2[:, sm, :], q),
                                                piece(W2P[:, 0, :], q).bitcast(f32), ALU.subtract).then_inc(w2_lo, 1)
                            if q == 0:
                                at_least(dve, y_ready, 3 * (t - 2))
                                v.tensor_copy(GY[:, sm:sm + 1, :, :], GT[:, ds(t - 1, 1), :, :]).then_inc(gy_ready, 1)
                    if is_tile(t):
                        dve.wait_ge(h_hi, PAIRS * t + j + 1)
                        v.tensor_tensor(HP[:, r, 1, 2 * j:2 * j + 2, :], HF[:, 2 * j:2 * j + 2, :],
                                        HP[:, r, 0, 2 * j:2 * j + 2, :].bitcast(f32), ALU.subtract).then_inc(h_lo, 1)
                    if j == 1 and is_tile(t + 1):
                        rows_in_parts(t + 1)
                    if j == 2 and is_tile(t - 2):
                        results(t - 2, r, n - 1)
                for q in range(PAIRS):
                    if is_tile(t + 2):
                        dve.wait_ge(w1_hi, PAIRS * (t + 2) + q + 1)
                        v.tensor_tensor(piece(W1P[:, r, 1, :], q), piece(WG1[:, r, :], q),
                                        piece(W1P[:, r, 0, :], q).bitcast(f32), ALU.subtract).then_inc(w1_lo, 1)
                    if is_tile(t + 1):
                        note(q)
                if is_tile(t + 1):
                    note_indices(t + 1, s1)
            over_turns(dve, do)

        @block.gpsimd
        def _(pool):
            g = nc.gpsimd

            def gather_rows(t, r, n):
                if is_tile(t - 2):
                    pool.wait_ge(xt_full, t - 1)
                    pool.wait_ge(x_noted, 3 * (t - 1))
                pool.sem_inc(alone, 1)
                for i in range(TH):
                    g.indirect_dma_start(out=XG[:, r, i, :], out_offset=None, in_=rows,
                                         in_offset=IND(ap=IX[:, r, i:i + 1], axis=0)).then_inc(x_gathered[r], 16)

            def gather_first(t, r, n):
                if is_tile(t - 2):
                    pool.wait_ge(w1_lo, PAIRS * (t - 1))
                    pool.wait_ge(b1_ready, t - 1)
                pool.sem_inc(alone, 1)
                g.indirect_dma_start(out=WG1[:, r, :], out_offset=None, in_=experts1,
                                     in_offset=IND(ap=IX[:, (r + 1) % 2, 2:3], axis=0)).then_inc(w1_gathered[r], 16)

            def gather_second(t, r, n):
                if is_tile(t - 2):
                    pool.wait_ge(w2_lo, DVE2 * (t - 1))
                    pool.wait_ge(w2_lo_pool, (PAIRS - DVE2) * (t - 1))
                pool.sem_inc(alone, 1)
                g.indirect_dma_start(out=WG2[:, r, :], out_offset=None, in_=experts2,
                                     in_offset=IND(ap=IX[:, r, 3:4], axis=0)).then_inc(w2_gathered[r], 16)

            pool.wait_ge(table_done, 1)
            pool.sem_inc(alone, 1)
            g.indirect_dma_start(out=WG1[:, 0, :], out_offset=None, in_=experts1,
                                 in_offset=IND(ap=RI[:, 0, 2:3], axis=0)).then_inc(w1_gathered[0], 16)

            def do(t, r, n):
                sm, nm = other(r, n, -1)
                if not isinstance(t, int) or t < TILES:
                    pool.wait_ge(ix_ready[r], n + 2)
                if is_tile(t):
                    gather_second(t, r, n)
                if is_tile(t + 3):
                    gather_first(t + 3, *other(r, n, 3))
                if is_tile(t - 1):
                    pool.wait_ge(gy_ready, t)
                    at_least(pool, y_ready, 3 * (t - 2))
                    g.tensor_tensor(BW[:, sm, :, :], WG2[:, sm, HC * D:].unsqueeze(1).to_broadcast([P, TH, D]),
                                    GY[:, sm, 0, :].unsqueeze(2).to_broadcast([P, TH, D]), ALU.mult).then_inc(b2_ready, 1)
                    for q in range(DVE2, PAIRS):
                        pool.wait_ge(w2_hi, PAIRS * (t - 1) + q + 1)
                        g.tensor_tensor(piece(W2P[:, 1, :], q), piece(WG2[:, sm, :], q),
                                        piece(W2P[:, 0, :], q).bitcast(f32), ALU.subtract).then_inc(w2_lo_pool, 1)
                if is_tile(t + 2):
                    gather_rows(t + 2, r, n + 1)
                if is_tile(t - 2):
                    wait_alone(pool, y_ready, 3 * (t - 1), alone)
                    for i in range(TH):
                        g.indirect_dma_start(out=ys, out_offset=IND(ap=DI[:, r, i:i + 1], axis=0),
                                             in_=Y[:, r, i, :], in_offset=None).then_inc(y_sent[r], 16)
            over_turns(pool, do)
            for r in range(2):
                pool.wait_ge(y_sent[r], 16 * TH * ((TILES + 1 - r) // 2))

        @block.scalar
        def _(act):
            a = nc.scalar

            def do(t, r, n):
                s1, n1 = other(r, n, 1)
                sm, nm = other(r, n, -1)
                for j in range(PAIRS):
                    if j < 2 and is_tile(t - 1):
                        if j == 0:
                            act.wait_ge(w2_gathered[sm], 16 * (nm + 1))
                            at_least(act, y_full, t - 1)
                        for q in (2 * j, 2 * j + 1):
                            a.copy(piece(W2P[:, 0, :], q), piece(WG2[:, sm, :], q)).then_inc(w2_hi, 1)
                    if is_tile(t):
                        act.wait_ge(h_full, PAIRS * t + j + 1)
                        at_least(act, h_lo, PAIRS * (t - 1) + j + 1)
                        if j == 0:
                            act.wait_ge(b1_ready, t + 1)
                        for c in (2 * j, 2 * j + 1):
                            a.activation(HF[:, c, :], PH[:, j, c % 2, :], ACT.Gelu_apprx_tanh,
                                         bias=B1[:, r, c:c + 1]).then_inc(h_raw, 1)
                        act.wait_ge(h_raw, HC * t + 2 * j + 2)
                        at_least(act, y_full, t - 1)
                        a.copy(HP[:, r, 0, 2 * j:2 * j + 2, :], HF[:, 2 * j:2 * j + 2, :]).then_inc(h_hi, 1)
                if is_tile(t + 2):
                    act.wait_ge(w1_gathered[r], 16 * (n + 2))
                    if is_tile(t):
                        act.wait_ge(h_raw, HC * (t + 1))
                        act.wait_ge(h_full, PAIRS * (t + 1))
                    a.copy(B1[:, r, :], WG1[:, r, KC * HID:]).then_inc(b1_ready, 1)
                    for q in range(PAIRS):
                        a.copy(piece(W1P[:, r, 0, :], q), piece(WG1[:, r, :], q)).then_inc(w1_hi, 1)
            over_turns(act, do)

        @block.tensor
        def _(pe):
            m = nc.tensor
            terms = ((0, 0), (0, 1), (1, 0))

            def do(t, r, n):
                s1, n1 = other(r, n, 1)
                sm, nm = other(r, n, -1)
                if is_tile(t):
                    pe.wait_ge(x_lo, t + 1)
                    pe.wait_ge(w1_lo, PAIRS * (t + 1))
                    for c in range(HC):
                        if is_tile(t - 1) and c % 2 == 0:
                            pe.wait_ge(h_raw, HC * (t - 1) + c + 2)
                        for k in range(KC):
                            for a, o in terms:
                                i = m.matmul(PH[:, c // 2, c % 2, :], W1P[:, r, a, k * HID + c * P:k * HID + c * P + P], XP[:, o, k, :],
                                             start=(k == 0 and (a, o) == terms[0]), stop=(k == KC - 1 and (a, o) == terms[-1]))
                        if c % 2 == 1:
                            i.then_inc(h_full, 1)
                if is_tile(t + 1):
                    pe.wait_ge(x_gathered[s1], 16 * TH * (n1 + 1))
                    at_least(pe, x_lo, t + 1)
                    for k in range(KC):
                        for i in range(TH):
                            last = m.transpose(PT[:, k, i * P:i * P + P], XG[:, s1, i, k * P:k * P + P], const("ident"))
                    last.then_inc(xt_full, 1)
                if is_tile(t - 1):
                    if is_tile(t - 3):
                        pe.wait_ge(y_ready, 3 * (t - 2))
                    for i in range(TH):
                        for c in range(HC):
                            if i == 0 and c % 2 == 0:
                                pe.wait_ge(h_lo, PAIRS * (t - 1) + c // 2 + 1)
                                q = c // 2
                                if q < DVE2:
                                    pe.wait_ge(w2_lo, DVE2 * (t - 1) + q + 1)
                                else:
                                    pe.wait_ge(w2_lo_pool, (PAIRS - DVE2) * (t - 1) + q - DVE2 + 1)
                            for a, o in terms:
                                last = m.matmul(PY[:, sm, i, :], HP[:, sm, a, c, i * P:i * P + P], W2P[:, o, c * D:(c + 1) * D],
                                                start=(c == 0 and (a, o) == terms[0]), stop=(c == HC - 1 and (a, o) == terms[-1]))
                    last.then_inc(y_full, 1)
            over_turns(pe, do)


def stage3(nc, make, X, stats, stats_links, ys, out):
    f32 = mybir.dt.float32
    ALU = mybir.AluOpType
    ds = bass.ds
    ctx = ExitStack()
    with ctx:
        sb, pb, sem = make(ctx)
        YC = sb("YC", [P, 2, 2, C, D], f32)
        S = sb("S", [P, 2, C, D], f32)
        T = sb("T", [P, 2, C, D], f32)
        O = sb("O", [P, 2, C, D], f32)
        ST = sb("STF", [P, C, 6], f32)
        MV = sb("MVF", [P, C, 2], f32)
        SM = sb("SMF", [P, 4, C], f32)
        loaded = [sem("y_loaded0"), sem("y_loaded1")]
        summed, normed, added = sem("summed"), sem("normed"), sem("added")
        stored = [sem("stored0"), sem("stored1")]
        links = sem("finish_links")
        block = ctx.enter_context(nc.Block())
        yv = ys[0:2 * TOK].rearrange("(k b p c) e -> b p k (c e)", k=2, p=P, c=C)
        ov = out.rearrange("(b p c) e -> b p (c e)", p=P, c=C)

        def over_batches(eng, do):
            for r in range(2):
                do(0, r, r)
            with eng.Fori(1, B // 2) as lap:
                for r in range(2):
                    do(lap, r, 2 * lap + r)

        @block.sync
        def _(sp):
            def do(lap, r, b):
                at_least(sp, summed, b - 1) if isinstance(b, int) else sp.wait_ge(summed, b - 1)
                sp.dma_start(YC[:, r, :, :, :].rearrange("p k c e -> p k (c e)"), yv[ds(b, 1)].rearrange("a p k f -> (a p) k f")
                             ).then_inc(loaded[r], 16)
            over_batches(sp, do)

        @block.gpsimd
        def _(pool):
            def do(lap, r, b):
                pool.wait_ge(loaded[r], 16 * (lap + 1))
                at_least(pool, normed, b - 1)
                nc.gpsimd.tensor_tensor(S[:, r, :, :], YC[:, r, 0, :, :], YC[:, r, 1, :, :], ALU.add).then_inc(summed, 1)
            over_batches(pool, do)

        @block.vector
        def _(dve):
            v = nc.vector
            chain = Chain(dve, links, stats_links)

            def do(lap, r, b):
                chain.n = 0
                chain.at(b)
                dve.wait_ge(summed, b + 1)
                var, y, t, rs = (SM[:, i, :] for i in range(4))
                stats(v, chain, lambda c: S[:, r, c, :], ST, MV, var, y, t, rs)
                at_least(dve, added, b - 1)
                for c in range(C):
                    i = v.tensor_scalar(T[:, r, c, :], S[:, r, c, :], MV[:, c, 0:1], rs[:, c:c + 1], ALU.subtract, ALU.mult)
                i.then_inc(normed, 1)
                dve.wait_ge(normed, b + 1)
                at_least(dve, stored[r], 16 * lap)
                v.tensor_tensor(O[:, r, :, :], T[:, r, :, :], X[:, ds(C * b, C), :], ALU.add).then_inc(added, 1)
            over_batches(dve, do)

        @block.scalar
        def _(act):
            def do(lap, r, b):
                act.wait_ge(added, b + 1)
                act.dma_start(ov[ds(b, 1)].rearrange("a p f -> (a p) f"), O[:, r, :, :].rearrange("p c e -> p (c e)")
                              ).then_inc(stored[r], 16)
            over_batches(act, do)
            for r in range(2):
                act.wait_ge(stored[r], 16 * B // 2)


def constants():
    a = np.zeros((P, NCONST), np.float32)

    def put(name, value):
        at, w = CONST[name]
        a[:, at:at + w] = np.broadcast_to(value, (P, w))

    p, q = np.arange(P)[:, None], np.arange(P)[None, :]
    put("ident", p == q)
    put("lower", p < q)
    put("ones", 1)
    put("neg_half", np.where(p // CDH == q // CDH, -0.5, 0))
    put("indicator", np.concatenate([np.where(8 * m + p // DH == np.arange(H), -0.5, 0) for m in range(KC)], 1))
    put("iota8", np.tile(np.arange(NE), C))
    put("region", np.tile(np.arange(NE) * TOK, C))
    put("token", (np.arange(B)[None, :, None] * N + p[:, :, None] * C + np.arange(C)).reshape(P, -1))
    put("steps", np.tile(np.arange(THR) * TROWS, NE))
    put("tiles", np.arange(TILES))
    put("iota_t", np.tile(np.arange(NE), TILES))
    put("lane", p)
    put("dump", 2 * TOK + np.arange(TH) * P + p)
    return a


def kernel(**inputs):
    import concourse.bacc as bacc
    from concourse.bass_utils import run_bass_kernel_spmd
    g = {k.split("_", 2)[2]: np.asarray(v) for k, v in inputs.items()}

    def cols(v, n):
        return v.reshape(n, P).T

    def square(w):
        return w.reshape(KC, P, D).transpose(1, 0, 2).reshape(P, KC * D)

    def by_partition(w):
        return w.reshape(NE, -1, P, w.shape[-1]).transpose(0, 2, 1, 3).reshape(NE * P, -1)

    vecs = np.zeros((P, NVEC), np.float32)
    for name, value in [("gamma1", g["gamma1"]), ("gamma2", g["gamma2"]), ("tau_t", g["tau_t"].reshape(-1)),
                        ("tau_c", cols(np.repeat(g["tau_c"].reshape(-1), CDH), 2)),
                        ("ln1_w", cols(g["ln1_w"], KC)), ("ln1_b", cols(g["ln1_b"], KC)),
                        ("ln2_w", cols(g["ln2_w"], KC)), ("ln2_b", cols(g["ln2_b"], KC)),
                        ("router", g["w_router"].reshape(KC, P, NE).transpose(1, 0, 2).reshape(P, -1))]:
        at, w = VEC[name]
        vecs[:, at:at + w] = np.broadcast_to(value, (P, w))
    arrays = {
        "x": g["x"].reshape(TOK, D),
        "weights": np.concatenate([square(g[n]) for n in ("Wqk_t", "Wv_t", "Wo_t", "Wqk_c")]
                                  + [square(np.ascontiguousarray(g["Wv_c"].T)), square(g["Wo_c"])], 1),
        "vecs": vecs,
        "consts": constants(),
        "experts1": np.concatenate([by_partition(g["w1"]), by_partition(g["b1"][:, :, None])], 1),
        "experts2": np.concatenate([by_partition(g["w2"]), np.repeat(g["b2"], P, 0)], 1),
    }
    arrays = {k: np.ascontiguousarray(v) for k, v in arrays.items()}
    nc = bacc.Bacc("TRN2", target_bir_lowering=False, num_devices=1)
    aps = [nc.dram_tensor(k, v.shape, mybir.dt.from_np(v.dtype), kind="ExternalInput").ap() for k, v in arrays.items()]
    out = nc.dram_tensor("out", (TOK, D), mybir.dt.float32, kind="ExternalOutput").ap()
    program(nc, *aps, out)
    result = run_bass_kernel_spmd(nc, [arrays], core_ids=[0])
    return result.results[0]["out"].reshape(B, N, D)
```

```python
import math
from contextlib import ExitStack

import numpy as np

import concourse.bass as bass
from concourse import mybir

B, N, D = 8, 512, 256
H, DH = 16, 16
CH, CDH = 8, 32
NE, HID = 8, 1024
EPS = 1e-5
P = 128
C = N // P
KC = D // P
TOK = B * N
TROWS = 256
TH = TROWS // P
TILES = (2 * TOK + NE * (TROWS - 1)) // TROWS
THR = TOK // TROWS
ROW = D + 4
W1ROW = (D + 1) * HID // P
W2ROW = HID * D // P + D
DVE2 = 3
GROUPS = H // 4
SETS = 2 * GROUPS
UNITS = 4 * SETS
KA = 102
PRE_USES, POST_USES = 7, 22
BANK = POST_USES // 2
LOADS = 16 * 14

CONST = {}
_at = 0
for _name, _width in [("ident", P), ("lower", P), ("ones", P), ("neg_half", P), ("indicator", 2 * H),
                      ("iota8", 4 * NE), ("region", 4 * NE), ("token", B * C), ("steps", NE * THR),
                      ("tiles", TILES), ("iota_t", TILES * NE), ("lane", 1), ("dump", TH)]:
    CONST[_name] = (_at, _width)
    _at += _width
NCONST = _at
VEC = {}
_at = 0
for _name, _width in [("gamma1", D), ("gamma2", D), ("tau_t", H), ("tau_c", 2), ("ln1_w", KC), ("ln1_b", KC),
                      ("ln2_w", KC), ("ln2_b", KC), ("router", KC * NE)]:
    VEC[_name] = (_at, _width)
    _at += _width
NVEC = _at

EARLY_AT = {9: ['norm1']}
PRE_AT = {0: ['xt0'], 1: ['xt1'], 2: ['qk0'], 3: ['qk1'], 7: ['sq'], 14: ['v0'], 15: ['v1']}
POST_AT = {2: ['residual'], 3: ['untok0'], 4: ['untok1', 'ontok'], 5: ['proj'], 7: ['x2t'], 8: ['qkc'], 9: ['gram', 'clear'], 10: ['dist'], 11: ['mix', 'weff'], 12: ['chan']}
LATE_AT = {1: ['z3t'], 2: ['logits'], 3: ['prefix']}
STEPS = [name for at in (EARLY_AT, PRE_AT, POST_AT, LATE_AT) for names in at.values() for name in names]


def schedule(eng, own):
    do = dict.fromkeys(STEPS + ["att", "att_end", "drain"], lambda *_: None)
    do.update(own)

    def body(b, par, att=True, early=False, pre=False, post=False, late=False, first=False):
        for pos in range(2 * SETS):
            if att:
                do["att"](b, par, pos, first)
            for flag, at, of, of_par in ((early, EARLY_AT, b + 2, par), (pre, PRE_AT, b + 1, 1 - par), (late, LATE_AT, b - 2, par),
                                         (post, POST_AT, b - 1, 1 - par)):
                for name in at.get(pos, []):
                    if flag:
                        do[name](of, of_par)
            if att:
                do["att_end"](b, par, pos, first)

    body(-2, 0, att=False, early=True)
    body(-1, 1, att=False, early=True, pre=True)
    body(0, 0, early=True, pre=True, first=True)
    body(1, 1, early=True, pre=True, post=True)
    with eng.Fori(0, B // 2 - 2) as lap:
        b = 2 * lap + 2
        body(b, 0, early=True, pre=True, post=True, late=True)
        body(b + 1, 1, early=True, pre=True, post=True, late=True)
    body(B - 2, 0, pre=True, post=True, late=True)
    body(B - 1, 1, post=True, late=True)
    do["drain"](B - 1, 1)
    body(B, 0, att=False, post=True, late=True)
    body(B + 1, 1, att=False, late=True)


def at_least(eng, sem, value):
    if not isinstance(value, int) or value > 0:
        eng.wait_ge(sem, value)


def wait_alone(eng, sem, value, spare):
    eng.wait_ge(sem, value)
    eng.sem_inc(spare, 1)


class Chain:
    def __init__(self, eng, sem, per):
        self.eng, self.sem, self.per, self.n, self.b = eng, sem, per, 0, 0

    def did(self, ins):
        ins.then_inc(self.sem, 1)
        self.n += 1

    def at(self, b):
        assert self.n in (0, self.per), (self.n, self.per)
        self.b, self.n = b, 0

    def wait(self, spare=None):
        self.eng.wait_ge(self.sem, self.b * self.per + self.n)
        if spare is not None:
            self.eng.sem_inc(spare, 1)


def program(nc, x, weights, vecs, consts, experts1, experts2, out):
    f32, bf16, i32, u32 = mybir.dt.float32, mybir.dt.bfloat16, mybir.dt.int32, mybir.dt.uint32
    ACT, ALU, AX = mybir.ActivationFunctionType, mybir.AluOpType, mybir.AxisListType
    ds = bass.ds
    IND = bass.IndirectOffsetOnAxis

    qs = nc.dram_tensor("q_parts", (KC, 3, P, N), bf16, kind="Internal").ap()
    ns = nc.dram_tensor("norm_parts", (H, 3, N), bf16, kind="Internal").ap()
    rows = nc.dram_tensor("expert_rows", (NE * TOK, ROW), f32, kind="Internal").ap()
    ys = nc.dram_tensor("choice_rows", (2 * TOK + TILES * TROWS, D), f32, kind="Internal").ap()

    outer = ExitStack()
    with outer:
        def make(ctx):
            return (lambda n, s, d: ctx.enter_context(nc.sbuf_tensor(n, s, d)),
                    lambda n, s, d: ctx.enter_context(nc.psum_tensor(n, s, d)),
                    lambda n: ctx.enter_context(nc.semaphore(n)))

        sb, _, sem = make(outer)
        alone = sem("alone")
        X = sb("X", [P, B * C, D], f32)
        KT = sb("KT", [P, NCONST], f32)
        COUNT = sb("COUNT", [P, C + 1, NE], f32)
        RF = sb("RF", [P, TILES, 8], f32)
        RI = sb("RI", [P, TILES, 4], i32)
        RC = sb("RC", [P, TILES + 2, 4], i32)

        def const(name):
            a, w = CONST[name]
            return KT[:, a:a + w]

        def rsqrt(v, chain, out_ap, var, y, t):
            chain.did(v.tensor_scalar(y.bitcast(i32), var.bitcast(i32), -0.5, 1597463007.0, ALU.mult, ALU.add))
            chain.wait()
            for n in range(3):
                chain.did(v.tensor_tensor(t, y, y, ALU.mult))
                chain.wait()
                chain.did(v.scalar_tensor_tensor(t, t, -0.5, var, ALU.mult, ALU.mult))
                chain.wait()
                chain.did(v.scalar_tensor_tensor(out_ap if n == 2 else y, t, 1.5, y, ALU.add, ALU.mult))
                chain.wait()

        def stats(v, chain, src, st, mv, var, y, t, r):
            v.sem_inc(alone, 1)
            for c in range(C):
                chain.did(v.bn_stats(st[:, c, :], src(c)))
            chain.wait(alone)
            for c in range(C):
                chain.did(v.bn_aggr(mv[:, c, :], st[:, c, :]))
            chain.wait()
            chain.did(v.tensor_scalar_add(var, mv[:, :, 1], EPS))
            chain.wait()
            rsqrt(v, chain, r, var, y, t)
        STATS = 19

        mix = ExitStack()
        with mix:
            sb, pb, sem = make(mix)
            W = sb("W", [P, 6, KC, D], f32)
            wqk, wv, wo, wqkc, wvt, woc = range(6)
            VV = sb("VV", [P, NVEC], f32)
            MU = sb("MU", [P, B * C], f32)
            RS = sb("RS", [P, B * C], f32)
            ST = sb("ST", [P, C, 6], f32)
            MV = sb("MV", [P, C, 2], f32)
            SM = sb("SM", [P, 4, 2, C], f32)
            Z1 = sb("Z1", [P, C, D], f32)
            XT = sb("XT", [P, KC, N], f32)
            QF = sb("QF", [P, KC, N], f32)
            QR = sb("QR", [P, KC, N], f32)
            QP = sb("QP", [P, KC, 3, N], bf16)
            SQ = sb("SQ", [P, KC, N], f32)
            NF = sb("NF", [H, 2, N], f32)
            NP = sb("NP", [H, 3, N], bf16)
            OPA = sb("OPA", [KA, 2, 8 * N], bf16)
            OPB = sb("OPB", [KA, 2, 8 * N], bf16)
            VA = sb("VA", [P, 2, C, H, 32], f32)
            E = sb("E", [P, 2, 4, 2, N], f32)
            OT = sb("OT", [P, GROUPS, N], f32)
            ON = sb("ON", [P, C, D], f32)
            REC = sb("REC", [P, C, H], f32)
            OTN = sb("OTN", [P, KC, N], f32)
            ST2 = sb("ST2", [P, C, 6], f32)
            MV2 = sb("MV2", [P, C, 2], f32)
            SM2 = sb("SM2", [P, 6, C], f32)
            X1 = sb("X1", [P, C, D], f32)
            Z2, X2T, QC, Z3T = ON, OTN, ON, OTN
            GS = sb("GS", [P, 2, P], f32)
            DG = sb("DG", [P, 2, P], f32)
            L = sb("L", [P, 2, CDH], f32)
            LX = sb("LX", [P, 2, CDH], f32)
            LS = sb("LS", [P, 4, 2], f32)
            AT = sb("AT", [P, 2, P], f32)
            MB = sb("MB", [P, KC, D], f32)
            WE = sb("WE", [P, KC, D], f32)
            PAY = sb("PAY", [P, C, ROW], f32)
            ZERO = sb("ZERO", [P, C * ROW], f32)
            LG = sb("LG", [P, C, NE], f32)
            PR = sb("PR", [P, C, NE], f32)
            R4 = sb("R4", [P, 3, C], f32)
            TOP = sb("TOP", [P, C, NE], f32)
            TI = sb("TI", [P, C, NE], u32)
            TF = sb("TF", [P, C, NE], f32)
            OH = sb("OH", [P, 3, C, NE], f32)
            PX = sb("PX", [P, 2, C, NE], f32)
            RK = sb("RK", [P, 3, C, NE], f32)
            SF = sb("SF", [P, 2, C], f32)
            SLOT = sb("SLOT", [P, 2, C], i32)

            PS = pb("PS", [P, 2, 2, N], f32)
            PO = pb("PO", [P, N], f32)
            PA = pb("PA", [P, N], f32)
            PB = pb("PB", [P, 2, N], f32)

            def vec(name):
                a, w = VEC[name]
                return VV[:, a:a + w]

            x_loaded, v_loaded, w_loaded, x_rest = sem("x_loaded"), sem("v_loaded"), sem("w_loaded"), sem("x_rest")
            setup_done, setup_pool, early_links = sem("setup_done"), sem("setup_pool"), sem("early_links")
            pre_links, post_links = sem("pre_links"), sem("post_links")
            z1_ready, rs_ready = sem("z1_ready"), sem("rs_ready")
            qf_ready, sq_ready, qp_ready, np_ready = sem("qf_ready"), sem("sq_ready"), sem("qp_ready"), sem("np_ready")
            pre_full, pre_free = sem("pre_full"), sem("pre_free")
            post_full = sem("post_full")
            post_free = [sem("post_free0"), sem("post_free1")]
            q_written = sem("q_written")
            op_loaded = [sem("op_loaded0"), sem("op_loaded1")]
            s_full, e_ready, pv_done, po_read = sem("s_full"), sem("e_ready"), sem("pv_done"), sem("po_read")
            on_ready, otn_ready, z2_ready, x2t_ready = sem("on_ready"), sem("otn_ready"), sem("z2_ready"), sem("x2t_ready")
            qc_ready, dg_ready, l_ready, lx_ready, at_ready = (sem("qc_ready"), sem("dg_ready"), sem("l_ready"),
                                                              sem("lx_ready"), sem("at_ready"))
            mb_ready, we_ready, z3_ready, z3t_ready = sem("mb_ready"), sem("we_ready"), sem("z3_ready"), sem("z3t_ready")
            lg_ready, pr_ready, oh_ready, slot_ready = sem("lg_ready"), sem("pr_ready"), sem("oh_ready"), sem("slot_ready")
            table_links = sem("table_links")
            rows_clear, x1_ready, x1_links = sem("rows_clear"), sem("x1_ready"), sem("x1_links")
            sent, rows_free = sem("sent"), sem("rows_free")

            def emptied(eng, b, j):
                eng.wait_ge(post_free[j % 2], BANK * b + j // 2 + 2)

            block = mix.enter_context(nc.Block())

            @block.sync
            def _(sp):
                xv = x.rearrange("(b p c) e -> b p c e", p=P, c=C)
                sp.dma_start(X[:, 0:C, :], xv[0]).then_inc(x_loaded, 16)
                sp.dma_start(VV[:, :], vecs).then_inc(v_loaded, 16)
                sp.dma_start(KT[:, :], consts).then_inc(v_loaded, 16)
                sp.dma_start(W[:, :, :, :], weights.rearrange("p (w k n) -> p w k n", w=6, k=KC)).then_inc(w_loaded, 16)
                for b in range(1, B):
                    sp.dma_start(X[:, C * b:C * b + C, :], xv[b]).then_inc(x_rest, 16)
                sp.wait_ge(setup_pool, 4)
                sp.wait_ge(setup_pool, 6)

                def store(b, m):
                    wait_alone(sp, qp_ready, KC * b + m + 1, alone)
                    at_least(sp, op_loaded[m], LOADS * b)
                    sp.dma_start(qs[m].rearrange("x p n -> p x n"), QP[:, m, :, :]).then_inc(q_written, 16)

                def store_norms(b):
                    at_least(sp, np_ready, b + 1)
                    sp.dma_start(ns, NP[:, :, :]).then_inc(q_written, 16)

                def load(b, m):
                    wait_alone(sp, q_written, 48 * (b + 1), alone)
                    at_least(sp, s_full, UNITS * b - UNITS // 2 * (1 - m))
                    v = qs[m]
                    src = [v[k].rearrange("(h d) n -> d h n", d=DH) for k in range(3)]
                    a, o = OPA[:, m, :].rearrange("p (h n) -> p h n", h=8), OPB[:, m, :].rearrange("p (h n) -> p h n", h=8)
                    order_a, order_b = (0, 1, 2, 0, 1, 0), (0, 0, 0, 1, 1, 2)
                    for k in range(6):
                        sp.dma_start(a[DH * k:DH * k + DH], src[order_a[k]]).then_inc(op_loaded[m], 16)
                        sp.dma_start(o[DH * k:DH * k + DH], src[order_b[k]]).then_inc(op_loaded[m], 16)
                    nv = ns[8 * m:8 * m + 8].rearrange("h x n -> x h n")
                    sp.dma_start(a[6 * DH:6 * DH + 3], nv).then_inc(op_loaded[m], 16)
                    sp.dma_start(o[6 * DH + 3:6 * DH + 6], nv).then_inc(op_loaded[m], 16)

                def att(b, par, pos, first):
                    if pos == 0:
                        load(b, 1)

                do = {"att": att}

                def clear(b, par):
                    at_least(sp, rows_free, b + 1)
                    sp.dma_start(rows.rearrange("(e b p r) f -> b p e (r f)", e=NE, b=B, p=P)[ds(b, 1)]
                                 .rearrange("a p e f -> (a p) e f"),
                                 ZERO[:, :].unsqueeze(1).to_broadcast([P, NE, C * ROW])).then_inc(rows_clear, 16)
                do["clear"] = clear

                def sq(b, par):
                    store(b, 0)
                    store(b, 1)
                    store_norms(b)
                    load(b, 0)
                do["sq"] = sq
                schedule(sp, do)

            @block.gpsimd
            def _(pool):
                g = nc.gpsimd
                pool.sem_inc(rows_free, 1)
                g.memset(VA[:, :, :, :, :], 1.0).then_inc(setup_pool, 1)
                g.memset(AT[:, :, :], 0.0).then_inc(setup_pool, 1)
                g.memset(ZERO[:, :], 0.0).then_inc(setup_pool, 1)
                g.memset(COUNT[:, :, :], 0.0).then_inc(setup_pool, 1)
                pool.wait_ge(setup_pool, 4)
                g.memset(OPA[6 * DH:KA, :, :], 1.0).then_inc(setup_pool, 1)
                pool.wait_ge(setup_pool, 5)
                g.memset(OPB[6 * DH:KA, :, :], 1.0).then_inc(setup_pool, 1)

                do = {}

                def qk(m):
                    def step(b, par):
                        pool.wait_ge(qf_ready, KC * b + m + 1)
                        g.tensor_tensor(SQ[:, m, :], QF[:, m, :], QF[:, m, :], ALU.mult).then_inc(sq_ready, 1)
                    return step
                do["qk0"], do["qk1"] = qk(0), qk(1)

                def residual(b, par):
                    at_least(pool, z3_ready, b)
                    mus, rss = SM2[:, 4, :], SM2[:, 5, :]
                    pool.wait_ge(rs_ready, b + 1)
                    g.tensor_copy(mus, MU[:, ds(C * b, C)]).then_inc(x1_links, 1)
                    g.tensor_copy(rss, RS[:, ds(C * b, C)]).then_inc(x1_links, 1)
                    pool.wait_ge(x1_links, 2 * b + 2)
                    g.tensor_tensor(X1[:, :, :], X[:, ds(C * b, C), :], mus.unsqueeze(2).to_broadcast([P, C, D]), ALU.subtract
                                    ).then_inc(x1_ready, 1)
                    pool.wait_ge(x1_ready, 2 * b + 1)
                    g.tensor_tensor(X1[:, :, :], X1[:, :, :], rss.unsqueeze(2).to_broadcast([P, C, D]), ALU.mult
                                    ).then_inc(x1_ready, 1)
                do["residual"] = residual

                def prefix(b, par):
                    pool.wait_ge(rows_clear, 16 * (b + 1))
                    wait_alone(pool, slot_ready, b + 1, alone)
                    for c in range(C):
                        for k in range(2):
                            g.indirect_dma_start(out=rows, out_offset=IND(ap=SLOT[:, k, c:c + 1], axis=0),
                                                 in_=PAY[:, c, :], in_offset=None).then_inc(sent, 16)
                    pool.wait_ge(sent, 16 * 2 * C * (b + 1))
                    pool.sem_inc(rows_free, 1)
                do["prefix"] = prefix
                schedule(pool, do)

            @block.scalar
            def _(act):
                a = nc.scalar
                act.wait_ge(v_loaded, 32)
                act.wait_ge(setup_pool, 6)

                do = {}

                def take(b, j):
                    act.wait_ge(pre_full, PRE_USES * b + j + 1)

                def takep(b, j):
                    act.wait_ge(post_full, POST_USES * b + j + 1)
                    return PB[:, j % 2, :]

                def affine(dst, src, w, bias):
                    return a.activation(dst, src, ACT.Identity, scale=w, bias=bias)

                def xt(k):
                    def step(b, par):
                        take(b, k)
                        affine(XT[:, k, :], PA[:, :], vec("ln1_w")[:, k:k + 1], vec("ln1_b")[:, k:k + 1]).then_inc(pre_free, 1)
                    return step
                do["xt0"], do["xt1"] = xt(0), xt(1)

                def qk(m):
                    def step(b, par):
                        take(b, 2 + m)
                        at_least(act, sq_ready, KC * b)
                        at_least(act, qp_ready, KC * b)
                        at_least(act, q_written, 48 * b)
                        a.copy(QF[:, m, :], PA[:, :]).then_inc(qf_ready, 1)
                        a.copy(QP[:, m, 0, :], PA[:, :]).then_inc(pre_free, 1)
                    return step
                do["qk0"], do["qk1"] = qk(0), qk(1)

                def vv(i):
                    def step(b, par):
                        take(b, 5 + i)
                        at_least(act, pv_done, SETS * (b - 1))
                        a.copy(VA[:, par, 2 * i:2 * i + 2, :, 0:DH],
                               PA[:, :].rearrange("p (c h d) -> p c h d", c=2, h=H)).then_inc(pre_free, 1)
                    return step
                do["v0"], do["v1"] = vv(0), vv(1)

                def ontok(b, par):
                    for m in range(KC):
                        a.copy(OTN[:, m, :], takep(b, 4 + m)).then_inc(post_free[m], 1)
                do["ontok"] = ontok

                def x2t(b, par):
                    for k in range(KC):
                        affine(X2T[:, k, :], takep(b, 8 + k), vec("ln2_w")[:, k:k + 1], vec("ln2_b")[:, k:k + 1]
                               ).then_inc(post_free[k], 1)
                do["x2t"] = x2t

                def qkc(b, par):
                    for i in range(2):
                        a.copy(QC[:, 2 * i:2 * i + 2, :], takep(b, 10 + i).rearrange("p (c e) -> p c e", c=2)
                               ).then_inc(post_free[i], 1)
                do["qkc"] = qkc

                def mixc(b, par):
                    a.copy(MB[:, :, :], takep(b, 14).rearrange("p (k e) -> p k e", k=2)).then_inc(post_free[0], 1)
                do["mix"] = mixc

                def weff(b, par):
                    a.copy(WE[:, :, :], takep(b, 15).rearrange("p (k e) -> p k e", k=2)).then_inc(post_free[1], 1)
                do["weff"] = weff

                def z3t(b, par):
                    for k in range(KC):
                        a.copy(Z3T[:, k, :], takep(b, 18 + k)).then_inc(post_free[k], 1)
                do["z3t"] = z3t

                def att(b, par, pos, first):
                    s = pos // 2
                    if first and pos == 0:
                        act.wait_ge(setup_done, 1)
                    if pos % 2 == 0:
                        at_least(act, pv_done, SETS * b + s - 1)
                    for i in range(2):
                        h = 2 * (pos % 2) + i
                        u = 4 * s + h
                        act.wait_ge(s_full, UNITS * b + u + 1)
                        a.activation(E[:, s % 2, h, :, :], PS[:, u % 2, :, :], ACT.Exp,
                                     scale=vec("tau_t")[:, 4 * (s // 2) + h:4 * (s // 2) + h + 1]).then_inc(e_ready, 1)
                do["att"] = att

                def evacuate(b, g):
                    act.wait_ge(pv_done, SETS * b + 2 * g + 2)
                    if g == 0:
                        at_least(act, post_full, POST_USES * (b - 1) + C)
                    a.copy(OT[:, g, :], PO[:, :]).then_inc(po_read, 1)

                def att_end(b, par, pos, first):
                    if pos % 4 == 1:
                        if pos > 1:
                            evacuate(b, pos // 4 - 1)
                        elif not first:
                            evacuate(b - 1, GROUPS - 1)
                do["att_end"] = att_end
                do["drain"] = lambda b, par: evacuate(b, GROUPS - 1)

                def dist(b, par):
                    act.wait_ge(l_ready, b + 1)
                    for k in range(2):
                        a.activation(LX[:, k, :], L[:, k, :], ACT.Exp, bias=LS[:, 1, k:k + 1],
                                     accum_out=LS[:, 2, k:k + 1]).then_inc(lx_ready, 1)
                do["dist"] = dist

                def logits(b, par):
                    act.wait_ge(lg_ready, b + 1)
                    a.activation(PR[:, :, :], LG[:, :, :], ACT.Exp).then_inc(pr_ready, 1)
                do["logits"] = logits
                schedule(act, do)

            @block.vector
            def _(dve):
                v = nc.vector
                for bank in range(2):
                    dve.sem_inc(post_free[bank], 1)

                def scales():
                    dve.wait_ge(v_loaded, 32)
                    dve.wait_ge(w_loaded, 16)
                    v.tensor_scalar_mul(vec("tau_t"), vec("tau_t"), 2.0 / math.sqrt(DH))
                    v.tensor_scalar_mul(vec("tau_c"), vec("tau_c"), 2.0 / math.sqrt(N))
                    for k in range(KC):
                        v.tensor_tensor(W[:, wo, k, :], W[:, wo, k, :], vec("gamma1"), ALU.mult)
                        last = v.tensor_tensor(W[:, woc, k, :], W[:, woc, k, :], vec("gamma2"), ALU.mult)
                    last.then_inc(setup_done, 1)
                    dve.wait_ge(setup_done, 1)
                    dve.wait_ge(setup_pool, 4)

                early = Chain(dve, early_links, 2 * C + 3 + 10)
                pre = Chain(dve, pre_links, 2 * KC + 3)
                post = Chain(dve, post_links, 3 * STATS + 5 * C + 25)

                def take(b, j):
                    dve.wait_ge(pre_full, PRE_USES * b + j + 1)

                def takep(b, j):
                    dve.wait_ge(post_full, POST_USES * b + j + 1)
                    return PB[:, j % 2, :]

                def xs(b, c, n=1):
                    return X[:, ds(C * b + c, n), :]

                do = {}

                def norm1(b, par):
                    early.at(b)
                    if isinstance(b, int) and b == 0:
                        dve.wait_ge(x_loaded, 16)
                    if isinstance(b, int) and b == 1:
                        dve.wait_ge(x_rest, 16 * (B - 1))
                    var, y, t, r = (SM[:, i, :, :] for i in range(4))
                    dve.sem_inc(alone, 1)
                    for c in range(C):
                        early.did(v.bn_stats(ST[:, c, :], X[:, ds(C * b + c, 1), :].rearrange("p a e -> p (a e)")))
                    early.wait(alone)
                    for c in range(C):
                        early.did(v.bn_aggr(MV[:, c, :], ST[:, c, :]))
                    early.wait()
                    early.did(v.tensor_scalar_add(var[:, 0, :], MV[:, :, 1], EPS))
                    early.did(v.tensor_scalar(var[:, 1, :], MV[:, :, 1], 1.0 + EPS, EPS * EPS, ALU.mult, ALU.add))
                    early.did(v.tensor_copy(MU[:, ds(C * b, C)], MV[:, :, 0]))
                    early.wait()
                    rsqrt(v, early, r, var, y, t)
                    at_least(dve, pre_full, PRE_USES * (b - 1) + 2)
                    for c in range(C):
                        i = v.tensor_scalar(Z1[:, c:c + 1, :], xs(b, c), MV[:, c, 0:1], r[:, 1, c:c + 1],
                                            ALU.subtract, ALU.mult)
                    i.then_inc(z1_ready, 1)
                    v.tensor_copy(RS[:, ds(C * b, C)], r[:, 0, :]).then_inc(rs_ready, 1)
                    if isinstance(b, int) and b == 0:
                        scales()
                do["norm1"] = norm1

                def qk(m):
                    def step(b, par):
                        if m == 0:
                            pre.at(b)
                        dve.wait_ge(pre_free, PRE_USES * b + 3 + m)
                        pre.did(v.tensor_tensor(QR[:, m, :], QF[:, m, :], QP[:, m, 0, :], ALU.subtract))
                        pre.wait()
                        pre.did(v.tensor_copy(QP[:, m, 1, :], QR[:, m, :]))
                        pre.wait()
                        v.tensor_tensor(QP[:, m, 2, :], QR[:, m, :], QP[:, m, 1, :], ALU.subtract).then_inc(qp_ready, 1)
                    return step
                do["qk0"], do["qk1"] = qk(0), qk(1)

                def sq(b, par):
                    take(b, 4)
                    v.tensor_copy(NF[:, 0, :], PA[0:H, :]).then_inc(pre_free, 1)
                    dve.wait_ge(pre_free, PRE_USES * b + 5)
                    pre.did(v.tensor_copy(NP[:, 0, :], NF[:, 0, :]))
                    pre.wait()
                    pre.did(v.tensor_tensor(NF[:, 1, :], NF[:, 0, :], NP[:, 0, :], ALU.subtract))
                    pre.wait()
                    pre.did(v.tensor_copy(NP[:, 1, :], NF[:, 1, :]))
                    pre.wait()
                    v.tensor_tensor(NP[:, 2, :], NF[:, 1, :], NP[:, 1, :], ALU.subtract).then_inc(np_ready, 1)
                do["sq"] = sq

                def untok(half):
                    def step(b, par):
                        if half == 0:
                            post.at(b)
                        for c in (2 * half, 2 * half + 1):
                            ps = takep(b, c).rearrange("p (h e) -> p h e", e=32)
                            post.did(v.reciprocal(REC[:, c, :], ps[:, :, DH]))
                            post.wait()
                            v.tensor_tensor(ON[:, c, :].rearrange("p (h e) -> p h e", e=DH), ps[:, :, 0:DH],
                                            REC[:, c, :].unsqueeze(2).to_broadcast([P, H, DH]), ALU.mult).then_inc(post_free[c % 2], 1)
                    return step
                do["untok0"], do["untok1"] = untok(0), untok(1)

                def stats2(b, src):
                    var, y, t, r = (SM2[:, i, :] for i in range(4))
                    stats(v, post, src, ST2, MV2, var, y, t, r)
                    return MV2, r

                def proj(b, par):
                    dve.wait_ge(x1_ready, 2 * (b + 1))
                    dve.sem_inc(alone, 1)
                    for i in range(2):
                        v.tensor_tensor(X1[:, 2 * i:2 * i + 2, :], takep(b, 6 + i).rearrange("p (c e) -> p c e", c=2),
                                        X1[:, 2 * i:2 * i + 2, :], ALU.add).then_inc(post_free[i], 1)
                    emptied(dve, b, 6)
                    emptied(dve, b, 7)
                    mv, r = stats2(b, lambda c: X1[:, c, :])
                    for c in range(C):
                        i = v.tensor_scalar(Z2[:, c, :], X1[:, c, :], mv[:, c, 0:1], r[:, c:c + 1], ALU.subtract, ALU.mult)
                    i.then_inc(z2_ready, 1)
                do["proj"] = proj

                def gram(b, par):
                    v.tensor_copy(GS[:, :, :], takep(b, 12)[:, 0:2 * P].rearrange("p (k e) -> p k e", k=2)).then_inc(post_free[0], 1)
                    emptied(dve, b, 12)
                    v.tensor_tensor(DG[:, :, :], GS[:, :, :], const("ident").unsqueeze(1).to_broadcast([P, 2, P]),
                                    ALU.mult).then_inc(dg_ready, 1)
                do["gram"] = gram

                def dist(b, par):
                    ps = takep(b, 13)[:, 0:2 * P].rearrange("p (k e) -> p k e", k=2)
                    for q in range(4):
                        r = slice(CDH * q, CDH * q + CDH)
                        i = v.tensor_tensor(L[r, :, :], ps[r, :, r], GS[r, :, r], ALU.add)
                        if q < 3:
                            post.did(i)
                    i.then_inc(post_free[1], 1)
                    emptied(dve, b, 13)
                    post.wait()
                    for k in range(2):
                        post.did(v.tensor_scalar_mul(L[:, k, :], L[:, k, :], vec("tau_c")[:, k:k + 1]))
                    post.wait()
                    post.did(v.reduce_max(LS[:, 0, :], L[:, :, :], AX.X))
                    post.wait()
                    v.tensor_scalar_mul(LS[:, 1, :], LS[:, 0, :], -1.0).then_inc(l_ready, 1)
                do["dist"] = dist

                def mixc(b, par):
                    dve.wait_ge(lx_ready, 2 * b + 2)
                    post.did(v.reciprocal(LS[:, 3, :], LS[:, 2, :]))
                    post.wait()
                    for k in range(2):
                        post.did(v.tensor_scalar_mul(LX[:, k, :], LX[:, k, :], LS[:, 3, k:k + 1]))
                    post.wait()
                    for q in range(4):
                        r = slice(CDH * q, CDH * q + CDH)
                        i = v.tensor_copy(AT[r, :, r], LX[r, :, :])
                    i.then_inc(at_ready, 1)
                do["mix"] = mixc

                def chan(b, par):
                    for i in range(2):
                        v.tensor_tensor(X1[:, 2 * i:2 * i + 2, :], takep(b, 16 + i).rearrange("p (c e) -> p c e", c=2),
                                        X1[:, 2 * i:2 * i + 2, :], ALU.add).then_inc(post_free[i], 1)
                    emptied(dve, b, 16)
                    emptied(dve, b, 17)
                    mv, r = stats2(b, lambda c: X1[:, c, :])
                    for c in range(C):
                        post.did(v.tensor_scalar(X1[:, c, :], X1[:, c, :], mv[:, c, 0:1], r[:, c:c + 1], ALU.subtract, ALU.mult))
                    post.wait()
                    post.did(v.tensor_tensor(xs(b, 0, C), xs(b, 0, C), X1[:, :, :], ALU.add))
                    post.wait()
                    mv, r = stats2(b, lambda c: X[:, ds(C * b + c, 1), :].rearrange("p a e -> p (a e)"))
                    dve.wait_ge(rows_free, b + 1)
                    for c in range(C):
                        i = v.tensor_scalar(PAY[:, c:c + 1, 0:D], xs(b, c), mv[:, c, 0:1], r[:, c:c + 1], ALU.subtract, ALU.mult)
                    i.then_inc(z3_ready, 1)
                do["chan"] = chan

                def bc(ap):
                    return ap.unsqueeze(2).to_broadcast([P, C, NE])

                def logits(b, par):
                    post.b = b
                    ps = takep(b, 20)[:, 0:C * NE].rearrange("p (c e) -> p c e", e=NE)
                    post.did(v.reduce_max(R4[:, 0, :], ps, AX.X))
                    post.wait()
                    v.tensor_tensor(LG[:, :, :], ps, bc(R4[:, 0, :]), ALU.subtract).then_inc(post_free[0], 1)
                    emptied(dve, b, 20)
                    v.tensor_copy(PAY[:, :, D + 3], const("token").rearrange("p (b c) -> p b c", c=C)[:, ds(b, 1), :]
                                  .rearrange("p a c -> p (a c)")).then_inc(lg_ready, 1)
                    dve.wait_ge(pr_ready, b + 1)
                    post.did(v.reduce_sum(R4[:, 1, :], PR[:, :, :], AX.X))
                    post.wait()
                    post.did(v.reciprocal(R4[:, 2, :], R4[:, 1, :]))
                    post.wait()
                    post.did(v.tensor_tensor(PR[:, :, :], PR[:, :, :], bc(R4[:, 2, :]), ALU.mult))
                    post.wait(alone)
                    for c in range(C):
                        post.did(v.max(TOP[:, c, :], PR[:, c, :]))
                    post.wait(alone)
                    for c in range(C):
                        post.did(v.max_index(TI[:, c, :], TOP[:, c, :], PR[:, c, :]))
                    post.wait()
                    post.did(v.tensor_copy(TF[:, :, 0:2], TI[:, :, 0:2]))
                    post.wait()
                    iota = const("iota8").rearrange("p (c e) -> p c e", e=NE)
                    for k in range(2):
                        post.did(v.tensor_tensor(OH[:, k, :, :], iota, bc(TF[:, :, k]), ALU.is_equal))
                    post.did(v.tensor_copy(PAY[:, :, D:D + 2], TOP[:, :, 0:2]))
                    post.did(v.tensor_copy(PAY[:, :, D + 2], TF[:, :, 0]))
                    post.wait()
                    v.tensor_tensor(OH[:, 2, :, :], OH[:, 0, :, :], OH[:, 1, :, :], ALU.add).then_inc(oh_ready, 1)
                do["logits"] = logits

                def prefix(b, par):
                    v.tensor_copy(PX[:, :, :, :], takep(b, 21)[:, 0:2 * C * NE].rearrange("p (k c e) -> p k c e", k=2, c=C)
                                  ).then_inc(post_free[1], 1)
                    emptied(dve, b, 21)
                    for c in range(C):
                        post.did(v.tensor_tensor(COUNT[:, c + 1, :], COUNT[:, c, :], PX[:, 1, c, :], ALU.add))
                        post.wait()
                    post.did(v.tensor_tensor(RK[:, 0, :, :], COUNT[:, 0:C, :], PX[:, 0, :, :], ALU.add))
                    post.wait()
                    post.did(v.tensor_copy(COUNT[:, 0, :], COUNT[:, C, :]))
                    post.did(v.tensor_tensor(RK[:, 0, :, :], RK[:, 0, :, :],
                                             const("region").rearrange("p (c e) -> p c e", e=NE), ALU.add))
                    post.wait()
                    for k in range(2):
                        post.did(v.tensor_tensor(RK[:, 1 + k, :, :], RK[:, 0, :, :], OH[:, k, :, :], ALU.mult))
                    post.wait()
                    post.did(v.reduce_sum(SF[:, :, :], RK[:, 1:3, :, :], AX.X))
                    post.wait()
                    v.tensor_copy(SLOT[:, :, :], SF[:, :, :]).then_inc(slot_ready, 1)
                do["prefix"] = prefix
                schedule(dve, do)
                scratch = [QR[:, k, 0:TILES * NE].rearrange("p (t e) -> p t e", e=NE) for k in range(2)]
                scratch += [SQ[:, 0, 0:6 * TILES].rearrange("p (n t) -> p n t", n=6),
                            SQ[:, 1, 0:NE * THR].rearrange("p (e k) -> p e k", e=NE),
                            SQ[:, 1, NE * THR:NE * THR + 4 * NE].rearrange("p (n e) -> p n e", n=2),
                            SQ[:, 1, NE * THR + 4 * NE:NE * THR + 5 * NE]]
                fill_tables(nc, dve, table_links, COUNT, const, scratch, (RF, RI, RC))

            @block.tensor
            def _(pe):
                t = nc.tensor
                ident = const("ident")
                pe.wait_ge(v_loaded, 32)
                pe.wait_ge(w_loaded, 16)

                def give(b, j):
                    at_least(pe, pre_free, PRE_USES * b + j)
                    return PA

                def givep(b, j):
                    pe.wait_ge(post_free[j % 2], BANK * b + j // 2 + 1)
                    return PB[:, j % 2, :]

                do = {}

                def pv(b, par, s, jc):
                    g, jp = s // 2, s % 2
                    if jc == 0:
                        pe.wait_ge(e_ready, UNITS * b + 4 * s + 4)
                        if s == 0:
                            pe.wait_ge(pre_free, PRE_USES * (b + 1))
                        if jp == 0:
                            at_least(pe, po_read, GROUPS * b + g)
                    for h in range(4):
                        i = t.matmul(PO[32 * h:32 * h + 32, :], VA[:, par, 2 * jp + jc, 4 * g + h, :],
                                     E[:, s % 2, h, jc, :], start=(jp == 0 and jc == 0), stop=(jp == 1 and jc == 1))
                    if jc == 1:
                        i.then_inc(pv_done, 1)

                def att(b, par, pos, first):
                    s = pos // 2
                    m = s // (SETS // 2)
                    if pos % SETS == 0:
                        pe.wait_ge(op_loaded[m], LOADS * (b + 1))
                    for i in range(2):
                        h = 2 * (pos % 2) + i
                        u = 4 * s + h
                        at_least(pe, e_ready, UNITS * b + u - 1)
                        hh = (4 * (s // 2) + h) % 8
                        for jc in range(2):
                            key = hh * N + (2 * (s % 2) + jc) * P
                            ins = t.matmul(PS[:, u % 2, jc, :], OPA[0:KA, m, key:key + P], OPB[0:KA, m, hh * N:hh * N + N],
                                           start=True, stop=True)
                        ins.then_inc(s_full, 1)
                do["att"] = att

                def att_end(b, par, pos, first):
                    if pos > 1:
                        pv(b, par, pos // 2 - 1, pos % 2)
                    elif not first:
                        pv(b - 1, 1 - par, SETS - 1, pos % 2)
                do["att_end"] = att_end

                def drain(b, par):
                    pv(b, par, SETS - 1, 0)
                    pv(b, par, SETS - 1, 1)
                do["drain"] = drain

                def xt(k):
                    def step(b, par):
                        pe.wait_ge(z1_ready, b + 1)
                        ps = give(b, k)
                        for c in range(C):
                            i = t.transpose(ps[:, c * P:c * P + P], Z1[:, c, k * P:k * P + P], ident)
                        i.then_inc(pre_full, 1)
                    return step
                do["xt0"], do["xt1"] = xt(0), xt(1)

                def qk(m):
                    def step(b, par):
                        ps = give(b, 2 + m)
                        for k in range(KC):
                            i = t.matmul(ps[:, :], W[:, wqk, k, m * P:m * P + P], XT[:, k, :], start=(k == 0), stop=(k == KC - 1))
                        i.then_inc(pre_full, 1)
                    return step
                do["qk0"], do["qk1"] = qk(0), qk(1)

                def sq(b, par):
                    ps = give(b, 4)
                    for m in range(KC):
                        pe.wait_ge(sq_ready, KC * b + m + 1)
                        i = t.matmul(ps[0:H, :], const("indicator")[:, H * m:H * m + H], SQ[:, m, :], start=(m == 0), stop=(m == KC - 1))
                    i.then_inc(pre_full, 1)
                do["sq"] = sq

                def vv(i):
                    def step(b, par):
                        ps = give(b, 5 + i)
                        for c in range(2):
                            for k in range(KC):
                                cc = 2 * i + c
                                ins = t.matmul(ps[:, c * D:c * D + D], XT[:, k, cc * P:cc * P + P], W[:, wv, k, :],
                                               start=(k == 0), stop=(k == KC - 1))
                        ins.then_inc(pre_full, 1)
                    return step
                do["v0"], do["v1"] = vv(0), vv(1)

                def untok(half):
                    def step(b, par):
                        pe.wait_ge(po_read, GROUPS * (b + 1))
                        for c in (2 * half, 2 * half + 1):
                            ps = givep(b, c)
                            for g in range(GROUPS):
                                i = t.transpose(ps[:, g * P:g * P + P], OT[:, g, c * P:c * P + P], ident)
                            i.then_inc(post_full, 1)
                    return step
                do["untok0"], do["untok1"] = untok(0), untok(1)

                def ontok(b, par):
                    emptied(pe, b, 2)
                    emptied(pe, b, 3)
                    for m in range(KC):
                        ps = givep(b, 4 + m)
                        for c in range(C):
                            i = t.transpose(ps[:, c * P:c * P + P], ON[:, c, m * P:m * P + P], ident)
                        i.then_inc(post_full, 1)
                do["ontok"] = ontok

                def rows_times(b, j, lhs, rhs):
                    for i in range(2):
                        ps = givep(b, j + i)
                        for c in range(2):
                            for k in range(KC):
                                cc = 2 * i + c
                                ins = t.matmul(ps[:, c * D:c * D + D], lhs[:, k, cc * P:cc * P + P], rhs(k),
                                               start=(k == 0), stop=(k == KC - 1))
                        ins.then_inc(post_full, 1)

                def proj(b, par):
                    if isinstance(b, int) and b == 0:
                        pe.wait_ge(setup_done, 1)
                    emptied(pe, b, 4)
                    emptied(pe, b, 5)
                    rows_times(b, 6, OTN, lambda k: W[:, wo, k, :])
                do["proj"] = proj

                def x2t(b, par):
                    pe.wait_ge(z2_ready, b + 1)
                    for k in range(KC):
                        ps = givep(b, 8 + k)
                        for c in range(C):
                            i = t.transpose(ps[:, c * P:c * P + P], Z2[:, c, k * P:k * P + P], ident)
                        i.then_inc(post_full, 1)
                do["x2t"] = x2t

                def qkc(b, par):
                    emptied(pe, b, 8)
                    emptied(pe, b, 9)
                    rows_times(b, 10, X2T, lambda k: W[:, wqkc, k, :])
                do["qkc"] = qkc

                def gram(b, par):
                    emptied(pe, b, 10)
                    emptied(pe, b, 11)
                    ps = givep(b, 12)
                    for k in range(2):
                        for c in range(C):
                            i = t.matmul(ps[:, k * P:k * P + P], QC[:, c, k * P:k * P + P], QC[:, c, k * P:k * P + P],
                                         start=(c == 0), stop=(c == C - 1))
                    i.then_inc(post_full, 1)
                do["gram"] = gram

                def dist(b, par):
                    pe.wait_ge(dg_ready, b + 1)
                    ps = givep(b, 13)
                    for k in range(2):
                        t.matmul(ps[:, k * P:k * P + P], DG[:, k, :], const("neg_half"), start=True, stop=False)
                        i = t.matmul(ps[:, k * P:k * P + P], const("neg_half"), DG[:, k, :], start=False, stop=True)
                    i.then_inc(post_full, 1)
                do["dist"] = dist

                def mixc(b, par):
                    pe.wait_ge(at_ready, b + 1)
                    ps = givep(b, 14)
                    for k in range(2):
                        i = t.matmul(ps[:, k * D:k * D + D], AT[:, k, :], W[:, woc, k, :], start=True, stop=True)
                    i.then_inc(post_full, 1)
                do["mix"] = mixc

                def weff(b, par):
                    emptied(pe, b, 14)
                    ps = givep(b, 15)
                    for m in range(KC):
                        for k in range(KC):
                            i = t.matmul(ps[:, m * D:m * D + D], W[:, wvt, k, m * P:m * P + P], MB[:, k, :],
                                         start=(k == 0), stop=(k == KC - 1))
                    i.then_inc(post_full, 1)
                do["weff"] = weff

                def chan(b, par):
                    emptied(pe, b, 15)
                    rows_times(b, 16, X2T, lambda k: WE[:, k, :])
                do["chan"] = chan

                def z3t(b, par):
                    pe.wait_ge(z3_ready, b + 1)
                    for k in range(KC):
                        ps = givep(b, 18 + k)
                        for c in range(C):
                            i = t.transpose(ps[:, c * P:c * P + P], PAY[:, c, k * P:k * P + P], ident)
                        i.then_inc(post_full, 1)
                do["z3t"] = z3t

                def logits(b, par):
                    emptied(pe, b, 18)
                    emptied(pe, b, 19)
                    ps = givep(b, 20)
                    for c in range(C):
                        for k in range(KC):
                            i = t.matmul(ps[:, c * NE:c * NE + NE], Z3T[:, k, c * P:c * P + P], vec("router")[:, k * NE:k * NE + NE],
                                         start=(k == 0), stop=(k == KC - 1))
                    i.then_inc(post_full, 1)
                do["logits"] = logits

                def prefix(b, par):
                    pe.wait_ge(oh_ready, b + 1)
                    ps = givep(b, 21)
                    sel = OH[:, 2, :, :].rearrange("p c e -> p (c e)")
                    t.matmul(ps[:, 0:C * NE], const("lower"), sel, start=True, stop=True)
                    t.matmul(ps[:, C * NE:2 * C * NE], const("ones"), sel, start=True, stop=True).then_inc(post_full, 1)
                do["prefix"] = prefix
                schedule(pe, do)

        stage2(nc, make, RF, RI, RC, const, alone, rows, ys, experts1, experts2)
        stage3(nc, make, X, rsqrt, ys, out)


def fill_tables(nc, dve, table_links, COUNT, const, scratch, tables):
    v, ALU, AX = nc.vector, mybir.AluOpType, mybir.AxisListType
    RF, RI, RC = tables
    TB, OE, TF, TS, CS, T1 = scratch
    linked = [0]

    def link(i):
        linked[0] += 1
        i.then_inc(table_links, 1)
        dve.wait_ge(table_links, linked[0])

    rows_of = COUNT[:, 0, :]
    link(v.memset(CS[:, :, :], 0.0))
    link(v.tensor_tensor(TS[:, :, :], rows_of.unsqueeze(2).to_broadcast([P, NE, THR]),
                         const("steps").rearrange("p (e k) -> p e k", e=NE), ALU.is_gt))
    link(v.reduce_sum(T1[:, :], TS[:, :, :], AX.X))
    link(v.tensor_copy(CS[:, 0, NE:2 * NE], T1[:, :]))
    for n, s in enumerate((1, 2, 4)):
        a, o = CS[:, n % 2, :], CS[:, (n + 1) % 2, :]
        link(v.tensor_tensor(o[:, NE:2 * NE], a[:, NE:2 * NE], a[:, NE - s:2 * NE - s], ALU.add))
    ends = CS[:, 1, NE:2 * NE]
    tile, expert, first, n_rows, rank, t = (TF[:, i, :] for i in range(6))
    link(v.tensor_scalar(t, const("tiles"), 1.0, None, ALU.add))
    link(v.tensor_scalar(tile, t, ends[:, NE - 1:NE], -1.0, ALU.min, ALU.add))
    link(v.tensor_tensor(TB[:, :, :], tile.unsqueeze(2).to_broadcast([P, TILES, NE]),
                         ends.unsqueeze(1).to_broadcast([P, TILES, NE]), ALU.is_ge))
    link(v.reduce_sum(expert, TB[:, :, :], AX.X))
    link(v.tensor_tensor(TB[:, :, :], TB[:, :, :], T1[:, :].unsqueeze(1).to_broadcast([P, TILES, NE]), ALU.mult))
    link(v.reduce_sum(first, TB[:, :, :], AX.X))
    link(v.tensor_tensor(OE[:, :, :], const("iota_t").rearrange("p (t e) -> p t e", e=NE),
                         expert.unsqueeze(2).to_broadcast([P, TILES, NE]), ALU.is_equal))
    link(v.tensor_tensor(OE[:, :, :], OE[:, :, :], rows_of.unsqueeze(1).to_broadcast([P, TILES, NE]), ALU.mult))
    link(v.reduce_sum(n_rows, OE[:, :, :], AX.X))
    link(v.tensor_tensor(rank, const("tiles"), first, ALU.subtract))
    link(v.tensor_scalar(rank, rank, float(TROWS), const("lane"), ALU.mult, ALU.add))
    for i in range(TH):
        link(v.tensor_scalar(t, rank, float(i * P), None, ALU.add))
        link(v.tensor_tensor(RF[:, :, 4 + i], t, n_rows, ALU.is_lt))
        link(v.tensor_scalar(tile, n_rows, 1.0, None, ALU.subtract))
        link(v.tensor_tensor(t, t, tile, ALU.min))
        link(v.scalar_tensor_tensor(RF[:, :, i], expert, float(TOK), t, ALU.mult, ALU.add))
        link(v.tensor_scalar(RF[:, :, 6 + i], const("tiles"), float(TROWS), const("dump")[:, i:i + 1], ALU.mult, ALU.add))
    link(v.tensor_scalar(RF[:, :, 2], expert, float(P), const("lane"), ALU.mult, ALU.add))
    link(v.tensor_copy(RF[:, :, 3], expert))
    link(v.tensor_copy(RI[:, :, :], RF[:, :, 0:4]))

    link(v.memset(RC[:, :, :], 0))
    link(v.tensor_copy(RC[:, 0:TILES, 0:2], RI[:, :, 0:2]))
    link(v.tensor_copy(RC[:, 0:TILES - 1, 2], RI[:, 1:TILES, 2]))
    link(v.tensor_copy(RC[:, 1:TILES + 1, 3], RI[:, :, 2]))


def stage2(nc, make, RF, RI, RC, const, alone, rows, ys, experts1, experts2):
    f32, f32r, i32 = mybir.dt.float32, mybir.dt.float32r, mybir.dt.int32
    ACT, ALU, AX = mybir.ActivationFunctionType, mybir.AluOpType, mybir.AxisListType
    ds = bass.ds
    IND = bass.IndirectOffsetOnAxis
    HC = HID // P
    PAIRS = HC // 2
    PIECE = KC * HID // PAIRS
    LOOP_FROM, LOOP_TO = 5, TILES - 4
    assert (LOOP_TO - LOOP_FROM) % 2 == 0 and KC * HID == HC * D
    ctx = ExitStack()
    with ctx:
        sb, pb, sem = make(ctx)
        IX = sb("IX", [P, 2, 4], i32)
        FX = sb("FX", [P, 8], f32)
        XG = sb("XG", [P, 2, TH, ROW], f32)
        WG1 = sb("WG1", [P, 2, W1ROW], f32)
        WG2 = sb("WG2", [P, 2, W2ROW], f32)
        B1 = sb("B1", [P, 2, HC], f32)
        BW = sb("BW", [P, 2, TH, D], f32)
        W1P = sb("W1P", [P, 2, 2, KC * HID], f32r)
        W2P = sb("W2P", [P, 2, HC * D], f32r)
        XP = sb("XP", [P, 2, KC, TROWS], f32r)
        HF = sb("HF", [P, HC, TROWS], f32)
        HP = sb("HP", [P, 2, 2, HC, TROWS], f32r)
        Y = sb("Y", [P, 2, TH, D], f32)
        G = sb("G", [P, 4, TH], f32)
        GT = sb("GT", [P, TILES, 2, TH], f32)
        GY = sb("GY", [P, 2, 2, TH], f32)
        DI = sb("DI", [P, 2, TH], i32)
        PT = pb("PT", [P, KC, TROWS], f32)
        PH = pb("PH", [P, PAIRS, 2, TROWS], f32)
        PY = pb("PY", [P, 2, TH, D], f32)

        tile_links = sem("tile_links")
        ix_ready = [sem("ix_ready0"), sem("ix_ready1")]
        x_gathered = [sem("x_gathered0"), sem("x_gathered1")]
        w1_gathered = [sem("w1_gathered0"), sem("w1_gathered1")]
        w2_gathered = [sem("w2_gathered0"), sem("w2_gathered1")]
        y_sent = [sem("y_sent0"), sem("y_sent1")]
        w1_hi, w1_lo, w2_hi, w2_lo, w2_lo_pool = sem("w1_hi"), sem("w1_lo"), sem("w2_hi"), sem("w2_lo"), sem("w2_lo_pool")
        b1_ready, gy_ready, b2_ready = sem("b1_ready"), sem("gy_ready"), sem("b2_ready")
        xt_full, x_hi, x_lo, x_noted = sem("xt_full"), sem("x_hi"), sem("x_lo"), sem("x_noted")
        h_full, h_raw, h_hi, h_lo = sem("h_full"), sem("h_raw"), sem("h_hi"), sem("h_lo")
        y_full, y_summed, y_ready = sem("y_full"), sem("y_summed"), sem("y_ready")
        block = ctx.enter_context(nc.Block())

        def over_turns(eng, do):
            for t in range(-2, LOOP_FROM):
                do(t, t % 2, t // 2)
            with eng.Fori(0, (LOOP_TO - LOOP_FROM) // 2) as lap:
                for i in range(2):
                    t = LOOP_FROM + i
                    do(2 * lap + t, t % 2, lap + t // 2)
            for t in range(LOOP_TO, TILES + 2):
                do(t, t % 2, t // 2)

        def is_tile(t):
            return not isinstance(t, int) or 0 <= t < TILES

        def other(r, n, k):
            return (r + k) % 2, n + (r + k) // 2

        def piece(tile, q):
            return tile[:, q * PIECE:(q + 1) * PIECE]

        @block.vector
        def _(dve):
            v = nc.vector
            def note_indices(t, r):
                v.tensor_copy(IX[:, r:r + 1, :], RC[:, ds(t + 2, 1), :]).then_inc(ix_ready[r], 1)

            note_indices(-2, 0)
            note_indices(-1, 1)

            notes = Chain(dve, tile_links, 7)

            def results(t, r, n):
                dve.wait_ge(y_full, t + 1)
                dve.wait_ge(b2_ready, t + 1)
                at_least(dve, y_sent[r], 16 * TH * n)
                for i in range(TH):
                    v.scalar_tensor_tensor(Y[:, r, i, :], PY[:, r, i, :], GY[:, r, 0, i:i + 1], BW[:, r, i, :], ALU.mult, ALU.add
                                           ).then_inc(y_ready, 1)
                v.tensor_copy(DI[:, r, :], GY[:, r, 1, :]).then_inc(y_ready, 1)

            def rows_in_parts(t):
                dve.wait_ge(xt_full, t + 1)
                if is_tile(t - 1):
                    dve.wait_ge(h_full, PAIRS * t)
                v.tensor_copy(XP[:, 0, :, :], PT[:, :, :]).then_inc(x_hi, 1)
                dve.wait_ge(x_hi, t + 1)
                v.tensor_tensor(XP[:, 1, :, :], PT[:, :, :], XP[:, 0, :, :].bitcast(f32), ALU.subtract).then_inc(x_lo, 1)

            def do(t, r, n):
                s1, n1 = other(r, n, 1)
                sm, nm = other(r, n, -1)
                g = [G[:, i, :] for i in range(4)]
                w0, w1, e0, token = (XG[:, s1, :, D + i] for i in range(4))

                def note(j):
                    if j == 0:
                        notes.at(t + 1)
                        dve.wait_ge(x_gathered[s1], 16 * TH * (n1 + 1))
                        notes.did(v.tensor_copy(FX[:, :].unsqueeze(1), RF[:, ds(t + 1, 1), :]))
                        notes.did(v.tensor_tensor(g[1], w0, w1, ALU.subtract))
                        notes.wait()
                    elif j == 1:
                        notes.did(v.tensor_scalar(g[0], e0, FX[:, 3:4], None, ALU.is_equal))
                        notes.wait()
                        notes.did(v.tensor_tensor(g[1], g[1], g[0], ALU.mult))
                        notes.did(v.tensor_scalar(g[2], g[0], -float(TOK), float(TOK), ALU.mult, ALU.add))
                        notes.wait()
                    elif j == 2:
                        v.tensor_tensor(GT[:, ds(t + 1, 1), 0, :], g[1].unsqueeze(1), w1.unsqueeze(1), ALU.add
                                        ).then_inc(x_noted, 1)
                        v.tensor_tensor(g[2], g[2], token, ALU.add).then_inc(x_noted, 1)
                        dve.wait_ge(x_noted, 3 * (t + 1) + 2)
                        notes.did(v.tensor_tensor(g[2], g[2], FX[:, 6:8], ALU.subtract))
                        notes.wait()
                    else:
                        notes.did(v.tensor_tensor(g[2], g[2], FX[:, 4:6], ALU.mult))
                        notes.wait()
                        v.tensor_tensor(GT[:, ds(t + 1, 1), 1, :], g[2].unsqueeze(1), FX[:, 6:8].unsqueeze(1), ALU.add
                                        ).then_inc(x_noted, 1)

                for j in range(PAIRS):
                    if j < 2 and is_tile(t - 1):
                        for q in (2 * j, 2 * j + 1):
                            if q < DVE2:
                                dve.wait_ge(w2_hi, PAIRS * (t - 1) + q + 1)
                                v.tensor_tensor(piece(W2P[:, 1, :], q), piece(WG2[:, sm, :], q),
                                                piece(W2P[:, 0, :], q).bitcast(f32), ALU.subtract).then_inc(w2_lo, 1)
                            if q == 0:
                                at_least(dve, y_ready, 3 * (t - 2))
                                v.tensor_copy(GY[:, sm:sm + 1, :, :], GT[:, ds(t - 1, 1), :, :]).then_inc(gy_ready, 1)
                    if is_tile(t):
                        dve.wait_ge(h_hi, PAIRS * t + j + 1)
                        v.tensor_tensor(HP[:, r, 1, 2 * j:2 * j + 2, :], HF[:, 2 * j:2 * j + 2, :],
                                        HP[:, r, 0, 2 * j:2 * j + 2, :].bitcast(f32), ALU.subtract).then_inc(h_lo, 1)
                    if j == 1 and is_tile(t + 1):
                        rows_in_parts(t + 1)
                    if j == 2 and is_tile(t - 2):
                        results(t - 2, r, n - 1)
                for q in range(PAIRS):
                    if is_tile(t + 2):
                        dve.wait_ge(w1_hi, PAIRS * (t + 2) + q + 1)
                        v.tensor_tensor(piece(W1P[:, r, 1, :], q), piece(WG1[:, r, :], q),
                                        piece(W1P[:, r, 0, :], q).bitcast(f32), ALU.subtract).then_inc(w1_lo, 1)
                    if is_tile(t + 1):
                        note(q)
                if is_tile(t + 1):
                    if is_tile(t):
                        dve.wait_ge(w2_gathered[r], 16 * (n + 1))
                    note_indices(t + 1, s1)
            over_turns(dve, do)

        @block.gpsimd
        def _(pool):
            g = nc.gpsimd

            def gather_rows(t, r, n):
                if is_tile(t - 2):
                    pool.wait_ge(xt_full, t - 1)
                    pool.wait_ge(x_noted, 3 * (t - 1))
                pool.sem_inc(alone, 1)
                for i in range(TH):
                    g.indirect_dma_start(out=XG[:, r, i, :], out_offset=None, in_=rows,
                                         in_offset=IND(ap=IX[:, r, i:i + 1], axis=0)).then_inc(x_gathered[r], 16)

            def gather_first(t, r, n):
                if is_tile(t - 2):
                    pool.wait_ge(w1_lo, PAIRS * (t - 1))
                    pool.wait_ge(b1_ready, t - 1)
                pool.sem_inc(alone, 1)
                g.indirect_dma_start(out=WG1[:, r, :], out_offset=None, in_=experts1,
                                     in_offset=IND(ap=IX[:, (r + 1) % 2, 2:3], axis=0)).then_inc(w1_gathered[r], 16)

            def gather_second(t, r, n):
                if is_tile(t - 2):
                    pool.wait_ge(w2_lo, DVE2 * (t - 1))
                    pool.wait_ge(w2_lo_pool, (PAIRS - DVE2) * (t - 1))
                pool.sem_inc(alone, 1)
                g.indirect_dma_start(out=WG2[:, r, :], out_offset=None, in_=experts2,
                                     in_offset=IND(ap=IX[:, (r + 1) % 2, 3:4], axis=0)).then_inc(w2_gathered[r], 16)

            g.indirect_dma_start(out=WG1[:, 0, :], out_offset=None, in_=experts1,
                                 in_offset=IND(ap=RI[:, 0, 2:3], axis=0)).then_inc(w1_gathered[0], 16)
            for i in range(TH):
                g.indirect_dma_start(out=XG[:, 0, i, :], out_offset=None, in_=rows,
                                     in_offset=IND(ap=RI[:, 0, i:i + 1], axis=0)).then_inc(x_gathered[0], 16)

            def do(t, r, n):
                sm, nm = other(r, n, -1)
                if not isinstance(t, int) or t < TILES:
                    pool.wait_ge(ix_ready[r], n + 2)
                if is_tile(t + 3):
                    gather_first(t + 3, *other(r, n, 3))
                if is_tile(t - 1):
                    pool.wait_ge(gy_ready, t)
                    at_least(pool, y_ready, 3 * (t - 2))
                    g.tensor_tensor(BW[:, sm, :, :], WG2[:, sm, HC * D:].unsqueeze(1).to_broadcast([P, TH, D]),
                                    GY[:, sm, 0, :].unsqueeze(2).to_broadcast([P, TH, D]), ALU.mult).then_inc(b2_ready, 1)
                    for q in range(DVE2, PAIRS):
                        pool.wait_ge(w2_hi, PAIRS * (t - 1) + q + 1)
                        g.tensor_tensor(piece(W2P[:, 1, :], q), piece(WG2[:, sm, :], q),
                                        piece(W2P[:, 0, :], q).bitcast(f32), ALU.subtract).then_inc(w2_lo_pool, 1)
                if is_tile(t + 1):
                    gather_second(t + 1, *other(r, n, 1))
                if is_tile(t + 1) and is_tile(t + 2):
                    gather_rows(t + 2, r, n + 1)
                if is_tile(t - 2):
                    wait_alone(pool, y_ready, 3 * (t - 1), alone)
                    for i in range(TH):
                        g.indirect_dma_start(out=ys, out_offset=IND(ap=DI[:, r, i:i + 1], axis=0),
                                             in_=Y[:, r, i, :], in_offset=None).then_inc(y_sent[r], 16)
            over_turns(pool, do)
            for r in range(2):
                pool.wait_ge(y_sent[r], 16 * TH * ((TILES + 1 - r) // 2))

        @block.scalar
        def _(act):
            a = nc.scalar

            def do(t, r, n):
                s1, n1 = other(r, n, 1)
                sm, nm = other(r, n, -1)
                for j in range(PAIRS):
                    if j < 2 and is_tile(t - 1):
                        if j == 0:
                            act.wait_ge(w2_gathered[sm], 16 * (nm + 1))
                            at_least(act, y_full, t - 1)
                        for q in (2 * j, 2 * j + 1):
                            a.copy(piece(W2P[:, 0, :], q), piece(WG2[:, sm, :], q)).then_inc(w2_hi, 1)
                    if is_tile(t):
                        act.wait_ge(h_full, PAIRS * t + j + 1)
                        at_least(act, h_lo, PAIRS * (t - 1) + j + 1)
                        if j == 0:
                            act.wait_ge(b1_ready, t + 1)
                        for c in (2 * j, 2 * j + 1):
                            a.activation(HF[:, c, :], PH[:, j, c % 2, :], ACT.Gelu_apprx_tanh,
                                         bias=B1[:, r, c:c + 1]).then_inc(h_raw, 1)
                        act.wait_ge(h_raw, HC * t + 2 * j + 2)
                        at_least(act, y_full, t - 1)
                        a.copy(HP[:, r, 0, 2 * j:2 * j + 2, :], HF[:, 2 * j:2 * j + 2, :]).then_inc(h_hi, 1)
                if is_tile(t + 2):
                    act.wait_ge(w1_gathered[r], 16 * (n + 2))
                    if is_tile(t):
                        act.wait_ge(h_raw, HC * (t + 1))
                        act.wait_ge(h_full, PAIRS * (t + 1))
                    a.copy(B1[:, r, :], WG1[:, r, KC * HID:]).then_inc(b1_ready, 1)
                    for q in range(PAIRS):
                        a.copy(piece(W1P[:, r, 0, :], q), piece(WG1[:, r, :], q)).then_inc(w1_hi, 1)
            over_turns(act, do)

        @block.tensor
        def _(pe):
            m = nc.tensor
            terms = ((0, 0), (0, 1), (1, 0))

            def do(t, r, n):
                s1, n1 = other(r, n, 1)
                sm, nm = other(r, n, -1)
                if is_tile(t):
                    pe.wait_ge(x_lo, t + 1)
                    pe.wait_ge(w1_lo, PAIRS * (t + 1))
                    for c in range(HC):
                        if is_tile(t - 1) and c % 2 == 0:
                            pe.wait_ge(h_raw, HC * (t - 1) + c + 2)
                        for k in range(KC):
                            for a, o in terms:
                                i = m.matmul(PH[:, c // 2, c % 2, :], W1P[:, r, a, k * HID + c * P:k * HID + c * P + P], XP[:, o, k, :],
                                             start=(k == 0 and (a, o) == terms[0]), stop=(k == KC - 1 and (a, o) == terms[-1]))
                        if c % 2 == 1:
                            i.then_inc(h_full, 1)
                if is_tile(t + 1):
                    pe.wait_ge(x_gathered[s1], 16 * TH * (n1 + 1))
                    at_least(pe, x_lo, t + 1)
                    for k in range(KC):
                        for i in range(TH):
                            last = m.transpose(PT[:, k, i * P:i * P + P], XG[:, s1, i, k * P:k * P + P], const("ident"))
                    last.then_inc(xt_full, 1)
                if is_tile(t - 1):
                    if is_tile(t - 3):
                        pe.wait_ge(y_ready, 3 * (t - 2))
                    for i in range(TH):
                        for c in range(HC):
                            if i == 0 and c % 2 == 0:
                                pe.wait_ge(h_lo, PAIRS * (t - 1) + c // 2 + 1)
                                q = c // 2
                                if q < DVE2:
                                    pe.wait_ge(w2_lo, DVE2 * (t - 1) + q + 1)
                                else:
                                    pe.wait_ge(w2_lo_pool, (PAIRS - DVE2) * (t - 1) + q - DVE2 + 1)
                            for a, o in terms:
                                last = m.matmul(PY[:, sm, i, :], HP[:, sm, a, c, i * P:i * P + P], W2P[:, o, c * D:(c + 1) * D],
                                                start=(c == 0 and (a, o) == terms[0]), stop=(c == HC - 1 and (a, o) == terms[-1]))
                    last.then_inc(y_full, 1)
            over_turns(pe, do)


def stage3(nc, make, X, rsqrt, ys, out):
    f32 = mybir.dt.float32
    ACT, ALU = mybir.ActivationFunctionType, mybir.AluOpType
    STEPS3 = B // 2
    CC = 2 * C
    ctx = ExitStack()
    with ctx:
        sb, pb, sem = make(ctx)
        YC = sb("YC", [P, 2, 2, 2, C * D], f32)
        S = sb("S", [P, 2, CC, D], f32)
        T = sb("T", [P, 2, CC, D], f32)
        O = sb("O", [P, 2, CC, D], f32)
        ST = sb("STF", [P, CC, 6], f32)
        MV = sb("MVF", [P, CC, 2], f32)
        SM = sb("SMF", [P, 3, CC], f32)
        R = sb("RF3", [P, 2, 2, CC], f32)
        loaded = [[sem(f"y_loaded{slot}_{half}") for half in range(2)] for slot in range(2)]
        stored = [sem("stored0"), sem("stored1")]
        summed, scaled, normed, added = sem("summed"), sem("scaled"), sem("normed"), sem("added")
        links = sem("finish_links")
        block = ctx.enter_context(nc.Block())
        yv = ys[0:2 * TOK].rearrange("(k b p c) e -> b p k (c e)", k=2, p=P, c=C)
        ov = out.rearrange("(b p c) e -> b p (c e)", p=P, c=C)

        @block.sync
        def _(sp):
            for i in range(STEPS3):
                at_least(sp, summed, 2 * (i - 1))
                for h in range(2):
                    sp.dma_start(YC[:, i % 2, h, :, :], yv[2 * i + h]).then_inc(loaded[i % 2][h], 16)

        @block.gpsimd
        def _(pool):
            for i in range(STEPS3):
                at_least(pool, normed, CC * (i - 1))
                for h in range(2):
                    pool.wait_ge(loaded[i % 2][h], 16 * (i // 2 + 1))
                    y = YC[:, i % 2, h, :, :].rearrange("p k (c e) -> p k c e", c=C)
                    nc.gpsimd.tensor_tensor(S[:, i % 2, C * h:C * h + C, :], y[:, 0], y[:, 1], ALU.add).then_inc(summed, 1)

        @block.vector
        def _(dve):
            v = nc.vector
            chain = Chain(dve, links, 2 * CC + 11)
            var, y, t = (SM[:, n, :] for n in range(3))

            def add(i):
                at_least(dve, stored[i % 2], 32 * (i // 2))
                for h in range(2):
                    dve.wait_ge(normed, CC * i + C * h + C)
                    b = 2 * i + h
                    v.tensor_tensor(O[:, i % 2, C * h:C * h + C, :], T[:, i % 2, C * h:C * h + C, :],
                                    X[:, C * b:C * b + C, :], ALU.add).then_inc(added, 1)

            for i in range(STEPS3):
                chain.at(i)
                for c in range(CC):
                    if c % C == 0:
                        dve.wait_ge(summed, 2 * i + c // C + 1)
                    chain.did(v.bn_stats(ST[:, c, :], S[:, i % 2, c, :]))
                chain.wait()
                for c in range(CC):
                    chain.did(v.bn_aggr(MV[:, c, :], ST[:, c, :]))
                chain.wait()
                chain.did(v.tensor_scalar_add(var, MV[:, :, 1], EPS))
                chain.wait()
                at_least(dve, normed, CC * (i - 1))
                rsqrt(v, chain, R[:, i % 2, 0, :], var, y, t)
                v.scalar_tensor_tensor(R[:, i % 2, 1, :], MV[:, :, 0], -1.0, R[:, i % 2, 0, :], ALU.mult, ALU.mult
                                       ).then_inc(scaled, 1)
                dve.wait_ge(scaled, i + 1)
                if i > 0:
                    add(i - 1)
            add(STEPS3 - 1)

        @block.scalar
        def _(act):
            def store(i):
                for h in range(2):
                    act.wait_ge(added, 2 * i + h + 1)
                    act.dma_start(ov[2 * i + h], O[:, i % 2, C * h:C * h + C, :].rearrange("p c e -> p (c e)")
                                  ).then_inc(stored[i % 2], 16)

            for i in range(STEPS3):
                act.wait_ge(scaled, i + 1)
                at_least(act, added, 2 * (i - 1))
                for c in range(CC):
                    nc.scalar.activation(T[:, i % 2, c, :], S[:, i % 2, c, :], ACT.Identity, scale=R[:, i % 2, 0, c:c + 1],
                                         bias=R[:, i % 2, 1, c:c + 1]).then_inc(normed, 1)
                if i > 0:
                    store(i - 1)
            store(STEPS3 - 1)
            for slot in range(2):
                act.wait_ge(stored[slot], 16 * STEPS3)


def constants():
    a = np.zeros((P, NCONST), np.float32)

    def put(name, value):
        at, w = CONST[name]
        a[:, at:at + w] = np.broadcast_to(value, (P, w))

    p, q = np.arange(P)[:, None], np.arange(P)[None, :]
    put("ident", p == q)
    put("lower", p < q)
    put("ones", 1)
    put("neg_half", np.where(p // CDH == q // CDH, -0.5, 0))
    put("indicator", np.concatenate([np.where(8 * m + p // DH == np.arange(H), -0.5, 0) for m in range(KC)], 1))
    put("iota8", np.tile(np.arange(NE), C))
    put("region", np.tile(np.arange(NE) * TOK, C))
    put("token", (np.arange(B)[None, :, None] * N + p[:, :, None] * C + np.arange(C)).reshape(P, -1))
    put("steps", np.tile(np.arange(THR) * TROWS, NE))
    put("tiles", np.arange(TILES))
    put("iota_t", np.tile(np.arange(NE), TILES))
    put("lane", p)
    put("dump", 2 * TOK + np.arange(TH) * P + p)
    return a


def kernel(**inputs):
    import concourse.bacc as bacc
    from concourse.bass_utils import run_bass_kernel_spmd
    g = {k.split("_", 2)[2]: np.asarray(v) for k, v in inputs.items()}

    def cols(v, n):
        return v.reshape(n, P).T

    def square(w):
        return w.reshape(KC, P, D).transpose(1, 0, 2).reshape(P, KC * D)

    def by_partition(w):
        return w.reshape(NE, -1, P, w.shape[-1]).transpose(0, 2, 1, 3).reshape(NE * P, -1)

    vecs = np.zeros((P, NVEC), np.float32)
    for name, value in [("gamma1", g["gamma1"]), ("gamma2", g["gamma2"]), ("tau_t", g["tau_t"].reshape(-1)),
                        ("tau_c", cols(np.repeat(g["tau_c"].reshape(-1), CDH), 2)),
                        ("ln1_w", cols(g["ln1_w"], KC)), ("ln1_b", cols(g["ln1_b"], KC)),
                        ("ln2_w", cols(g["ln2_w"], KC)), ("ln2_b", cols(g["ln2_b"], KC)),
                        ("router", g["w_router"].reshape(KC, P, NE).transpose(1, 0, 2).reshape(P, -1))]:
        at, w = VEC[name]
        vecs[:, at:at + w] = np.broadcast_to(value, (P, w))
    arrays = {
        "x": g["x"].reshape(TOK, D),
        "weights": np.concatenate([square(g[n]) for n in ("Wqk_t", "Wv_t", "Wo_t", "Wqk_c")]
                                  + [square(np.ascontiguousarray(g["Wv_c"].T)), square(g["Wo_c"])], 1),
        "vecs": vecs,
        "consts": constants(),
        "experts1": np.concatenate([by_partition(g["w1"]), by_partition(g["b1"][:, :, None])], 1),
        "experts2": np.concatenate([by_partition(g["w2"]), np.repeat(g["b2"], P, 0)], 1),
    }
    arrays = {k: np.ascontiguousarray(v) for k, v in arrays.items()}
    nc = bacc.Bacc("TRN2", target_bir_lowering=False, num_devices=1)
    aps = [nc.dram_tensor(k, v.shape, mybir.dt.from_np(v.dtype), kind="ExternalInput").ap() for k, v in arrays.items()]
    out = nc.dram_tensor("out", (TOK, D), mybir.dt.float32, kind="ExternalOutput").ap()
    program(nc, *aps, out)
    result = run_bass_kernel_spmd(nc, [arrays], core_ids=[0])
    return result.results[0]["out"].reshape(B, N, D)
```
